# Optimizing a Trainium2 kernel written in Bass

```python
import numpy as np
import jax
import jax.numpy as jnp

def _softmax(x, axis=-1):
    return jax.nn.softmax(x, axis=axis)

def _gelu(x):
    return jax.nn.gelu(x, approximate=True)

def _silu(x):
    return jax.nn.silu(x)

def _sigmoid(x):
    return jax.nn.sigmoid(x)

def _layernorm(x, axis=-1, eps=1e-05):
    m = jnp.mean(x, axis=axis, keepdims=True)
    v = jnp.var(x, axis=axis, keepdims=True)
    return (x - m) / jnp.sqrt(v + eps)

def _scatter_add(tgt, idx, src, axis=0):
    return tgt.at[idx].add(src)

def _segment_sum(src, seg, n):
    return jax.ops.segment_sum(src, seg, n)
kernel_name = 'mk_xattn_ffn_d2_seqx_r4_fb588c'

def setup_inputs(seed: int=0):
    np.random.seed(seed)
    _w = jnp.asarray

    def _rec_inputs():
        import jax
        import jax.numpy as jnp
        _rk = jax.random.key(seed)
        x = 0.0002417 + 0.9998 * jax.random.normal(jax.random.fold_in(_rk, 1), (8, 512, 256), jnp.float32)
        _lenS = 512 - jax.random.randint(jax.random.fold_in(_rk, 7), (8,), 0, max(1, 512 // 4) + 1, jnp.int32)
        _lenS2 = 512 - jax.random.randint(jax.random.fold_in(_rk, 8), (8,), 0, max(1, 512 // 4) + 1, jnp.int32)
        _ctx_1024P = jax.random.normal(jax.random.fold_in(_rk, 11), (8, 16, 256), jnp.float32)
        _ctx_1024c = jax.random.dirichlet(jax.random.fold_in(_rk, 511), 0.3 * jnp.ones((16,), jnp.float32), (8, 512))
        _ctx_1024t = jnp.einsum('bsk,bkd->bsd', _ctx_1024c, _ctx_1024P)
        _ctx_1024t = _ctx_1024t * jax.lax.rsqrt(jnp.mean(jnp.square(_ctx_1024t)) + 1e-12) * 0.953939
        ctx_1024 = 7.22013e-05 + 1.00017 * (_ctx_1024t + 0.3 * jax.random.normal(jax.random.fold_in(_rk, 611), (8, 512, 256), jnp.float32))
        _validS = jnp.arange(512)[None, :] < _lenS[:, None]
        _validS2 = jnp.arange(512)[None, :] < _lenS2[:, None]
        _causal = jnp.tril(jnp.ones((512, 512), dtype=bool))
        mask_Bx1xS2_bf1 = jnp.ones((8, 1, 512), dtype=bool)
        return (x, ctx_1024, mask_Bx1xS2_bf1)
    x, ctx_1024, mask_Bx1xS2_bf1 = _rec_inputs()

    def _L0_xattn_setup():
        import jax, jax.numpy as jnp
        import numpy as np
        H = 16
        D = 256
        HD = D // H
        key = jax.random.key(seed)
        ks = jax.random.split(key, 12)
        B, S = (4, 512)
        scale = 1.0 / np.sqrt(D)
        inp = {'k': jax.random.normal(ks[0], (B, S, D), jnp.float32), 'v': jax.random.normal(ks[1], (B, S, D), jnp.float32), 'q': jax.random.normal(ks[2], (B, S, D), jnp.float32), 'mask': jnp.ones((B, 1, S), dtype=bool), 'Wk': jax.random.normal(ks[3], (D, D), jnp.float32) * scale, 'bk': jax.random.normal(ks[4], (D,), jnp.float32) * 0.01, 'Wv': jax.random.normal(ks[5], (D, D), jnp.float32) * scale, 'bv': jax.random.normal(ks[6], (D,), jnp.float32) * 0.01, 'Wq': jax.random.normal(ks[7], (D, D), jnp.float32) * scale, 'bq': jax.random.normal(ks[8], (D,), jnp.float32) * 0.01, 'Wo': jax.random.normal(ks[9], (D, D), jnp.float32) * scale, 'bo': jax.random.normal(ks[10], (D,), jnp.float32) * 0.01}
        return inp
    _L0_xattn_all = _L0_xattn_setup()
    _L0_xattn_in = {k: v for k, v in _L0_xattn_all.items() if k in ('Wk', 'bk', 'Wv', 'bv', 'Wq', 'bq', 'Wo', 'bo')}
    del _L0_xattn_all

    def _L0_ffn_setup():
        import jax, jax.numpy as jnp
        import numpy as np
        H = 16
        TOP_K = 2
        EPS = 1e-05

        def _layer_norm(x, g, b):
            m = x.mean(-1, keepdims=True)
            v = ((x - m) ** 2).mean(-1, keepdims=True)
            return (x - m) * jax.lax.rsqrt(v + EPS) * g + b

        def _block(x, ln1_g, ln1_b, ln2_g, ln2_b, w_qkv, w_o, w_gate, w1, b1, w2, b2):
            B, S, D = x.shape
            hd = D // H
            h = _layer_norm(x, ln1_g, ln1_b)
            qkv = h @ w_qkv
            q, k, v = jnp.split(qkv, 3, axis=-1)
            q = q.reshape(B, S, H, hd)
            k = k.reshape(B, S, H, hd)
            v = v.reshape(B, S, H, hd)
            scores = jnp.einsum('bqhd,bkhd->bhqk', q, k) * hd ** (-0.5)
            causal = jnp.tril(jnp.ones((S, S), bool))
            scores = jnp.where(causal, scores, jnp.finfo(scores.dtype).min)
            attn = jax.nn.softmax(scores, axis=-1)
            o = jnp.einsum('bhqk,bkhd->bqhd', attn, v).reshape(B, S, D)
            x_resid = x + o @ w_o
            moe_in = _layer_norm(x_resid, ln2_g, ln2_b)
            N = B * S
            xf = moe_in.reshape(N, D)
            probs = jax.nn.softmax(xf @ w_gate, axis=-1)
            top_w, top_i = jax.lax.top_k(probs, TOP_K)
            top_w = top_w / top_w.sum(-1, keepdims=True)
            E = w1.shape[0]
            out = jnp.zeros_like(xf)
            for e in range(E):
                gate_e = jnp.sum(jnp.where(top_i == e, top_w, 0.0), axis=-1)
                he = jax.nn.gelu(xf @ w1[e] + b1[e])
                out = out + gate_e[:, None] * (he @ w2[e] + b2[e])
            return out.reshape(B, S, D) + x_resid
        key = jax.random.key(seed)
        ks = jax.random.split(key, 12)
        B, S, D, F, E = (8, 128, 256, 1024, 8)
        inp = {'x': jax.random.normal(ks[0], (B, S, D), jnp.float32), 'ln1_g': jnp.ones((D,), jnp.float32), 'ln1_b': jnp.zeros((D,), jnp.float32), 'ln2_g': jnp.ones((D,), jnp.float32), 'ln2_b': jnp.zeros((D,), jnp.float32), 'w_qkv': jax.random.normal(ks[1], (D, 3 * D), jnp.float32) * D ** (-0.5), 'w_o': jax.random.normal(ks[2], (D, D), jnp.float32) * D ** (-0.5), 'w_gate': jax.random.normal(ks[3], (D, E), jnp.float32) * D ** (-0.5), 'w1': jax.random.normal(ks[4], (E, D, F), jnp.float32) * D ** (-0.5), 'b1': jnp.zeros((E, F), jnp.float32), 'w2': jax.random.normal(ks[5], (E, F, D), jnp.float32) * F ** (-0.5), 'b2': jnp.zeros((E, D), jnp.float32)}
        return inp
    _L0_ffn_all = _L0_ffn_setup()
    _L0_ffn_in = {k: v for k, v in _L0_ffn_all.items() if k in ('ln1_g', 'ln1_b', 'ln2_g', 'ln2_b', 'w_qkv', 'w_o', 'w_gate', 'w1', 'b1', 'w2', 'b2')}
    del _L0_ffn_all

    def _L1_xattn_setup():
        import jax, jax.numpy as jnp
        import numpy as np
        HIDDEN = 256
        key = jax.random.key(seed)
        ks = jax.random.split(key, 8)
        s = 1.0 / np.sqrt(HIDDEN)
        return {'query': jax.random.normal(ks[0], (8, 256, HIDDEN), dtype=jnp.float32), 'ref': jax.random.normal(ks[1], (8, 1024, HIDDEN), dtype=jnp.float32), 'Wq': jax.random.normal(ks[2], (HIDDEN, HIDDEN), dtype=jnp.float32) * s, 'bq': jax.random.normal(ks[3], (HIDDEN,), dtype=jnp.float32) * s, 'Wk': jax.random.normal(ks[4], (HIDDEN, HIDDEN), dtype=jnp.float32) * s, 'bk': jax.random.normal(ks[5], (HIDDEN,), dtype=jnp.float32) * s, 'Wv': jax.random.normal(ks[6], (HIDDEN, HIDDEN), dtype=jnp.float32) * s, 'bv': jax.random.normal(ks[7], (HIDDEN,), dtype=jnp.float32) * s}
    _L1_xattn_all = _L1_xattn_setup()
    _L1_xattn_in = {k: v for k, v in _L1_xattn_all.items() if k in ('Wq', 'bq', 'Wk', 'bk', 'Wv', 'bv')}
    del _L1_xattn_all

    def _L1_ffn_setup():
        import jax, jax.numpy as jnp
        import numpy as np
        DIM = 256
        HIDDEN = 768
        SCALE = 1.0 / 127.0

        def _dequant(w_int, dtype):
            return w_int.astype(dtype) * jnp.asarray(SCALE, dtype)
        key = jax.random.key(seed)
        k_x, k_g, k_u, k_d = jax.random.split(key, 4)
        x = jax.random.normal(k_x, (4, 512, DIM), dtype=jnp.float32)
        w_gate = jax.random.randint(k_g, (HIDDEN, DIM), -127, 128, dtype=jnp.int32)
        w_up = jax.random.randint(k_u, (HIDDEN, DIM), -127, 128, dtype=jnp.int32)
        w_down = jax.random.randint(k_d, (DIM, HIDDEN), -127, 128, dtype=jnp.int32)
        return {'x': x, 'w_gate': w_gate, 'w_up': w_up, 'w_down': w_down}
    _L1_ffn_all = _L1_ffn_setup()
    _L1_ffn_in = {k: v for k, v in _L1_ffn_all.items() if k in ('w_gate', 'w_up', 'w_down')}
    del _L1_ffn_all
    return {'x': x, 'ctx_1024': ctx_1024, 'mask_Bx1xS2_bf1': mask_Bx1xS2_bf1, 'L0_xattn_Wk': _L0_xattn_in['Wk'], 'L0_xattn_bk': _L0_xattn_in['bk'], 'L0_xattn_Wv': _L0_xattn_in['Wv'], 'L0_xattn_bv': _L0_xattn_in['bv'], 'L0_xattn_Wq': _L0_xattn_in['Wq'], 'L0_xattn_bq': _L0_xattn_in['bq'], 'L0_xattn_Wo': _L0_xattn_in['Wo'], 'L0_xattn_bo': _L0_xattn_in['bo'], 'L0_ffn_ln1_g': _L0_ffn_in['ln1_g'], 'L0_ffn_ln1_b': _L0_ffn_in['ln1_b'], 'L0_ffn_ln2_g': _L0_ffn_in['ln2_g'], 'L0_ffn_ln2_b': _L0_ffn_in['ln2_b'], 'L0_ffn_w_qkv': _L0_ffn_in['w_qkv'], 'L0_ffn_w_o': _L0_ffn_in['w_o'], 'L0_ffn_w_gate': _L0_ffn_in['w_gate'], 'L0_ffn_w1': _L0_ffn_in['w1'], 'L0_ffn_b1': _L0_ffn_in['b1'], 'L0_ffn_w2': _L0_ffn_in['w2'], 'L0_ffn_b2': _L0_ffn_in['b2'], 'L1_xattn_Wq': _L1_xattn_in['Wq'], 'L1_xattn_bq': _L1_xattn_in['bq'], 'L1_xattn_Wk': _L1_xattn_in['Wk'], 'L1_xattn_bk': _L1_xattn_in['bk'], 'L1_xattn_Wv': _L1_xattn_in['Wv'], 'L1_xattn_bv': _L1_xattn_in['bv'], 'L1_ffn_w_gate': _L1_ffn_in['w_gate'], 'L1_ffn_w_up': _L1_ffn_in['w_up'], 'L1_ffn_w_down': _L1_ffn_in['w_down']}

def reference(x, ctx_1024, mask_Bx1xS2_bf1, L0_xattn_Wk, L0_xattn_bk, L0_xattn_Wv, L0_xattn_bv, L0_xattn_Wq, L0_xattn_bq, L0_xattn_Wo, L0_xattn_bo, L0_ffn_ln1_g, L0_ffn_ln1_b, L0_ffn_ln2_g, L0_ffn_ln2_b, L0_ffn_w_qkv, L0_ffn_w_o, L0_ffn_w_gate, L0_ffn_w1, L0_ffn_b1, L0_ffn_w2, L0_ffn_b2, L1_xattn_Wq, L1_xattn_bq, L1_xattn_Wk, L1_xattn_bk, L1_xattn_Wv, L1_xattn_bv, L1_ffn_w_gate, L1_ffn_w_up, L1_ffn_w_down):
    import jax
    import jax.numpy as jnp

    def _L0_xattn_ref(k, v, q, mask, Wk, bk, Wv, bv, Wq, bq, Wo, bo):
        import jax, jax.numpy as jnp
        import numpy as np
        H = 16
        D = 256
        HD = D // H
        B, Sq, _ = q.shape
        Sk = k.shape[1]
        kh = (k @ Wk.T + bk).reshape(B, Sk, H, HD).transpose(0, 2, 1, 3)
        vh = (v @ Wv.T + bv).reshape(B, Sk, H, HD).transpose(0, 2, 1, 3)
        qh = (q @ Wq.T + bq).reshape(B, Sq, H, HD).transpose(0, 2, 1, 3)
        qh = qh / jnp.sqrt(jnp.asarray(HD, qh.dtype))
        scores = jnp.einsum('bhqd,bhkd->bhqk', qh, kh)
        scores = jnp.where(mask[:, None, :, :], scores, jnp.asarray(-jnp.inf, scores.dtype))
        attn = jax.nn.softmax(scores, axis=-1)
        ctx = jnp.einsum('bhqk,bhkd->bhqd', attn, vh)
        ctx = ctx.transpose(0, 2, 1, 3).reshape(B, Sq, H * HD)
        out = ctx @ Wo.T + bo
        return out

    def _L0_ffn_ref(x, ln1_g, ln1_b, ln2_g, ln2_b, w_qkv, w_o, w_gate, w1, b1, w2, b2):
        import jax, jax.numpy as jnp
        import numpy as np
        H = 16
        TOP_K = 2
        EPS = 1e-05

        def _layer_norm(x, g, b):
            m = x.mean(-1, keepdims=True)
            v = ((x - m) ** 2).mean(-1, keepdims=True)
            return (x - m) * jax.lax.rsqrt(v + EPS) * g + b

        def _block(x, ln1_g, ln1_b, ln2_g, ln2_b, w_qkv, w_o, w_gate, w1, b1, w2, b2):
            B, S, D = x.shape
            hd = D // H
            h = _layer_norm(x, ln1_g, ln1_b)
            qkv = h @ w_qkv
            q, k, v = jnp.split(qkv, 3, axis=-1)
            q = q.reshape(B, S, H, hd)
            k = k.reshape(B, S, H, hd)
            v = v.reshape(B, S, H, hd)
            scores = jnp.einsum('bqhd,bkhd->bhqk', q, k) * hd ** (-0.5)
            causal = jnp.tril(jnp.ones((S, S), bool))
            scores = jnp.where(causal, scores, jnp.finfo(scores.dtype).min)
            attn = jax.nn.softmax(scores, axis=-1)
            o = jnp.einsum('bhqk,bkhd->bqhd', attn, v).reshape(B, S, D)
            x_resid = x + o @ w_o
            moe_in = _layer_norm(x_resid, ln2_g, ln2_b)
            N = B * S
            xf = moe_in.reshape(N, D)
            probs = jax.nn.softmax(xf @ w_gate, axis=-1)
            top_w, top_i = jax.lax.top_k(probs, TOP_K)
            top_w = top_w / top_w.sum(-1, keepdims=True)
            E = w1.shape[0]
            out = jnp.zeros_like(xf)
            for e in range(E):
                gate_e = jnp.sum(jnp.where(top_i == e, top_w, 0.0), axis=-1)
                he = jax.nn.gelu(xf @ w1[e] + b1[e])
                out = out + gate_e[:, None] * (he @ w2[e] + b2[e])
            return out.reshape(B, S, D) + x_resid
        return _block(x, ln1_g, ln1_b, ln2_g, ln2_b, w_qkv, w_o, w_gate, w1, b1, w2, b2)

    def _L1_xattn_ref(query, ref, Wq, bq, Wk, bk, Wv, bv):
        import jax, jax.numpy as jnp
        import numpy as np
        HIDDEN = 256
        norm_fact = 1.0 / np.sqrt(HIDDEN).astype(np.float32)
        Q = query @ Wq + bq
        K = ref @ Wk + bk
        V = ref @ Wv + bv
        scores = jnp.einsum('bqh,bkh->bqk', Q, K)
        attn = jax.nn.softmax(scores, axis=-1) * norm_fact
        return jnp.einsum('bqk,bkh->bqh', attn, V)

    def _L1_ffn_ref(x, w_gate, w_up, w_down):
        import jax, jax.numpy as jnp
        import numpy as np
        DIM = 256
        HIDDEN = 768
        SCALE = 1.0 / 127.0

        def _dequant(w_int, dtype):
            return w_int.astype(dtype) * jnp.asarray(SCALE, dtype)
        wg = _dequant(w_gate, x.dtype)
        wu = _dequant(w_up, x.dtype)
        wd = _dequant(w_down, x.dtype)
        gate = jnp.einsum('bsd,hd->bsh', x, wg)
        up = jnp.einsum('bsd,hd->bsh', x, wu)
        h = jax.nn.silu(gate) * up
        return jnp.einsum('bsh,dh->bsd', h, wd)
    x = x + _L0_xattn_ref(ctx_1024, ctx_1024, _layernorm(x, axis=-1), mask_Bx1xS2_bf1, L0_xattn_Wk, L0_xattn_bk, L0_xattn_Wv, L0_xattn_bv, L0_xattn_Wq, L0_xattn_bq, L0_xattn_Wo, L0_xattn_bo)
    x = x + _L0_ffn_ref(_layernorm(x, axis=-1), L0_ffn_ln1_g, L0_ffn_ln1_b, L0_ffn_ln2_g, L0_ffn_ln2_b, L0_ffn_w_qkv, L0_ffn_w_o, L0_ffn_w_gate, L0_ffn_w1, L0_ffn_b1, L0_ffn_w2, L0_ffn_b2)
    x = x + _L1_xattn_ref(_layernorm(x, axis=-1), ctx_1024, L1_xattn_Wq, L1_xattn_bq, L1_xattn_Wk, L1_xattn_bk, L1_xattn_Wv, L1_xattn_bv)
    x = x + _L1_ffn_ref(_layernorm(x, axis=-1), L1_ffn_w_gate, L1_ffn_w_up, L1_ffn_w_down)
    return x

_drawn_inputs = setup_inputs


def setup_inputs(seed=0):
    import zlib

    import numpy as np

    out = dict(_drawn_inputs(seed))
    spreads = {'L0_ffn_ln1_g': (1.0, 0.2),
     'L0_ffn_ln1_b': (0.0, 0.1),
     'L0_ffn_ln2_g': (1.0, 0.2),
     'L0_ffn_ln2_b': (0.0, 0.1),
     'L0_ffn_b1': (0.0, 0.1),
     'L0_ffn_b2': (0.0, 0.1)}
    factors = {'L0_xattn_bk': 64.0,
     'L0_xattn_bq': 7.009,
     'L1_xattn_bq': 8.0,
     'L1_xattn_bk': 64.0,
     'L1_xattn_bv': 22.948}
    for name, (base, spread) in spreads.items():
        noise = np.random.default_rng([zlib.crc32(name.encode()), seed]).standard_normal(out[name].shape)
        drawn = base * np.exp(spread * noise) if base else spread * noise
        out[name] = jnp.asarray(drawn.astype(out[name].dtype))
    for name, factor in factors.items():
        out[name] = (out[name] * factor).astype(out[name].dtype)
    return out
```

```python
import numpy as np
import concourse.bass as bass
from concourse import mybir
from contextlib import ExitStack

F32 = mybir.dt.float32
BF16 = mybir.dt.bfloat16
I32 = mybir.dt.int32
U8 = mybir.dt.uint8
ALU = mybir.AluOpType
ACT = mybir.ActivationFunctionType
AX = mybir.AxisListType
ds = bass.ds

P = 128
B, S, D = 8, 512, 256
TT = S // P
DC = D // P
H, HD = 16, 16
HP = 32
GH = 4
NG = H // GH
G_ALL = B * NG
EPS = 1e-5
NEG = -1e30
E_N, FF = 8, 1024
FC = FF // P
F2 = 768
F2C = F2 // P
SCALE2 = 1.0 / 127.0
NPART = 3
NTERM = 6
KM = NTERM * HD
K_MAX = KM + 1
K_EXP = KM + 1 + NPART


class Chain:

    def __init__(self, eng, sem):
        self.eng, self.sem, self.n = eng, sem, 0

    def __call__(self, ins):
        self.n += 1
        ins.then_inc(self.sem, 1)
        self.eng.wait_ge(self.sem, self.n)

    def reset(self):
        self.eng.sem_clear(self.sem)
        self.n = 0


def by_pairs(eng, body, peel_last=False):
    for par in range(2):
        body(par, par)
    with eng.Fori(1, B // 2 - peel_last) as i:
        for par in range(2):
            body(i * 2 + par, par)
    if peel_last:
        for par in range(2):
            body(B - 2 + par, par)


def inverse_deviations(pool, c, mv, rstd, var_ready, rstd_ready, times):
    power, var, eps, own = c.half_power
    pool.memset(power[:], -0.5).then_inc(own, 1)
    pool.memset(eps[:], EPS).then_inc(own, 1)
    pool.wait_ge(own, 2)
    with pool.Fori(0, times) as k:
        pool.wait_ge(var_ready, k + 1)
        pool.tensor_tensor(var[:], mv[:, :, 1], eps[:], ALU.add).then_inc(own, 1)
        pool.wait_ge(own, k + 3)
        pool.tensor_tensor(rstd[:], var[:], power[:], ALU.pow).then_inc(rstd_ready, 1)


class Ctx:

    def __init__(self, nc, tag, stack):
        self.nc, self.tag, self.stack, self.sems = nc, tag, stack, []

    def sb(self, name, shape, dt=F32):
        return self.stack.enter_context(self.nc.sbuf_tensor(f"{self.tag}_{name}", shape, dt))

    def ps(self, name, shape, dt=F32):
        return self.stack.enter_context(self.nc.psum_tensor(f"{self.tag}_{name}", shape, dt))

    def sem(self, name):
        self.sems.append(self.stack.enter_context(self.nc.semaphore(f"{self.tag}_{name}")))
        return self.sems[-1]


def phase_tokens(nc, c, stage, w, scr):
    xin = [c.sb(f"xin{p}", [P, TT, D]) for p in range(2)]
    cin = [c.sb(f"cin{p}", [P, DC, S] if stage == 0 else [P, NG, S]) for p in range(2)]
    y = c.sb("y", [P, TT, D])
    y0 = [c.sb(f"y0{p}", [P, TT, D]) for p in range(2)]
    XS = 2 if stage == 1 else 1
    XL = 2 if stage == 2 else 1
    yT = c.sb("yT", [P, DC, S])
    stats = c.sb("stats", [P, TT, 6])
    mv = c.sb("mv", [P, TT, 2])
    rstd = c.sb("rstd", [P, TT])
    xo = [c.sb(f"xo{p}", [P, TT, D]) for p in range(2)]
    ident = c.sb("ident", [P, P])
    psT = c.ps("psT", [P, DC * S])
    psQ = [c.ps(f"psQ{k}", [P, S]) for k in range(2)]
    psV = [c.ps(f"psV{k}", [P, 512]) for k in range(2)]
    if stage < 2:
        full = c.sb("full", [P, 2, DC, S])
        rest = c.sb("rest", [P, DC, S])
        parts = [c.sb(f"parts{p}", [P, 2, NPART, DC, S], BF16) for p in range(2)]
        vaug = [c.sb(f"vaug{p}", [P, TT, H, HP]) for p in range(2)]
        wk, wq, wv = (c.sb(n, [P, DC, D]) for n in ("wk", "wq", "wv"))
        bv = c.sb("bv", [P, D])
        bk, bq = c.sb("bk", [P, DC]), c.sb("bq", [P, DC])
    if stage == 2:
        wg = c.sb("wg", [P, DC, E_N])
        lg = c.sb("lg", [P, TT, E_N])
        lmax = c.sb("lmax", [P, TT])
        ex = c.sb("ex", [P, TT, E_N])
        gt = c.sb("gt", [P, TT, E_N, E_N])
        eq = c.sb("eq", [P, TT, E_N, E_N])
        lower = c.sb("lower", [P, E_N, E_N])
        rank = c.sb("rank", [P, TT, E_N])
        tot = c.sb("tot", [P, TT])
        gate = [c.sb(f"gate{p}", [P, TT, E_N]) for p in range(2)]
    if stage > 0:
        wo = c.sb("wo", [P, NG, D])
        lng, lnb = c.sb("lng", [P, DC]), c.sb("lnb", [P, DC])
    if stage == 1:
        bo = c.sb("bo", [1, D])
    ones = c.sb("ones", [1, P])

    n_const = [0]
    const_in = c.sem("const_in")
    set_done = c.sem("set_done")
    x_in = [c.sem(f"x_in{p}") for p in range(2)]
    c_in = [c.sem(f"c_in{p}") for p in range(2)]
    x_used, c_used = c.sem("x_used"), c.sem("c_used")
    y_ready, tr_ps, yT_ready = c.sem("y_ready"), c.sem("tr_ps"), c.sem("yT_ready")
    q_ps, q_free, v_ps, v_free = c.sem("q_ps"), c.sem("q_free"), c.sem("v_ps"), c.sem("v_free")
    full_ready, split_done = c.sem("full_ready"), c.sem("split_done")
    v_ready = c.sem("v_ready")
    qk_out = [c.sem(f"qk_out{p}") for p in range(2)]
    v_out = [c.sem(f"v_out{p}") for p in range(2)]
    x_out = [c.sem(f"x_out{p}") for p in range(2)]
    xo_ready, gates_ready, logit_ready, exp_ready = (
        c.sem("xo_ready"), c.sem("gates_ready"), c.sem("logit_ready"), c.sem("exp_ready"))
    yT_used = c.sem("yT_used")
    y0_ready = c.sem("y0_ready")
    var_ready, rstd_ready = c.sem("var_ready"), c.sem("rstd_ready")
    c.half_power = (c.sb("power", [P, TT]), c.sb("var", [P, TT]), c.sb("eps", [P, TT]), c.sem("pool_own"))
    NORMS = 2 if stage == 1 else 1
    dve_own, act_own = c.sem("dve_own"), c.sem("act_own")
    QK = 4
    VU = {0: TT, 1: 2 * TT, 2: 2 * TT}[stage]
    QKD = 2 * DC * NPART
    consts = []
    if stage < 2:
        consts += [(wk, w["wk"]), (wq, w["wq"]), (wv, w["wv"])]
        if stage == 0:
            consts += [(bk, w["bk"]), (bq, w["bq"])]
    if stage > 0:
        consts += [(wo, w["wo"]), (lng, w["lng"]), (lnb, w["lnb"])]
    if stage == 1:
        consts += [(bo, w["bo"])]
    if stage == 2:
        consts += [(wg, w["wg"])]
    if stage == 0:
        consts += [(bv, w["bv"])]
    n_consts = len(consts)

    with nc.Block() as block:

        @block.sync
        def _(sp):
            for tile, src in consts:
                sp.dma_start(tile[:], src).then_inc(const_in, 16)

            def load(n, par):
                sp.wait_ge(x_used, n + 1)
                sp.dma_start(xin[par][:], scr["x_src"][ds(n, 1)].rearrange("o (t p) d -> p (o t) d", p=P)
                             ).then_inc(x_in[par], 16)
                if stage == 2:
                    sp.dma_start(y0[par][:], scr["y_src"][ds(n, 1)].rearrange("o (t p) d -> p (o t) d", p=P)
                                 ).then_inc(x_in[par], 16)
                sp.wait_ge(c_used, n + 1)
                if stage == 0:
                    src = scr["c_src"][ds(n, 1)].rearrange("o (c p) s -> p (o c) s", p=P)
                else:
                    src = scr["c_src"][ds(n * NG, NG)].rearrange("g p s -> p g s")
                sp.dma_start(cin[par][:], src).then_inc(c_in[par], 16)

            def store(n, par):
                if stage > 0:
                    sp.wait_ge(xo_ready, n + 1)
                    sp.dma_start(scr["x_dst"][ds(n, 1)].rearrange("o (t p) d -> p (o t) d", p=P), xo[par][:]
                                 ).then_inc(x_out[par], 16)
                if stage == 1:
                    sp.wait_ge(y0_ready, n + 1)
                    sp.dma_start(scr["y_dst"][ds(n, 1)].rearrange("o (t p) d -> p (o t) d", p=P), y0[par][:]
                                 ).then_inc(x_out[par], 16)
                if stage == 2:
                    sp.wait_ge(yT_ready, n * DC + DC)
                    sp.dma_start(scr["xfT"][ds(n, 1)].rearrange("o (c p) s -> p (o c) s", p=P), yT[:]
                                 ).then_inc(v_out[par], 16)
                    sp.wait_ge(gates_ready, n + 1)
                    sp.dma_start(scr["gates"][ds(n, 1)].rearrange("o p t e -> p (o t) e"), gate[par][:]
                                 ).then_inc(qk_out[par], 16)
                    return
                for k in range(2):
                    sp.wait_ge(split_done, n * 2 + k + 1)
                    for blk in range(DC):
                        at = 0
                        for r in range(NPART):
                            m = NPART - r
                            src = parts[par][:, k, 0:m, blk, :] if k == 0 else (
                                parts[par][:, k, r:r + 1, blk, :].to_broadcast([P, m, S]))
                            sp.dma_start(scr["qk"][ds(n * DC + blk, 1), k, at:at + m].rearrange("o t p s -> p (o t) s"),
                                         src).then_inc(qk_out[par], 16)
                            at += m
                sp.wait_ge(v_ready, n + 1)
                sp.dma_start(scr["v"][ds(n, 1)].rearrange("o (t p) c -> p (o t) c", p=P),
                             vaug[par][:].rearrange("p t h c -> p t (h c)")).then_inc(v_out[par], 16)

            sp.sem_inc(x_used, 2)
            sp.sem_inc(c_used, 2)
            load(0, 0)

            def body(n, par):
                if not (isinstance(n, int) and n == B - 1):
                    load(n + 1, 1 - par)
                store(n, par)

            by_pairs(sp, body, peel_last=True)
            for par in range(2):
                if stage < 2:
                    sp.wait_ge(qk_out[par], 16 * QKD * (B // 2))
                else:
                    sp.wait_ge(qk_out[par], 16 * (B // 2))
                sp.wait_ge(v_out[par], 16 * (B // 2))
                if stage > 0:
                    sp.wait_ge(x_out[par], 16 * XS * (B // 2))

        @block.gpsimd
        def _(pool):
            pool.memset(ident[:], 0.0).then_inc(set_done, 1)
            pool.wait_ge(set_done, 1)
            pool.affine_select(out=ident[:], in_=ident[:], compare_op=ALU.not_equal, fill=1.0, base=0,
                               pattern=[[-1, P]], channel_multiplier=1).then_inc(set_done, 1)
            pool.memset(ones[:], 1.0).then_inc(set_done, 1)
            if stage < 2:
                for p in range(2):
                    pool.memset(vaug[p][:], 0.0).then_inc(set_done, 1)
                pool.wait_ge(set_done, 5)
                for p in range(2):
                    pool.memset(vaug[p][:, :, :, HD:HD + 1], 1.0).then_inc(set_done, 1)
            else:
                pool.memset(lower[:], 0.0).then_inc(set_done, 1)
                pool.wait_ge(set_done, 4)
                pool.affine_select(out=lower[:], in_=lower[:], compare_op=ALU.is_ge, fill=1.0, base=0,
                                   pattern=[[-1, E_N], [1, E_N]], channel_multiplier=0).then_inc(set_done, 1)
            inverse_deviations(pool, c, mv, rstd, var_ready, rstd_ready, B * NORMS)

        n_set = 7 if stage < 2 else 5

        @block.vector
        def _(dve):
            link = Chain(dve, dve_own)
            dve.wait_ge(set_done, n_set)
            dve.wait_ge(const_in, 16 * n_consts)

            norms = [0]

            def norm(n, src, dst):
                for t in range(TT):
                    last = dve.bn_stats(stats[:, t, :], src[:, t, :])
                link(last)
                for t in range(TT):
                    last = dve.bn_aggr(mv[:, t, :], stats[:, t, :])
                last.then_inc(var_ready, 1)
                norms[0] += 1
                dve.wait_ge(rstd_ready, n * NORMS + norms[0])
                for t in range(TT):
                    last = dve.tensor_scalar(dst[:, t, :], src[:, t, :], mv[:, t, 0:1], rstd[:, t:t + 1],
                                             ALU.subtract, ALU.mult)
                return last

            def split(n, par, k):
                dve.wait_ge(full_ready, n * QK + DC * (k + 1))
                dve.wait_ge(split_done, n * 2 + k)
                a = parts[par]
                link(dve.tensor_tensor(rest[:], full[:, k], a[:, k, 0], ALU.subtract))
                link(dve.tensor_copy(a[:, k, 1], rest[:]))
                dve.tensor_tensor(a[:, k, 2], rest[:], a[:, k, 1], ALU.subtract).then_inc(split_done, 1)

            def values(n, par):
                dve.wait_ge(v_out[par], (n - par) * 8)
                for t in range(TT):
                    dve.wait_ge(v_ps, n * VU + (VU - TT) + t + 1)
                    src = psV[t % 2][:, 0:D].rearrange("p (h d) -> p h d", h=H)
                    dst = vaug[par][:, t, :, 0:HD]
                    if stage == 0:
                        last = dve.tensor_tensor(dst, src, bv[:].rearrange("p (h d) -> p h d", h=H), ALU.add)
                    else:
                        last = dve.tensor_copy(dst, src)
                    last.then_inc(v_free, 1)
                dve.drain().then_inc(v_ready, 1)

            def body(n, par):
                dve.wait_ge(x_in[par], (n - par) * (8 * XL) + 16 * XL)
                if stage > 0:
                    dve.wait_ge(x_out[par], (n - par) * (8 * XS))
                    for t in range(TT):
                        dve.wait_ge(v_ps, n * VU + t + 1)
                        last = dve.tensor_tensor(xo[par][:, t, :], psV[t % 2][:, 0:D],
                                                 (y0 if stage == 2 else xin)[par][:, t, :], ALU.add)
                        last.then_inc(v_free, 1)
                    dve.drain().then_inc(xo_ready if stage == 1 else v_ready, 1)
                    if stage == 1:
                        dve.sem_inc(x_used, 1)
                        link(norm(n, xo[par], y0[par]))
                        dve.sem_inc(y0_ready, 1)
                        src = y0[par]
                    else:
                        src = xo[par]
                else:
                    src = xin[par]
                dve.wait_ge(tr_ps, n)
                norm(n, src, y)
                dve.drain().then_inc(y_ready, 1)
                if stage == 0:
                    dve.sem_inc(x_used, 1)
                if stage == 2:
                    link(dve.tensor_tensor(xo[par][:], xo[par][:], xin[par][:], ALU.add))
                    dve.sem_inc(x_used, 1)
                    dve.sem_inc(xo_ready, 1)
                    experts(n, par)
                else:
                    dve.wait_ge(qk_out[par], (n - par) * (8 * QKD))
                    split(n, par, 0)
                    if stage == 0:
                        values(n, par)
                        split(n, par, 1)
                    else:
                        split(n, par, 1)
                        values(n, par)
                link.reset()
                norms[0] = 0

            def experts(n, par):
                for t in range(TT):
                    dve.wait_ge(v_ps, n * VU + TT + t + 1)
                    last = dve.tensor_copy(lg[:, t, :], psV[t % 2][:, 0:E_N])
                    last.then_inc(v_free, 1)
                dve.wait_ge(v_free, n * VU + VU + 2)
                link(dve.tensor_reduce(lmax[:], lg[:], axis=AX.X, op=ALU.max))
                dve.tensor_tensor(ex[:], lg[:], lmax[:, :].unsqueeze(2).to_broadcast([P, TT, E_N]), ALU.subtract
                                  ).then_inc(logit_ready, 1)
                mine = lg[:, :, :].unsqueeze(3).to_broadcast([P, TT, E_N, E_N])
                other = lg[:, :, :].unsqueeze(2).to_broadcast([P, TT, E_N, E_N])
                dve.tensor_tensor(gt[:], other, mine, ALU.is_gt)
                link(dve.tensor_tensor(eq[:], other, mine, ALU.is_equal))
                for t in range(TT):
                    last = dve.tensor_tensor(eq[:, t], eq[:, t], lower[:], ALU.mult)
                link(last)
                link(dve.tensor_tensor(gt[:], gt[:], eq[:], ALU.add))
                link(dve.tensor_reduce(rank[:], gt[:], axis=AX.X, op=ALU.add))
                dve.wait_ge(exp_ready, n + 1)
                link(dve.scalar_tensor_tensor(out=ex[:], in0=rank[:], scalar=1.5, in1=ex[:], op0=ALU.is_lt, op1=ALU.mult))
                link(dve.tensor_reduce(tot[:], ex[:], axis=AX.X, op=ALU.add))
                link(dve.reciprocal(tot[:], tot[:]))
                dve.wait_ge(qk_out[par], (n - par) * 8)
                dve.tensor_tensor(gate[par][:], ex[:], tot[:, :].unsqueeze(2).to_broadcast([P, TT, E_N]), ALU.mult
                                  ).then_inc(gates_ready, 1)

            by_pairs(dve, body)

        @block.scalar
        def _(act):
            link = Chain(act, act_own)
            act.wait_ge(const_in, 16 * n_consts)
            act.wait_ge(set_done, n_set)
            if stage == 0:
                link(act.mul(bq[:], bq[:], 0.25))

            def project(n, par, k, scale, bias):
                act.wait_ge(split_done, n * 2)
                for u in range(DC):
                    act.wait_ge(q_ps, n * QK + DC * k + u + 1)
                    dst = full[:, k, u, :]
                    if bias is None:
                        ins = act.mul(dst, psQ[u][:], scale)
                    else:
                        ins = act.activation(dst, psQ[u][:], ACT.Identity, bias=bias[:, u:u + 1], scale=scale)
                    ins.then_inc(q_free, 1)
                act.wait_ge(q_free, n * QK + DC * (k + 1) + 2)
                act.wait_ge(qk_out[par], (n - par) * (8 * QKD))
                for u in range(DC):
                    act.copy(parts[par][:, k, 0, u, :], full[:, k, u, :]).then_inc(full_ready, 1)

            def transposed(n, par):
                act.wait_ge(tr_ps, n + 1)
                act.wait_ge(yT_used, n)
                if stage == 0:
                    act.copy(yT[:].rearrange("p c s -> p (c s)"), psT[:]).then_inc(yT_ready, 1)
                else:
                    if stage == 2:
                        other = 1 - par
                        act.wait_ge(v_out[other], (n - par) * 8 + (16 if par else 0))
                    for u in range(DC):
                        act.activation(yT[:, u, :], psT[:, u * S:(u + 1) * S], ACT.Identity,
                                       bias=lnb[:, u:u + 1], scale=lng[:, u:u + 1]).then_inc(yT_ready, 1)

            def body(n, par):
                    if stage == 0:
                        project(n, par, 0, 1.0, bk)
                        transposed(n, par)
                        project(n, par, 1, 0.25, bq)
                    elif stage == 1:
                        transposed(n, par)
                        project(n, par, 0, 1.0, None)
                        project(n, par, 1, 0.25, None)
                    else:
                        transposed(n, par)
                        act.wait_ge(logit_ready, n + 1)
                        act.activation(ex[:], ex[:], ACT.Exp).then_inc(exp_ready, 1)

            by_pairs(act, body)

        @block.tensor
        def _(pe):
            pe.wait_ge(const_in, 16 * n_consts)
            pe.wait_ge(set_done, n_set)
            pe.sem_inc(q_free, 2)
            pe.sem_inc(v_free, 2)
            per_T = 1 if stage == 0 else DC

            def project(n, k, src, wt):
                for u in range(DC):
                    pe.wait_ge(q_free, n * QK + DC * k + u + 1)
                    for d in range(DC):
                        last = pe.matmul(psQ[u][:], wt[:, d, u * P:(u + 1) * P], src[:, d, :],
                                         start=d == 0, stop=d == DC - 1)
                    last.then_inc(q_ps, 1)

            def values(n, src):
                for t in range(TT):
                    pe.wait_ge(v_free, n * VU + (VU - TT) + t + 1)
                    for d in range(DC):
                        last = pe.matmul(psV[t % 2][:, 0:D], src[:, d, t * P:(t + 1) * P], wv[:, d, :],
                                         start=d == 0, stop=d == DC - 1)
                    last.then_inc(v_ps, 1)
                return last

            def out_proj(n, par):
                for t in range(TT):
                    pe.wait_ge(v_free, n * VU + t + 1)
                    for g in range(NG):
                        last = pe.matmul(psV[t % 2][:, 0:D], cin[par][:, g, t * P:(t + 1) * P], wo[:, g, :],
                                         start=g == 0, stop=stage == 2 and g == NG - 1)
                    if stage == 1:
                        last = pe.matmul(psV[t % 2][:, 0:D], ones[:], bo[:], start=False, stop=True)
                    last.then_inc(v_ps, 1)

            def body(n, par):
                    pe.wait_ge(c_in[par], (n - par) * 8 + 16)
                    if stage == 0:
                        project(n, 0, cin[par], wk)
                        values(n, cin[par])
                        pe.drain().then_inc(c_used, 1)
                    else:
                        out_proj(n, par)
                        pe.drain().then_inc(c_used, 1)
                    pe.wait_ge(y_ready, n + 1)
                    pe.wait_ge(yT_ready, n * per_T)
                    for t in range(TT):
                        for d in range(DC):
                            last = pe.transpose(psT[:, d * S + t * P:d * S + (t + 1) * P],
                                                y[:, t, d * P:(d + 1) * P], ident[:])
                    last.then_inc(tr_ps, 1)
                    pe.wait_ge(yT_ready, n * per_T + per_T)
                    if stage == 0:
                        project(n, 1, yT, wq)
                    elif stage == 1:
                        project(n, 0, yT, wk)
                        project(n, 1, yT, wq)
                        values(n, yT)
                    else:
                        for t in range(TT):
                            pe.wait_ge(v_free, n * VU + TT + t + 1)
                            for d in range(DC):
                                last = pe.matmul(psV[t % 2][:, 0:E_N], yT[:, d, t * P:(t + 1) * P], wg[:, d, :],
                                                 start=d == 0, stop=d == DC - 1)
                            last.then_inc(v_ps, 1)
                    pe.drain().then_inc(yT_used, 1)

            by_pairs(pe, body)


def half_of(x):
    return x // 2


def quarter_of(x):
    return x // 4


def phase_attention(nc, c, causal, scr):
    SLOTS = 8
    LA = 2
    U = GH * TT
    NP_BUF = 8
    K6 = [c.sb(f"K6_{s}", [K_EXP, GH, S], BF16) for s in range(SLOTS)]
    Q6 = [c.sb(f"Q6_{s}", [K_EXP, GH, S], BF16) for s in range(SLOTS)]
    V = [c.sb(f"V_{s}", [P, TT, GH * HP]) for s in range(SLOTS)]
    NM_BUF = 4
    nm = [c.sb(f"nm{s}", [P, TT, GH]) for s in range(NM_BUF)]
    nr = c.sb("nr", [P, TT, GH])
    nparts = c.sb("nparts", [P, TT, NPART * GH], BF16)
    nrow = [c.sb(f"nrow{s}", [NPART * GH, S], BF16) for s in range(2)]
    prob = [c.sb(f"prob{s}", [P, S]) for s in range(NP_BUF)]
    oT = [c.sb(f"oT{s}", [P, S]) for s in range(2)]
    rc = [c.sb(f"rc{s}", [P, S]) for s in range(2)]
    on = [c.sb(f"on{s}", [P, S]) for s in range(2)]
    identb = c.sb("identb", [P, P], BF16)
    sel = c.sb("sel", [P, P])
    cmq = c.sb("cmq", [P, P], BF16)
    cmk = c.sb("cmk", [P, P], BF16)
    NS, NE = 2, 4
    psS = [c.ps(f"psS{k}", [P, S]) for k in range(NS)]
    psE = [c.ps(f"psE{k}", [P, S]) for k in range(NE)]
    psO = c.ps("psO", [P, S])
    psM = c.ps("psM", [P, S])
    psMb = psM[:, :].bitcast(BF16)

    set_done, rows_set = c.sem("set_done"), c.sem("rows_set")
    g_in = [c.sem(f"g_in{s}") for s in range(SLOTS)]
    s_ps, s_free = c.sem("s_ps"), c.sem("s_free")
    e_ps, p_ready, pv_done = c.sem("e_ps"), c.sem("p_ready"), c.sem("pv_done")
    nparts_ready, nT_ps, nrow_ready = c.sem("nparts_ready"), c.sem("nT_ps"), c.sem("nrow_ready")
    nrow_in = [c.sem(f"nrow_in{s}") for s in range(2)]
    oT_ready, den_ps, on_ready, rc_ready = c.sem("oT_ready"), c.sem("den_ps"), c.sem("on_ready"), c.sem("rc_ready")
    o_out = [c.sem(f"o_out{s}") for s in range(2)]
    dve_own = c.sem("dve_own")
    N_LOAD = 3 if causal else 4

    def steps(eng, first, step):
        step(0, 0)
        with eng.Fori(0, 3) as i:
            for s in range(1, SLOTS + 1):
                step(i * SLOTS + s, s % SLOTS)
        for G in range(3 * SLOTS + 1, G_ALL):
            step(G, G % SLOTS)

    def last_of(G, k):
        return isinstance(G, int) and G + k >= G_ALL

    n_set = 8 if causal else 4

    with nc.Block() as block:

        @block.gpsimd
        def _(pool):
            pool.memset(identb[:], 0.0).then_inc(set_done, 1)
            pool.memset(sel[:], 0.0).then_inc(set_done, 1)
            pool.wait_ge(set_done, 2)
            pool.affine_select(out=identb[:], in_=identb[:], compare_op=ALU.not_equal, fill=1.0, base=0,
                               pattern=[[-1, P]], channel_multiplier=1).then_inc(set_done, 1)
            v = sel[:].rearrange("p (i m) -> p i m", i=GH)
            pool.affine_select(out=v, in_=v, compare_op=ALU.not_equal, fill=1.0, base=-HD,
                               pattern=[[-HP, GH], [0, HP]], channel_multiplier=1).then_inc(set_done, 1)
            if causal:
                pool.memset(cmq[:], 0.0).then_inc(set_done, 1)
                pool.memset(cmk[:], 0.0).then_inc(set_done, 1)
                pool.wait_ge(set_done, 6)
                pool.affine_select(out=cmq[:], in_=cmq[:], compare_op=ALU.is_ge, fill=NEG, base=0,
                                   pattern=[[-1, P]], channel_multiplier=1).then_inc(set_done, 1)
                pool.affine_select(out=cmk[:], in_=cmk[:], compare_op=ALU.is_ge, fill=NEG, base=0,
                                   pattern=[[1, P]], channel_multiplier=-1).then_inc(set_done, 1)

            pool.sem_inc(on_ready, 2)

            def scale(i, s):
                pool.wait_ge(rc_ready, i * 2 + (2 + s + 1))
                pool.wait_ge(o_out[s], i * 16)
                pool.tensor_tensor(on[s][:], oT[s][:], rc[s][:], ALU.mult).then_inc(on_ready, 1)

            for s in range(2):
                scale(0, s)
            with pool.Fori(1, G_ALL // 2) as i:
                for s in range(2):
                    scale(i, s)

        @block.sync
        def _(sp):
            def load(G, s):
                if not (isinstance(G, int) and G < SLOTS):
                    sp.wait_ge(oT_ready, G - SLOTS + 1)
                g = s % NG
                blk, half = g // 2, g % 2
                row = (G - g) // 2 + blk if isinstance(G, int) else half_of(G - g) + blk
                for k, tile in ((0, K6[s]), (1, Q6[s])):
                    src = scr["qk"][ds(row, 1), k].rearrange("o t (d e h) n -> (o t d) e (h n)", d=HD, e=2)
                    sp.dma_start(tile[0:KM].rearrange("p h n -> p (h n)"), src[:, half, :]).then_inc(g_in[s], 16)
                b = (G - g) // NG if isinstance(G, int) else quarter_of(G - g)
                sp.dma_start(V[s][:], scr["v"][ds(b, 1), :, g * GH * HP:(g + 1) * GH * HP]
                             .rearrange("o (t p) c -> p (o t) c", p=P)).then_inc(g_in[s], 16)
                if not causal:
                    sp.dma_start(K6[s][KM:KM + 1, :, :],
                                 scr["mask"][ds(b, 1), :].unsqueeze(1).to_broadcast([1, GH, S])
                                 ).then_inc(g_in[s], 16)

            sp.wait_ge(rows_set, 1)
            for G in range(SLOTS):
                load(G, G)

            def maxima(G, s):
                sp.wait_ge(nrow_ready, G + 1)
                for r in range(NPART):
                    sp.dma_start(Q6[s][KM + 1 + r:KM + 2 + r, :, :],
                                 nrow[s % 2][r * GH:(r + 1) * GH, :]).then_inc(nrow_in[s % 2], 16)

            def result(G, s):
                sp.wait_ge(on_ready, 2 + G + 1)
                sp.dma_start(scr["o"][ds(G, 1)].rearrange("o p s -> p (o s)"), on[s % 2][:]
                             ).then_inc(o_out[s % 2], 16)

            maxima(0, 0)

            def step(G, s):
                if not last_of(G, 1):
                    maxima(G + 1, (s + 1) % SLOTS)
                if isinstance(G, int) and G == 0:
                    return
                result(G - 1, (s - 1) % SLOTS)
                if not last_of(G, SLOTS - 1):
                    load(G + SLOTS - 1, (s - 1) % SLOTS)

            steps(sp, 0, step)
            result(G_ALL - 1, (G_ALL - 1) % SLOTS)
            for k in range(2):
                sp.wait_ge(o_out[k], 16 * (G_ALL // 2))

        @block.tensor
        def _(pe):
            pe.wait_ge(set_done, n_set)
            pe.wait_ge(rows_set, 1)
            pe.sem_inc(s_free, NS)
            pe.sem_inc(rc_ready, 2)

            def score(G, s, j):
                h, t = j // TT, j % TT
                bank = psS[j % NS]
                n = (t + 1) * P if causal else S
                pe.wait_ge(s_free, G * U + j + 1)
                last = pe.matmul(bank[:, 0:n], Q6[s][0:K_MAX, h, t * P:(t + 1) * P], K6[s][0:K_MAX, h, 0:n],
                                 start=True, stop=not causal)
                if causal:
                    last = pe.matmul(bank[:, t * P:n], identb[:], cmq[:], start=False, stop=True)
                last.then_inc(s_ps, 1)

            def shifted(G, s, j):
                t, h = j // GH, j % GH
                bank = psE[j % NE]
                q0 = t * P if causal else 0
                if not (isinstance(G, int) and G == 0 and j < NE):
                    pe.wait_ge(p_ready, G * U + j + 1 - NE)
                last = pe.matmul(bank[:, 0:S - q0], K6[s][0:K_EXP, h, t * P:(t + 1) * P], Q6[s][0:K_EXP, h, q0:S],
                                 start=True, stop=not causal)
                if causal:
                    last = pe.matmul(bank[:, 0:P], identb[:], cmk[:], start=False, stop=True)
                last.then_inc(e_ps, 1)

            def weigh(G, s, j):
                t, h = j // GH, j % GH
                q0 = t * P if causal else 0
                if j == 0:
                    pe.wait_ge(oT_ready, G)
                pe.wait_ge(p_ready, G * U + j + 1)
                pe.matmul(psO[h * HP:(h + 1) * HP, q0:S], V[s][:, t, h * HP:(h + 1) * HP],
                          prob[j % NP_BUF][:, 0:S - q0], start=t == 0, stop=t == TT - 1).then_inc(pv_done, 1)

            def maxima(G, s):
                pe.wait_ge(nparts_ready, G + 1)
                pe.wait_ge(rc_ready, G)
                for t in range(TT):
                    last = pe.transpose(psMb[0:NPART * GH, t * P:(t + 1) * P], nparts[:, t, :], identb[:])
                last.then_inc(nT_ps, 1)

            def denominators(G, s):
                pe.wait_ge(oT_ready, G + 1)
                pe.wait_ge(nrow_ready, G + 3 if not last_of(G, 2) else G_ALL)
                if isinstance(G, int) and G > G_ALL - 3:
                    pe.wait_ge(rc_ready, 2 + G)
                pe.matmul(psM[:], sel[:], oT[s % 2][:], start=True, stop=True).then_inc(den_ps, 1)

            for G in range(LA):
                pe.wait_ge(g_in[G], 16 * N_LOAD)
                for j in range(U):
                    score(G, G, j)
                    if G == 1 and j == 5:
                        maxima(0, 0)

            def step(G, s):
                if isinstance(G, int) and G == 0:
                    first = True
                else:
                    first = False
                pe.wait_ge(nrow_in[s % 2], (G - s % 2) * 24 + 48)
                more = not last_of(G, LA)
                s2 = (s + LA) % SLOTS
                if more:
                    pe.wait_ge(g_in[s2], loads_of(G + LA, s2))
                for j in range(U):
                    if more:
                        score(G + LA, s2, j)
                    shifted(G, s, j)
                    if j >= 2:
                        weigh(G, s, j - 2)
                    elif not first:
                        weigh(G - 1, (s - 1) % SLOTS, U - 2 + j)
                    if j == 2 and not last_of(G, 1):
                        maxima(G + 1, (s + 1) % SLOTS)
                    if j == 9 and not first:
                        denominators(G - 1, (s - 1) % SLOTS)

            def loads_of(G, s):
                return (G - s) * (16 * N_LOAD // SLOTS) + 16 * N_LOAD

            steps(pe, 0, step)
            G, s = G_ALL - 1, (G_ALL - 1) % SLOTS
            weigh(G, s, U - 2)
            weigh(G, s, U - 1)
            denominators(G, s)

        @block.scalar
        def _(act):
            def evacuate(G, s):
                act.wait_ge(pv_done, G * U + U)
                act.wait_ge(on_ready, G + 1)
                act.copy(oT[s % 2][:], psO[:]).then_inc(oT_ready, 1)

            def step(G, s):
                for j in range(U):
                    t = j // GH
                    n = S - t * P if causal else S
                    act.wait_ge(e_ps, G * U + j + 1)
                    if not (isinstance(G, int) and G == 0 and j < NP_BUF):
                        act.wait_ge(pv_done, G * U + j + 1 - NP_BUF)
                    act.activation(prob[j % NP_BUF][:, 0:n], psE[j % NE][:, 0:n], ACT.Exp).then_inc(p_ready, 1)
                    if j == 1 and not (isinstance(G, int) and G == 0):
                        evacuate(G - 1, (s - 1) % SLOTS)

            steps(act, 0, step)
            evacuate(G_ALL - 1, (G_ALL - 1) % SLOTS)

        @block.vector
        def _(dve):
            link = Chain(dve, dve_own)
            for s in range(SLOTS):
                dve.memset(K6[s][KM:K_EXP, :, :], 1.0)
                last = dve.memset(Q6[s][KM:K_EXP, :, :], 1.0)
            if causal:
                link(last)
                for s in range(SLOTS):
                    last = dve.memset(K6[s][KM:KM + 1, :, :], 0.0)
            last.then_inc(rows_set, 1)

            def top(G, s, j):
                h, t = j // TT, j % TT
                n = (t + 1) * P if causal else S
                dve.wait_ge(s_ps, G * U + j + 1)
                dve.tensor_reduce(nm[s % NM_BUF][:, t, h:h + 1], psS[j % NS][:, 0:n], axis=AX.X,
                                  op=ALU.max, negate=True).then_inc(s_free, 1)

            def shift_parts(G, s):
                m = nm[s % NM_BUF]
                np_ = nparts[:].rearrange("p t (r h) -> p r t h", r=NPART)
                dve.wait_ge(s_free, G * U + U + NS)
                dve.wait_ge(nT_ps, G)
                link(dve.tensor_copy(np_[:, 0], m[:]))
                link(dve.tensor_tensor(nr[:], m[:], np_[:, 0], ALU.subtract))
                link(dve.tensor_copy(np_[:, 1], nr[:]))
                dve.tensor_tensor(np_[:, 2], nr[:], np_[:, 1], ALU.subtract).then_inc(nparts_ready, 1)

            def shift_rows(G, s):
                dve.wait_ge(nT_ps, G + 1)
                if not (isinstance(G, int) and G < 2):
                    dve.wait_ge(nrow_in[s % 2], (G - s % 2) * 24)
                dve.tensor_copy(nrow[s % 2][:], psMb[0:NPART * GH, 0:S]).then_inc(nrow_ready, 1)

            def divide(G, s):
                dve.wait_ge(den_ps, G + 1)
                dve.wait_ge(on_ready, G + 1)
                dve.reciprocal(rc[s % 2][:], psM[:]).then_inc(rc_ready, 1)

            for G in range(LA):
                for j in range(U):
                    top(G, G, j)
                    if G == 1 and j == 2:
                        shift_parts(0, 0)
                    if G == 1 and j == 8:
                        shift_rows(0, 0)

            def step(G, s):
                if not last_of(G, 1):
                    shift_parts(G + 1, (s + 1) % SLOTS)
                for j in range(U):
                    if not last_of(G, LA):
                        top(G + LA, (s + LA) % SLOTS, j)
                    if j == 5 and not last_of(G, 1):
                        shift_rows(G + 1, (s + 1) % SLOTS)
                    if j == 13 and not (isinstance(G, int) and G == 0):
                        divide(G - 1, (s - 1) % SLOTS)
                link.reset()

            link.reset()
            steps(dve, 0, step)
            divide(G_ALL - 1, (G_ALL - 1) % SLOTS)


def phase_experts(nc, c, w, scr):
    NT = B * TT
    xf = c.sb("xf", [P, DC, B * S])
    acc = c.sb("acc", [P, NT, D])
    gates = c.sb("gates", [P, NT, E_N])
    w1 = [c.sb(f"w1_{p}", [P, DC, FF]) for p in range(2)]
    w2 = [c.sb(f"w2_{p}", [P, FC, D]) for p in range(2)]
    b1 = [c.sb(f"b1_{p}", [P, FC]) for p in range(2)]
    b2 = [c.sb(f"b2_{p}", [1, D]) for p in range(2)]
    ones = c.sb("ones", [1, P])
    hT = [c.sb(f"hT{p}", [P, FC, S]) for p in range(2)]
    psH = [c.ps(f"psH{k}", [P, S]) for k in range(4)]
    psY = [c.ps(f"psY{k}", [P, S]) for k in range(4)]
    in_sb, w_in = c.sem("in_sb"), [c.sem(f"w_in{p}") for p in range(2)]
    h_ps, h_ready, y_ps, y_free, w_used, out_done, ones_set = (
        c.sem(n) for n in ("h_ps", "h_ready", "y_ps", "y_free", "w_used", "out_done", "ones_set"))
    LAG = 2

    def units(eng, body, per_expert=None):
        with eng.Fori(0, E_N // 2) as i:
            for ep in range(2):
                if per_expert is not None:
                    per_expert(i * 2 + ep, ep)
                with eng.Fori(0, B // 2) as k:
                    for q in range(2):
                        body(i * (2 * B) + k * 2 + (ep * B + q), i * 2 + ep, ep, k * 2 + q, q)

    with nc.Block() as block:

        @block.sync
        def _(sp):
            sp.sem_inc(w_used, 2)
            with sp.Fori(0, E_N // 2) as i:
                for ep in range(2):
                    e = i * 2 + ep
                    sp.wait_ge(w_used, e + 1)
                    sp.dma_start(w1[ep][:], scr["w1"][ds(e, 1)].rearrange("o (c p) f -> p (o c) f", p=P)
                                 ).then_inc(w_in[ep], 16)
                    sp.dma_start(w2[ep][:], scr["w2"][ds(e, 1)].rearrange("o (c p) d -> p (o c) d", p=P)
                                 ).then_inc(w_in[ep], 16)
                    sp.dma_start(b2[ep][:], scr["b2"][ds(e, 1), :]).then_inc(w_in[ep], 16)
                    sp.dma_start(b1[ep][:], scr["b1"][ds(e, 1)].rearrange("o p f -> p (o f)")).then_inc(w_in[ep], 16)
            sp.wait_ge(y_free, E_N * B * TT + TT)
            for b in range(B):
                sp.dma_start(scr["x2"][b].rearrange("(t p) d -> p t d", p=P), acc[:, b * TT:(b + 1) * TT, :]
                             ).then_inc(out_done, 16)
            sp.wait_ge(out_done, 16 * B)

        @block.gpsimd
        def _(pool):
            pool.memset(ones[:], 1.0).then_inc(ones_set, 1)
            for b in range(B):
                pool.dma_start(xf[:, :, b * S:(b + 1) * S], scr["xfT"][b].rearrange("(c p) s -> p c s", p=P)
                               ).then_inc(in_sb, 16)
                pool.dma_start(acc[:, b * TT:(b + 1) * TT, :], scr["base"][b].rearrange("(t p) d -> p t d", p=P)
                               ).then_inc(in_sb, 16)
                pool.dma_start(gates[:, b * TT:(b + 1) * TT, :], scr["gates"][b]).then_inc(in_sb, 16)

        n_in = 16 * 3 * B

        @block.tensor
        def _(pe):
            pe.wait_ge(in_sb, n_in)
            pe.wait_ge(ones_set, 1)
            pe.sem_inc(h_ready, 4)
            pe.sem_inc(y_free, TT)

            def body(W, e, ep, tb, q):
                pe.wait_ge(w_in[ep], (e - ep) * 32 + 64)

                def first(f):
                    pe.wait_ge(h_ready, W * FC + (f + 1))
                    for d in range(DC):
                        last = pe.matmul(psH[f % 4][:], w1[ep][:, d, f * P:(f + 1) * P], xf[:, d, ds(tb * S, S)],
                                         start=d == 0, stop=d == DC - 1)
                    last.then_inc(h_ps, 1)

                def second(f):
                    pe.wait_ge(h_ready, W * FC + (f + 1 + 4))
                    if f == 0:
                        pe.wait_ge(y_free, W * TT + TT)
                    for t in range(TT):
                        last = pe.matmul(psY[t][:, 0:D], hT[q][:, f, t * P:(t + 1) * P], w2[ep][:, f, :],
                                         start=f == 0, stop=False)
                        if f == FC - 1:
                            pe.matmul(psY[t][:, 0:D], ones[:], b2[ep][:], start=False, stop=True).then_inc(y_ps, 1)

                for f in range(FC):
                    first(f)
                    if f >= LAG:
                        second(f - LAG)
                for f in range(FC - LAG, FC):
                    second(f)
            with pe.Fori(0, E_N // 2) as i:
                for ep in range(2):
                    with pe.Fori(0, B // 2) as k:
                        for q in range(2):
                            body(i * (2 * B) + k * 2 + (ep * B + q), i * 2 + ep, ep, k * 2 + q, q)
                    pe.drain().then_inc(w_used, 1)

        @block.scalar
        def _(act):
            act.wait_ge(in_sb, n_in)

            def body(W, e, ep, tb, q):
                act.wait_ge(w_in[ep], (e - ep) * 32 + 64)
                for f in range(FC):
                    act.wait_ge(h_ps, W * FC + (f + 1))
                    act.activation(hT[q][:, f, :], psH[f % 4][:], ACT.Gelu_apprx_tanh,
                                   bias=b1[ep][:, f:f + 1]).then_inc(h_ready, 1)

            units(act, body)

        @block.vector
        def _(dve):
            dve.wait_ge(in_sb, n_in)

            def body(W, e, ep, tb, q):
                for t in range(TT):
                    dve.wait_ge(y_ps, W * TT + (t + 1))
                    row = acc[:, ds(tb * TT + t, 1), :].rearrange("p o d -> p (o d)")
                    g = gates[:, ds(tb * TT + t, 1), ds(e, 1)].rearrange("p o e -> p (o e)")
                    dve.scalar_tensor_tensor(out=row, in0=psY[t][:, 0:D], scalar=g, in1=row,
                                             op0=ALU.mult, op1=ALU.add).then_inc(y_free, 1)

            units(dve, body)


def phase_last(nc, c, w, scr):
    wi = [c.sb(f"wi{k}", [P, DC * F2], I32) for k in range(3)]
    wgate, wup = c.sb("wgate", [P, DC, F2]), c.sb("wup", [P, DC, F2])
    wdown = c.sb("wdown", [P, F2C, D])
    wq, wk, wv = (c.sb(n, [P, DC, D]) for n in ("wq", "wk", "wv"))
    bq, bk, bv = c.sb("bq", [P, DC]), c.sb("bk", [P, DC]), c.sb("bv", [P, D])
    ident = c.sb("ident", [P, P])
    xin = [c.sb(f"xin{p}", [P, TT, D]) for p in range(2)]
    cin = [c.sb(f"cin{p}", [P, DC, S]) for p in range(2)]
    xo = [c.sb(f"xo{p}", [P, TT, D]) for p in range(2)]
    x3 = c.sb("x3", [P, TT, D])
    y = c.sb("y", [P, TT, D])
    yT = c.sb("yT", [P, DC, S])
    kT, qT = c.sb("kT", [P, DC, S]), c.sb("qT", [P, DC, S])
    vv = c.sb("vv", [P, TT, D])
    pr = c.sb("pr", [P, TT, S])
    pT = c.sb("pT", [P, TT, S])
    sg = c.sb("sg", [P, 2, S])
    hT = c.sb("hT", [P, F2C, S])
    stats, mv, rstd = c.sb("stats", [P, TT, 6]), c.sb("mv", [P, TT, 2]), c.sb("rstd", [P, TT])
    nmax, tot, rec = c.sb("nmax", [P, TT]), c.sb("tot", [P, TT]), c.sb("rec", [P, TT])
    psT = c.ps("psT", [P, 2 * S])
    psG = [c.ps(f"psG{k}", [P, S]) for k in range(2)]
    psU = [c.ps(f"psU{k}", [P, S]) for k in range(2)]
    psB = [c.ps(f"psB{k}", [P, S]) for k in range(2)]
    (const_in, set_done, w_ready, x_used, c_used, y_ready, t_ps, t_free, g_ps, g_free, u_ps, u_free, s_free, max_ready,
     b_ps, b_free, sg_ready, h_ready, xo_ready, dve_own, act_own, sum_ready) = (
        c.sem(n) for n in ("const_in", "set_done", "w_ready", "x_used", "c_used", "y_ready", "t_ps", "t_free", "g_ps",
                           "g_free", "u_ps", "u_free", "s_free", "max_ready", "b_ps", "b_free", "sg_ready",
                           "h_ready", "xo_ready", "dve_own", "act_own", "sum_ready"))
    x_in, c_in, x_out = ([c.sem(f"{n}{p}") for p in range(2)] for n in ("x_in", "c_in", "x_out"))
    var_ready, rstd_ready = c.sem("var_ready"), c.sem("rstd_ready")
    c.half_power = (c.sb("power", [P, TT]), c.sb("var", [P, TT]), c.sb("eps", [P, TT]), c.sem("pool_own"))
    NORMS = 2
    GU = 2 * DC + F2C
    UU = TT + F2C
    BU = 3 * TT
    TU = TT + 2
    consts = [(wi[0][:], w["gate"]), (wi[1][:], w["up"]), (wi[2][:], w["down"]), (wq[:], w["wq"]), (wk[:], w["wk"]),
              (wv[:], w["wv"]), (bq[:], w["bq"]), (bk[:], w["bk"]), (bv[:], w["bv"])]

    with nc.Block() as block:

        @block.sync
        def _(sp):
            for dst, src in consts:
                sp.dma_start(dst, src).then_inc(const_in, 16)
            sp.sem_inc(x_used, 2)
            sp.sem_inc(c_used, 2)

            def load(n, par):
                sp.wait_ge(x_used, n + 1)
                sp.dma_start(xin[par][:], scr["x2"][ds(n, 1)].rearrange("o (t p) d -> p (o t) d", p=P)
                             ).then_inc(x_in[par], 16)
                sp.wait_ge(c_used, n + 1)
                sp.dma_start(cin[par][:], scr["ctxT"][ds(n, 1)].rearrange("o (c p) s -> p (o c) s", p=P)
                             ).then_inc(c_in[par], 16)

            load(0, 0)

            def body(n, par):
                if not (isinstance(n, int) and n == B - 1):
                    load(n + 1, 1 - par)
                sp.wait_ge(xo_ready, n + 1)
                sp.dma_start(scr["out"][ds(n, 1)].rearrange("o (t p) d -> p (o t) d", p=P), xo[par][:]
                             ).then_inc(x_out[par], 16)

            by_pairs(sp, body, peel_last=True)
            for par in range(2):
                sp.wait_ge(x_out[par], 16 * (B // 2))

        @block.gpsimd
        def _(pool):
            pool.memset(ident[:], 0.0).then_inc(set_done, 1)
            pool.wait_ge(set_done, 1)
            pool.affine_select(out=ident[:], in_=ident[:], compare_op=ALU.not_equal, fill=1.0, base=0,
                               pattern=[[-1, P]], channel_multiplier=1).then_inc(set_done, 1)
            inverse_deviations(pool, c, mv, rstd, var_ready, rstd_ready, B * NORMS)

        @block.vector
        def _(dve):
            link = Chain(dve, dve_own)
            dve.wait_ge(const_in, 16 * len(consts))
            dve.tensor_copy(wgate[:].rearrange("p c f -> p (c f)"), wi[0][:])
            dve.tensor_copy(wup[:].rearrange("p c f -> p (c f)"), wi[1][:])
            dve.tensor_copy(wdown[:].rearrange("p c d -> p (c d)"), wi[2][:]).then_inc(w_ready, 1)

            norms = [0]

            def norm(n, src):
                for t in range(TT):
                    last = dve.bn_stats(stats[:, t, :], src[:, t, :])
                link(last)
                for t in range(TT):
                    last = dve.bn_aggr(mv[:, t, :], stats[:, t, :])
                last.then_inc(var_ready, 1)
                norms[0] += 1
                dve.wait_ge(rstd_ready, n * NORMS + norms[0])
                for t in range(TT):
                    last = dve.tensor_scalar(y[:, t, :], src[:, t, :], mv[:, t, 0:1], rstd[:, t:t + 1],
                                             ALU.subtract, ALU.mult)
                last.then_inc(y_ready, 1)

            def body(n, par):
                    dve.wait_ge(x_in[par], (n - par) * 8 + 16)
                    dve.wait_ge(t_ps, n * TU)
                    norm(n, xin[par])
                    for t in range(TT):
                        dve.wait_ge(b_ps, n * BU + t + 1)
                        dve.tensor_tensor(vv[:, t, :], psB[t % 2][:, 0:D], bv[:], ALU.add).then_inc(b_free, 1)
                    for t in range(TT):
                        dve.wait_ge(u_ps, n * UU + t + 1)
                        dve.tensor_reduce(nmax[:, t:t + 1], psU[t % 2][:], axis=AX.X, op=ALU.max, negate=True
                                          ).then_inc(max_ready, 1)
                    dve.wait_ge(sum_ready, n * TT + TT)
                    link(dve.reciprocal(rec[:], tot[:]))
                    link(dve.tensor_scalar(rec[:], rec[:], 1.0 / 16.0, None, ALU.mult))
                    for t in range(TT):
                        dve.wait_ge(b_ps, n * BU + TT + t + 1)
                        dve.scalar_tensor_tensor(out=x3[:, t, :], in0=psB[t % 2][:, 0:D], scalar=rec[:, t:t + 1],
                                                 in1=xin[par][:, t, :], op0=ALU.mult, op1=ALU.add).then_inc(b_free, 1)
                    dve.drain().then_inc(x_used, 1)
                    norm(n, x3)
                    for f in range(F2C):
                        dve.wait_ge(u_ps, n * UU + TT + f + 1)
                        dve.wait_ge(sg_ready, n * F2C + f + 1)
                        dve.scalar_tensor_tensor(out=hT[:, f, :], in0=psU[f % 2][:], scalar=SCALE2, in1=sg[:, f % 2, :],
                                                 op0=ALU.mult, op1=ALU.mult).then_inc(u_free, 1)
                    dve.wait_ge(x_out[par], (n - par) * 8)
                    for t in range(TT):
                        dve.wait_ge(b_ps, n * BU + 2 * TT + t + 1)
                        dve.scalar_tensor_tensor(out=xo[par][:, t, :], in0=psB[t % 2][:, 0:D], scalar=SCALE2,
                                                 in1=x3[:, t, :], op0=ALU.mult, op1=ALU.add).then_inc(b_free, 1)
                    dve.drain().then_inc(xo_ready, 1)
                    link.reset()
                    norms[0] = 0

            by_pairs(dve, body)

        @block.scalar
        def _(act):
            act.wait_ge(const_in, 16 * len(consts))

            def body(n, par):
                    for u in range(DC):
                        act.wait_ge(g_ps, n * GU + u + 1)
                        act.activation(kT[:, u, :], psG[u][:], ACT.Identity, bias=bk[:, u:u + 1]).then_inc(g_free, 1)
                    act.wait_ge(t_ps, n * TU + 1)
                    act.copy(yT[:].rearrange("p c s -> p (c s)"), psT[:]).then_inc(t_free, 1)
                    for u in range(DC):
                        act.wait_ge(g_ps, n * GU + DC + u + 1)
                        act.activation(qT[:, u, :], psG[u][:], ACT.Identity, bias=bq[:, u:u + 1]).then_inc(g_free, 1)
                    for t in range(TT):
                        act.wait_ge(max_ready, n * TT + t + 1)
                        act.activation(pr[:, t, :], psU[t % 2][:], ACT.Exp, bias=nmax[:, t:t + 1],
                                       accum_out=tot[:, t:t + 1]).then_inc(s_free, 1)
                    act.drain().then_inc(sum_ready, TT)
                    for t in range(TT):
                        act.wait_ge(t_ps, n * TU + 1 + t + 1)
                        act.copy(pT[:, :, t * P:(t + 1) * P], psT[:, (t % 2) * S:(t % 2 + 1) * S]
                                 .rearrange("p (k q) -> p k q", k=TT)).then_inc(t_free, 1)
                    act.wait_ge(t_ps, n * TU + TU)
                    act.copy(yT[:].rearrange("p c s -> p (c s)"), psT[:]).then_inc(t_free, 1)
                    for f in range(F2C):
                        act.wait_ge(g_ps, n * GU + 2 * DC + f + 1)
                        if f >= 2:
                            act.wait_ge(u_free, n * F2C + f - 1)
                        act.activation(sg[:, f % 2, :], psG[f % 2][:], ACT.Silu, scale=SCALE2).then_inc(g_free, 1)
                        act.drain().then_inc(sg_ready, 1)

            by_pairs(act, body)

        @block.tensor
        def _(pe):
            pe.wait_ge(const_in, 16 * len(consts))
            pe.wait_ge(w_ready, 1)
            pe.wait_ge(set_done, 2)
            pe.sem_inc(g_free, 2)
            pe.sem_inc(b_free, 2)

            def wide(n, j, bank, wt, u, src):
                for d in range(DC):
                    last = pe.matmul(bank[:], wt[:, d, u * P:(u + 1) * P], src[:, d, :], start=d == 0, stop=d == DC - 1)
                return last

            def body(n, par):
                    pe.wait_ge(c_in[par], (n - par) * 8 + 16)
                    for u in range(DC):
                        pe.wait_ge(g_free, n * GU + u + 1)
                        wide(n, u, psG[u], wk, u, cin[par]).then_inc(g_ps, 1)
                    for t in range(TT):
                        pe.wait_ge(b_free, n * BU + t + 1)
                        for d in range(DC):
                            last = pe.matmul(psB[t % 2][:, 0:D], cin[par][:, d, t * P:(t + 1) * P], wv[:, d, :],
                                             start=d == 0, stop=d == DC - 1)
                        last.then_inc(b_ps, 1)
                    pe.drain().then_inc(c_used, 1)

                    def transpose_y(k):
                        pe.wait_ge(y_ready, n * 2 + k + 1)
                        pe.wait_ge(t_free, n * TU + k * (TT + 1))
                        for t in range(TT):
                            for d in range(DC):
                                last = pe.transpose(psT[:, d * S + t * P:d * S + (t + 1) * P],
                                                    y[:, t, d * P:(d + 1) * P], ident[:])
                        last.then_inc(t_ps, 1)

                    transpose_y(0)
                    pe.wait_ge(t_free, n * TU + 1)
                    for u in range(DC):
                        pe.wait_ge(g_free, n * GU + DC + u + 1)
                        wide(n, u, psG[u], wq, u, yT).then_inc(g_ps, 1)
                    pe.wait_ge(g_free, n * GU + 2 * DC + 2)
                    for t in range(TT):
                        pe.wait_ge(s_free, n * TT + t - 1) if t >= 2 else pe.wait_ge(u_free, n * F2C)
                        for d in range(DC):
                            last = pe.matmul(psU[t % 2][:], qT[:, d, t * P:(t + 1) * P], kT[:, d, :],
                                             start=d == 0, stop=d == DC - 1)
                        last.then_inc(u_ps, 1)
                    for t in range(TT):
                        pe.wait_ge(s_free, n * TT + t + 1)
                        pe.wait_ge(t_free, n * TU + 1 + max(t - 1, 0))
                        for k in range(TT):
                            last = pe.transpose(psT[:, (t % 2) * S + k * P:(t % 2) * S + (k + 1) * P],
                                                pr[:, t, k * P:(k + 1) * P], ident[:])
                        last.then_inc(t_ps, 1)
                    for t in range(TT):
                        pe.wait_ge(t_free, n * TU + 1 + t + 1)
                        pe.wait_ge(b_free, n * BU + TT + t + 1)
                        for k in range(TT):
                            last = pe.matmul(psB[t % 2][:, 0:D], pT[:, k, t * P:(t + 1) * P], vv[:, k, :],
                                             start=k == 0, stop=k == TT - 1)
                        last.then_inc(b_ps, 1)
                    transpose_y(1)
                    pe.wait_ge(t_free, n * TU + TU)
                    for f in range(F2C):
                        pe.wait_ge(g_free, n * GU + 2 * DC + f + 1)
                        wide(n, f, psG[f % 2], wgate, f, yT).then_inc(g_ps, 1)
                        if f < 2:
                            pe.wait_ge(s_free, n * TT + TT)
                        else:
                            pe.wait_ge(u_free, n * F2C + f - 1)
                        wide(n, f, psU[f % 2], wup, f, yT).then_inc(u_ps, 1)
                    pe.wait_ge(u_free, n * F2C + F2C)
                    for t in range(TT):
                        pe.wait_ge(b_free, n * BU + 2 * TT + t + 1)
                        for f in range(F2C):
                            last = pe.matmul(psB[t % 2][:, 0:D], hT[:, f, t * P:(t + 1) * P], wdown[:, f, :],
                                             start=f == 0, stop=f == F2C - 1)
                        last.then_inc(b_ps, 1)

            by_pairs(pe, body)


def phase_mask(nc, c, mask, dst):
    m8, row = c.sb("m8", [B, S], U8), c.sb("row", [B, S], BF16)
    m_in, m_ready, m_out = c.sem("in"), c.sem("ready"), c.sem("out")
    with nc.Block() as block:

        @block.sync
        def _(sp):
            sp.dma_start(m8[:], mask).then_inc(m_in, 16)
            sp.wait_ge(m_ready, 1)
            sp.dma_start(dst, row[:]).then_inc(m_out, 16)
            sp.wait_ge(m_out, 16)

        @block.vector
        def _(dve):
            dve.wait_ge(m_in, 16)
            dve.tensor_scalar(row[:], m8[:], 1.0, -NEG, ALU.subtract, ALU.mult).then_inc(m_ready, 1)


def build(nc, a, out):
    def scratch(name, shape, dt=F32):
        return nc.dram_tensor(f"s_{name}", shape, dt).ap()

    qk0, qk1 = (scratch(f"qk{k}", [B * DC, 2, NTERM, P, S], BF16) for k in range(2))
    v0, v1 = (scratch(f"v{k}", [B, S, H * HP]) for k in range(2))
    o0, o1 = (scratch(f"o{k}", [G_ALL, P, S]) for k in range(2))
    mask = scratch("mask", [B, S], BF16)
    x1, y1, base, x2 = (scratch(n, [B, S, D]) for n in ("x1", "y1", "base", "x2"))
    xfT = scratch("xfT", [B, D, S])
    gates = scratch("gates", [B, P, TT, E_N])

    def chunks(ap):
        return ap.rearrange("(c p) n -> p c n", p=P)

    def phase(tag, run, *args):
        with ExitStack() as stack:
            c = Ctx(nc, tag, stack)
            run(nc, c, *args)
            for sem in c.sems:
                nc.sync.sem_clear(sem)
            nc.all_engine_barrier()

    phase("mask", phase_mask, a["mask"], mask)
    phase("t0", phase_tokens, 0,
          {"wk": chunks(a["wk0"]), "wq": chunks(a["wq0"]), "wv": chunks(a["wv0"]), "bk": a["bk0"], "bq": a["bq0"],
           "bv": a["bv0"].partition_broadcast(P)},
          {"x_src": a["x"], "c_src": a["ctxT"], "qk": qk0, "v": v0})
    phase("a0", phase_attention, False, {"qk": qk0, "v": v0, "mask": mask, "o": o0})
    phase("t1", phase_tokens, 1,
          {"wk": chunks(a["wk1"]), "wq": chunks(a["wq1"]), "wv": chunks(a["wv1"]), "wo": chunks(a["wo0"]),
           "bo": a["bo0"], "lng": a["g1"], "lnb": a["be1"]},
          {"x_src": a["x"], "c_src": o0, "x_dst": x1, "y_dst": y1, "qk": qk1, "v": v1})
    phase("a1", phase_attention, True, {"qk": qk1, "v": v1, "o": o1})
    phase("t2", phase_tokens, 2,
          {"wo": chunks(a["wo1"]), "lng": a["g2"], "lnb": a["be2"], "wg": chunks(a["wg"])},
          {"x_src": x1, "y_src": y1, "c_src": o1, "x_dst": base, "xfT": xfT, "gates": gates})
    phase("ex", phase_experts, {}, {"w1": a["w1"], "w2": a["w2"], "b1": a["b1"], "b2": a["b2"], "xfT": xfT,
                                    "base": base, "gates": gates, "x2": x2})
    phase("la", phase_last,
          {"gate": chunks(a["gate"]), "up": chunks(a["up"]), "down": chunks(a["down"]), "wq": chunks(a["wq2"]),
           "wk": chunks(a["wk2"]), "wv": chunks(a["wv2"]), "bq": a["bq2"], "bk": a["bk2"],
           "bv": a["bv2"].partition_broadcast(P)},
          {"x2": x2, "ctxT": a["ctxT"], "out": out})


def kernel(**inputs):
    import concourse.bacc as bacc
    from concourse.bass_utils import run_bass_kernel_spmd

    t = {k: np.asarray(v) for k, v in inputs.items()}
    order = np.array([(blk * 8 + h) * HD + d for blk in range(DC) for d in range(HD) for h in range(8)])

    def cols(v):
        return v.reshape(-1, P).T

    def padded(wt):
        out = np.zeros((H, HP, D), wt.dtype)
        out[:, :HD] = wt.reshape(H, HD, D)
        return out.reshape(H * HP, D)

    qkv = t["L0_ffn_w_qkv"]
    arrays = {
        "x": t["x"], "ctxT": t["ctx_1024"].transpose(0, 2, 1),
        "mask": t["mask_Bx1xS2_bf1"].reshape(B, S).view(np.uint8),
        "wk0": t["L0_xattn_Wk"].T[:, order], "wq0": t["L0_xattn_Wq"].T[:, order], "wv0": t["L0_xattn_Wv"].T,
        "bk0": cols(t["L0_xattn_bk"][order]), "bq0": cols(t["L0_xattn_bq"][order]), "bv0": t["L0_xattn_bv"],
        "wo0": padded(t["L0_xattn_Wo"].T), "bo0": t["L0_xattn_bo"].reshape(1, D),
        "g1": cols(t["L0_ffn_ln1_g"]), "be1": cols(t["L0_ffn_ln1_b"]),
        "g2": cols(t["L0_ffn_ln2_g"]), "be2": cols(t["L0_ffn_ln2_b"]),
        "wq1": qkv[:, 0:D][:, order], "wk1": qkv[:, D:2 * D][:, order], "wv1": qkv[:, 2 * D:],
        "wo1": padded(t["L0_ffn_w_o"]), "wg": t["L0_ffn_w_gate"],
        "w1": t["L0_ffn_w1"], "w2": t["L0_ffn_w2"], "b1": t["L0_ffn_b1"].reshape(E_N, FC, P).transpose(0, 2, 1),
        "b2": t["L0_ffn_b2"],
        "wq2": t["L1_xattn_Wq"], "wk2": t["L1_xattn_Wk"], "wv2": t["L1_xattn_Wv"],
        "bq2": cols(t["L1_xattn_bq"]), "bk2": cols(t["L1_xattn_bk"]), "bv2": t["L1_xattn_bv"],
        "gate": t["L1_ffn_w_gate"].T, "up": t["L1_ffn_w_up"].T, "down": t["L1_ffn_w_down"].T,
    }
    nc = bacc.Bacc("TRN2", target_bir_lowering=False, num_devices=1)
    feed, args = {}, {}
    for name, v in arrays.items():
        feed[f"in_{name}"] = np.ascontiguousarray(v)
        args[name] = nc.dram_tensor(f"in_{name}", v.shape, mybir.dt.from_np(v.dtype), kind="ExternalInput").ap()
    out = nc.dram_tensor("out_x", (B, S, D), F32, kind="ExternalOutput").ap()
    build(nc, args, out)
    return run_bass_kernel_spmd(nc, [feed], core_ids=[0]).results[0]["out_x"]
```

```python
import numpy as np
import concourse.bass as bass
from concourse import mybir
from contextlib import ExitStack

F32 = mybir.dt.float32
BF16 = mybir.dt.bfloat16
I32 = mybir.dt.int32
U8 = mybir.dt.uint8
U32 = mybir.dt.uint32
F16 = mybir.dt.float16
ALU = mybir.AluOpType
ACT = mybir.ActivationFunctionType
AX = mybir.AxisListType
ds = bass.ds

P = 128
B, S, D = 8, 512, 256
TT = S // P
DC = D // P
H, HD = 16, 16
HP = 32
GH = 4
NG = H // GH
G_ALL = B * NG
EPS = 1e-5
NEG = -1e30
E_N, FF = 8, 1024
FC = FF // P
NT = B * TT
TE = 256
CHOSEN = 2
TILES = CHOSEN * B * S // TE + E_N - 1
WSCALE = 64.0
F2 = 768
F2C = F2 // P
SCALE2 = 1.0 / 127.0
NPART = 3
NTERM = 6
KM = NTERM * HD
K_MAX = KM + 1
K_EXP = KM + 1 + NPART


class Chain:

    def __init__(self, eng, sem):
        self.eng, self.sem, self.n = eng, sem, 0

    def __call__(self, ins):
        self.n += 1
        ins.then_inc(self.sem, 1)
        self.eng.wait_ge(self.sem, self.n)

    def reset(self):
        self.eng.sem_clear(self.sem)
        self.n = 0


def by_pairs(eng, body, peel_last=False):
    for par in range(2):
        body(par, par)
    with eng.Fori(1, B // 2 - peel_last) as i:
        for par in range(2):
            body(i * 2 + par, par)
    if peel_last:
        for par in range(2):
            body(B - 2 + par, par)


def inverse_deviations(pool, c, mv, rstd, var_ready, rstd_ready, times):
    power, var, eps, own = c.half_power
    pool.memset(power[:], -0.5).then_inc(own, 1)
    pool.memset(eps[:], EPS).then_inc(own, 1)
    pool.wait_ge(own, 2)
    with pool.Fori(0, times) as k:
        pool.wait_ge(var_ready, k + 1)
        pool.tensor_tensor(var[:], mv[:, :, 1], eps[:], ALU.add).then_inc(own, 1)
        pool.wait_ge(own, k + 3)
        pool.tensor_tensor(rstd[:], var[:], power[:], ALU.pow).then_inc(rstd_ready, 1)


class Ctx:

    def __init__(self, nc, tag, stack):
        self.nc, self.tag, self.stack, self.sems = nc, tag, stack, []

    def sb(self, name, shape, dt=F32):
        return self.stack.enter_context(self.nc.sbuf_tensor(f"{self.tag}_{name}", shape, dt))

    def ps(self, name, shape, dt=F32):
        return self.stack.enter_context(self.nc.psum_tensor(f"{self.tag}_{name}", shape, dt))

    def sem(self, name):
        self.sems.append(self.stack.enter_context(self.nc.semaphore(f"{self.tag}_{name}")))
        return self.sems[-1]


def phase_tokens(nc, c, stage, w, scr):
    xin = [c.sb(f"xin{p}", [P, TT, D]) for p in range(2)]
    cin = [c.sb(f"cin{p}", [P, DC, S] if stage == 0 else [P, NG, S]) for p in range(2)]
    y = [c.sb(f"y{p}", [P, TT, D]) for p in range(2)]
    y0 = [c.sb(f"y0{p}", [P, TT, D]) for p in range(2)]
    XS = 2 if stage == 1 else 1
    XL = 2 if stage == 2 else 1
    yT = c.sb("yT", [P, DC, S])
    stats = c.sb("stats", [P, TT, 6])
    mv = c.sb("mv", [P, TT, 2])
    rstd = c.sb("rstd", [P, TT])
    xo = [c.sb(f"xo{p}", [P, TT, D]) for p in range(2)]
    ident = c.sb("ident", [P, P])
    psT = c.ps("psT", [P, DC * S])
    psQ = [c.ps(f"psQ{k}", [P, S]) for k in range(2)]
    NV = TT
    psV = [c.ps(f"psV{k}", [P, 512]) for k in range(NV)]
    if stage < 2:
        full = c.sb("full", [P, 2, DC, S])
        rest = c.sb("rest", [P, DC, S])
        parts = [c.sb(f"parts{p}", [P, 2, NPART, DC, S], BF16) for p in range(2)]
        vaug = [c.sb(f"vaug{p}", [P, TT, H, HP]) for p in range(2)]
        wk, wq, wv = (c.sb(n, [P, DC, D]) for n in ("wk", "wq", "wv"))
        bv = c.sb("bv", [P, D])
        bk, bq = c.sb("bk", [P, DC]), c.sb("bq", [P, DC])
    if stage == 2:
        wg = c.sb("wg", [P, DC, E_N])
        lg = c.sb("lg", [P, TT, E_N])
        lmax = c.sb("lmax", [P, TT])
        ex = c.sb("ex", [P, TT, E_N])
        gt = c.sb("gt", [P, TT, E_N, E_N])
        eq = c.sb("eq", [P, TT, E_N, E_N])
        lower = c.sb("lower", [P, E_N, E_N])
        tot = c.sb("tot", [P, TT])
        gate = [c.sb(f"gate{p}", [P, TT, 2, E_N]) for p in range(2)]
        gT = c.sb("gT", [E_N, S])
        b2 = c.sb("b2", [E_N, D])
        lngr, lnbr = c.sb("lngr", [P, D]), c.sb("lnbr", [P, D])
        xfs = [c.sb(f"xfs{p}", [P, TT, 2, D], F16) for p in range(2)]
    if stage > 0:
        wo = c.sb("wo", [P, NG, D])
        lng, lnb = c.sb("lng", [P, DC]), c.sb("lnb", [P, DC])
    if stage == 1:
        bo = c.sb("bo", [1, D])
    ones = c.sb("ones", [1, P])

    n_const = [0]
    const_in = c.sem("const_in")
    set_done = c.sem("set_done")
    x_in = [c.sem(f"x_in{p}") for p in range(2)]
    c_in = [c.sem(f"c_in{p}") for p in range(2)]
    x_used, c_used = c.sem("x_used"), c.sem("c_used")
    y_ready, tr_ps, yT_ready = c.sem("y_ready"), c.sem("tr_ps"), c.sem("yT_ready")
    q_ps, q_free, v_ps, v_free = c.sem("q_ps"), c.sem("q_free"), c.sem("v_ps"), c.sem("v_free")
    full_ready, split_done = c.sem("full_ready"), c.sem("split_done")
    v_ready = c.sem("v_ready")
    qk_out = [c.sem(f"qk_out{p}") for p in range(2)]
    v_out = [c.sem(f"v_out{p}") for p in range(2)]
    x_out = [c.sem(f"x_out{p}") for p in range(2)]
    xo_ready, gates_ready, logit_ready, exp_ready = (
        c.sem("xo_ready"), c.sem("gates_ready"), c.sem("logit_ready"), c.sem("exp_ready"))
    yT_used = c.sem("yT_used")
    y0_ready = c.sem("y0_ready")
    var_ready, rstd_ready = c.sem("var_ready"), c.sem("rstd_ready")
    c.half_power = (c.sb("power", [P, TT]), c.sb("var", [P, TT]), c.sb("eps", [P, TT]), c.sem("pool_own"))
    NORMS = 2 if stage == 1 else 1
    dve_own, act_own = c.sem("dve_own"), c.sem("act_own")
    QK = 4
    VU = {0: TT, 1: 2 * TT, 2: 3 * TT}[stage]

    def projected(n):
        return 0 if isinstance(n, int) and n == 0 else n * VU - TT

    def last_units(n):
        if stage == 0:
            return n * VU
        return n * VU + (VU - TT if isinstance(n, int) and n == B - 1 else VU)

    QKD = 2 * DC * NPART
    consts = []
    if stage < 2:
        consts += [(wk, w["wk"]), (wq, w["wq"]), (wv, w["wv"])]
        if stage == 0:
            consts += [(bk, w["bk"]), (bq, w["bq"])]
    if stage > 0:
        consts += [(wo, w["wo"])]
    if stage == 1:
        consts += [(bo, w["bo"]), (lng, w["lng"]), (lnb, w["lnb"])]
    if stage == 2:
        consts += [(wg, w["wg"]), (b2, w["b2"]), (lngr, w["lngr"]), (lnbr, w["lnbr"])]
    hi_ready, xfs_ready, gT_ps, gT_ready = c.sem("hi_ready"), c.sem("xfs_ready"), c.sem("gT_ps"), c.sem("gT_ready")
    if stage == 0:
        consts += [(bv, w["bv"])]
    n_consts = len(consts)

    with nc.Block() as block:

        @block.sync
        def _(sp):
            for tile, src in consts:
                sp.dma_start(tile[:], src).then_inc(const_in, 16)

            def load(n, par):
                sp.wait_ge(x_used, n + 1)
                sp.dma_start(xin[par][:], scr["x_src"][ds(n, 1)].rearrange("o (t p) d -> p (o t) d", p=P)
                             ).then_inc(x_in[par], 16)
                if stage == 2:
                    sp.dma_start(y0[par][:], scr["y_src"][ds(n, 1)].rearrange("o (t p) d -> p (o t) d", p=P)
                                 ).then_inc(x_in[par], 16)
                sp.wait_ge(c_used, n + 1)
                if stage == 0:
                    src = scr["c_src"][ds(n, 1)].rearrange("o (c p) s -> p (o c) s", p=P)
                else:
                    src = scr["c_src"][ds(n * NG, NG)].rearrange("g p s -> p g s")
                sp.dma_start(cin[par][:], src).then_inc(c_in[par], 16)

            def store_x(n, par):
                sp.wait_ge(xo_ready, n + 1)
                sp.dma_start(scr["x_dst"][ds(n, 1)].rearrange("o (t p) d -> p (o t) d", p=P), xo[par][:]
                             ).then_inc(x_out[par], 16)

            def store(n, par):
                if stage == 1:
                    store_x(n, par)
                if stage == 1:
                    sp.wait_ge(y0_ready, n + 1)
                    sp.dma_start(scr["y_dst"][ds(n, 1)].rearrange("o (t p) d -> p (o t) d", p=P), y0[par][:]
                                 ).then_inc(x_out[par], 16)
                if stage == 2:
                    sp.wait_ge(xfs_ready, n + 1)
                    sp.dma_start(scr["xfs"][ds(n, 1)].rearrange("o (t p) c -> p (o t) c", p=P),
                                 xfs[par][:].rearrange("p t r d -> p t (r d)")).then_inc(v_out[par], 16)
                    sp.wait_ge(gates_ready, n + 1)
                    sp.dma_start(scr["gates"][ds(n, 1)].rearrange("o p t r e -> p (o t r e)"),
                                 gate[par][:].rearrange("p t r e -> p (t r e)")).then_inc(qk_out[par], 16)
                    store_x(n, par)
                    return
                for k in range(2):
                    sp.wait_ge(split_done, n * 2 + k + 1)
                    for blk in range(DC):
                        at = 0
                        for r in range(NPART):
                            m = NPART - r
                            src = parts[par][:, k, 0:m, blk, :] if k == 0 else (
                                parts[par][:, k, r:r + 1, blk, :].to_broadcast([P, m, S]))
                            sp.dma_start(scr["qk"][ds(n * DC + blk, 1), k, at:at + m].rearrange("o t p s -> p (o t) s"),
                                         src).then_inc(qk_out[par], 16)
                            at += m
                sp.wait_ge(v_ready, n + 1)
                sp.dma_start(scr["v"][ds(n, 1)].rearrange("o (t p) c -> p (o t) c", p=P),
                             vaug[par][:].rearrange("p t h c -> p t (h c)")).then_inc(v_out[par], 16)

            sp.sem_inc(x_used, 2)
            sp.sem_inc(c_used, 2)
            load(0, 0)
            load(1, 1)

            def body(n, par):
                if not (isinstance(n, int) and n >= B - 2):
                    load(n + 2, par)
                store(n, par)

            by_pairs(sp, body, peel_last=True)
            for par in range(2):
                if stage < 2:
                    sp.wait_ge(qk_out[par], 16 * QKD * (B // 2))
                else:
                    sp.wait_ge(qk_out[par], 16 * (B // 2))
                sp.wait_ge(v_out[par], 16 * (B // 2))
                if stage > 0:
                    sp.wait_ge(x_out[par], 16 * XS * (B // 2))

        @block.gpsimd
        def _(pool):
            pool.memset(ident[:], 0.0).then_inc(set_done, 1)
            pool.wait_ge(set_done, 1)
            pool.affine_select(out=ident[:], in_=ident[:], compare_op=ALU.not_equal, fill=1.0, base=0,
                               pattern=[[-1, P]], channel_multiplier=1).then_inc(set_done, 1)
            pool.memset(ones[:], 1.0).then_inc(set_done, 1)
            if stage < 2:
                for p in range(2):
                    pool.memset(vaug[p][:], 0.0).then_inc(set_done, 1)
                pool.wait_ge(set_done, 5)
                for p in range(2):
                    pool.memset(vaug[p][:, :, :, HD:HD + 1], 1.0).then_inc(set_done, 1)
            else:
                pool.memset(lower[:], 0.0).then_inc(set_done, 1)
                pool.wait_ge(set_done, 4)
                pool.affine_select(out=lower[:], in_=lower[:], compare_op=ALU.is_ge, fill=1.0, base=0,
                                   pattern=[[-1, E_N], [1, E_N]], channel_multiplier=0).then_inc(set_done, 1)
            inverse_deviations(pool, c, mv, rstd, var_ready, rstd_ready, B * NORMS)

        n_set = 7 if stage < 2 else 5

        @block.vector
        def _(dve):
            link = Chain(dve, dve_own)
            dve.wait_ge(set_done, n_set)
            dve.wait_ge(const_in, 16 * n_consts)

            def norm(k, src, dst):
                for t in range(TT):
                    last = dve.bn_stats(stats[:, t, :], src[:, t, :])
                link(last)
                for t in range(TT):
                    last = dve.bn_aggr(mv[:, t, :], stats[:, t, :])
                last.then_inc(var_ready, 1)
                dve.wait_ge(rstd_ready, k + 1)
                for t in range(TT):
                    last = dve.tensor_scalar(dst[:, t, :], src[:, t, :], mv[:, t, 0:1], rstd[:, t:t + 1],
                                             ALU.subtract, ALU.mult)
                return last

            def split(n, par, k):
                dve.wait_ge(full_ready, n * QK + DC * (k + 1))
                dve.wait_ge(split_done, n * 2 + k)
                a = parts[par]
                link(dve.tensor_tensor(rest[:], full[:, k], a[:, k, 0], ALU.subtract))
                link(dve.tensor_copy(a[:, k, 1], rest[:]))
                dve.tensor_tensor(a[:, k, 2], rest[:], a[:, k, 1], ALU.subtract).then_inc(split_done, 1)

            def values(n, par):
                dve.wait_ge(v_out[par], (n - par) * 8)
                for t in range(TT):
                    dve.wait_ge(v_ps, last_units(n) + t + 1)
                    src = psV[t][:, 0:D].rearrange("p (h d) -> p h d", h=H)
                    dst = vaug[par][:, t, :, 0:HD]
                    if stage == 0:
                        last = dve.tensor_tensor(dst, src, bv[:].rearrange("p (h d) -> p h d", h=H), ALU.add)
                    else:
                        last = dve.tensor_copy(dst, src)
                    last.then_inc(v_free, 1)
                dve.drain().then_inc(v_ready, 1)

            def front(n, par):
                dve.wait_ge(x_in[par], (n - par) * (8 * XL) + 16 * XL)
                src = xin[par]
                if stage > 0:
                    dve.wait_ge(x_out[par], (n - par) * (8 * XS))
                    for t in range(TT):
                        dve.wait_ge(v_ps, projected(n) + t + 1)
                        last = dve.tensor_tensor(xo[par][:, t, :], psV[t][:, 0:D],
                                                 (y0 if stage == 2 else xin)[par][:, t, :], ALU.add)
                        last.then_inc(v_free, 1)
                    src = xo[par]
                    dve.wait_ge(v_free, projected(n) + TT + NV)
                if stage == 1:
                    dve.sem_inc(xo_ready, 1)
                    dve.sem_inc(x_used, 1)
                    link(norm(n * NORMS, src, y0[par]))
                    dve.sem_inc(y0_ready, 1)
                    src = y0[par]
                if not (isinstance(n, int) and n < 2):
                    dve.wait_ge(tr_ps, n - 1)
                last = norm(n * NORMS + NORMS - 1, src, y[par])
                if stage == 2:
                    link(last)
                    link(dve.tensor_tensor(y[par][:], y[par][:], lngr[:].unsqueeze(1).to_broadcast([P, TT, D]),
                                           ALU.mult))
                    last = dve.tensor_tensor(y[par][:], y[par][:], lnbr[:].unsqueeze(1).to_broadcast([P, TT, D]),
                                             ALU.add)
                link(last)
                dve.sem_inc(y_ready, 1)
                if stage == 0:
                    dve.sem_inc(x_used, 1)
                if stage == 2:
                    link(dve.tensor_tensor(xo[par][:], xo[par][:], xin[par][:], ALU.add))
                    dve.sem_inc(x_used, 1)

            def body(n, par):
                more = not (isinstance(n, int) and n == B - 1)
                if stage == 2:
                    experts(n, par)
                if more:
                    front(n + 1, 1 - par)
                if stage == 2:
                    dve.wait_ge(hi_ready, n + 1)
                    dve.tensor_tensor(xfs[par][:, :, 1, :], y[par][:], xfs[par][:, :, 0, :], ALU.subtract
                                      ).then_inc(xfs_ready, 1)
                    for t in range(TT):
                        dve.wait_ge(v_ps, last_units(n) + t + 1)
                        dve.tensor_tensor(xo[par][:, t, :], psV[t][:, 0:D], xo[par][:, t, :], ALU.add
                                          ).then_inc(v_free, 1)
                    dve.drain().then_inc(xo_ready, 1)
                else:
                    dve.wait_ge(qk_out[par], (n - par) * (8 * QKD))
                    split(n, par, 0)
                    if stage == 0:
                        values(n, par)
                        split(n, par, 1)
                    else:
                        split(n, par, 1)
                        values(n, par)
                link.reset()

            def experts(n, par):
                for t in range(TT):
                    dve.wait_ge(v_ps, n * VU + TT + t + 1)
                    last = dve.tensor_copy(lg[:, t, :], psV[t][:, 0:E_N])
                    last.then_inc(v_free, 1)
                dve.wait_ge(v_free, n * VU + 2 * TT + NV)
                link(dve.tensor_reduce(lmax[:], lg[:], axis=AX.X, op=ALU.max))
                dve.tensor_tensor(ex[:], lg[:], lmax[:, :].unsqueeze(2).to_broadcast([P, TT, E_N]), ALU.subtract
                                  ).then_inc(logit_ready, 1)
                mine = lg[:, :, :].unsqueeze(3).to_broadcast([P, TT, E_N, E_N])
                other = lg[:, :, :].unsqueeze(2).to_broadcast([P, TT, E_N, E_N])
                dve.tensor_tensor(gt[:], other, mine, ALU.is_gt)
                link(dve.tensor_tensor(eq[:], other, mine, ALU.is_equal))
                for t in range(TT):
                    last = dve.tensor_tensor(eq[:, t], eq[:, t], lower[:], ALU.mult)
                link(last)
                link(dve.tensor_tensor(gt[:], gt[:], eq[:], ALU.add))
                dve.wait_ge(qk_out[par], (n - par) * 8)
                rank = gate[par][:, :, 1, :]
                link(dve.tensor_reduce(rank, gt[:], axis=AX.X, op=ALU.add))
                dve.wait_ge(exp_ready, n + 1)
                for t in range(TT):
                    last = dve.scalar_tensor_tensor(out=ex[:, t, :], in0=gate[par][:, t, 1, :], scalar=CHOSEN - 0.5,
                                                    in1=ex[:, t, :], op0=ALU.is_lt, op1=ALU.mult)
                link(last)
                link(dve.tensor_reduce(tot[:], ex[:], axis=AX.X, op=ALU.add))
                link(dve.reciprocal(tot[:], tot[:]))
                dve.tensor_tensor(gate[par][:, :, 0, :], ex[:], tot[:, :].unsqueeze(2).to_broadcast([P, TT, E_N]),
                                  ALU.mult).then_inc(gates_ready, 1)

            front(0, 0)
            link.reset()
            by_pairs(dve, body, peel_last=True)

        @block.scalar
        def _(act):
            link = Chain(act, act_own)
            act.wait_ge(const_in, 16 * n_consts)
            act.wait_ge(set_done, n_set)
            if stage == 0:
                link(act.mul(bq[:], bq[:], 0.25))

            def project(n, par, k, scale, bias):
                if not (isinstance(n, int) and n == 0):
                    act.wait_ge(split_done, n * 2 - 1 + k)
                for u in range(DC):
                    act.wait_ge(q_ps, n * QK + DC * k + u + 1)
                    dst = full[:, k, u, :]
                    if bias is None:
                        ins = act.mul(dst, psQ[u][:], scale)
                    else:
                        ins = act.activation(dst, psQ[u][:], ACT.Identity, bias=bias[:, u:u + 1], scale=scale)
                    ins.then_inc(q_free, 1)
                act.wait_ge(q_free, n * QK + DC * (k + 1) + 2)
                act.wait_ge(qk_out[par], (n - par) * (8 * QKD))
                for u in range(DC):
                    act.copy(parts[par][:, k, 0, u, :], full[:, k, u, :]).then_inc(full_ready, 1)

            def transposed(n, par):
                act.wait_ge(tr_ps, n + 1)
                act.wait_ge(yT_used, n)
                if stage != 1:
                    act.copy(yT[:].rearrange("p c s -> p (c s)"), psT[:]).then_inc(yT_ready, 1)
                else:
                    for u in range(DC):
                        act.activation(yT[:, u, :], psT[:, u * S:(u + 1) * S], ACT.Identity,
                                       bias=lnb[:, u:u + 1], scale=lng[:, u:u + 1]).then_inc(yT_ready, 1)

            def body(n, par):
                    if stage == 0:
                        project(n, par, 0, 1.0, bk)
                        transposed(n, par)
                        project(n, par, 1, 0.25, bq)
                    elif stage == 1:
                        transposed(n, par)
                        project(n, par, 0, 1.0, None)
                        project(n, par, 1, 0.25, None)
                    else:
                        act.wait_ge(y_ready, n + 1)
                        act.wait_ge(v_out[par], (n - par) * 8)
                        act.copy(xfs[par][:, :, 0, :], y[par][:]).then_inc(hi_ready, 1)
                        transposed(n, par)
                        act.wait_ge(logit_ready, n + 1)
                        act.activation(ex[:], ex[:], ACT.Exp).then_inc(exp_ready, 1)
                        act.wait_ge(gT_ps, n + 1)
                        act.wait_ge(yT_used, n)
                        act.copy(gT[:], psQ[0][0:E_N, :]).then_inc(gT_ready, 1)

            by_pairs(act, body)

        @block.tensor
        def _(pe):
            pe.wait_ge(const_in, 16 * n_consts)
            pe.wait_ge(set_done, n_set)
            pe.sem_inc(q_free, 2)
            pe.sem_inc(v_free, NV)
            per_T = DC if stage == 1 else 1

            def project(n, k, src, wt):
                for u in range(DC):
                    pe.wait_ge(q_free, n * QK + DC * k + u + 1)
                    for d in range(DC):
                        last = pe.matmul(psQ[u][:], wt[:, d, u * P:(u + 1) * P], src[:, d, :],
                                         start=d == 0, stop=d == DC - 1)
                    last.then_inc(q_ps, 1)

            def values(n, src):
                for t in range(TT):
                    pe.wait_ge(v_free, last_units(n) + t + 1)
                    for d in range(DC):
                        last = pe.matmul(psV[t][:, 0:D], src[:, d, t * P:(t + 1) * P], wv[:, d, :],
                                         start=d == 0, stop=d == DC - 1)
                    last.then_inc(v_ps, 1)
                return last

            def out_proj(n, par):
                pe.wait_ge(c_in[par], (n - par) * 8 + 16)
                for t in range(TT):
                    pe.wait_ge(v_free, projected(n) + t + 1)
                    for g in range(NG):
                        last = pe.matmul(psV[t][:, 0:D], cin[par][:, g, t * P:(t + 1) * P], wo[:, g, :],
                                         start=g == 0, stop=stage == 2 and g == NG - 1)
                    if stage == 1:
                        last = pe.matmul(psV[t][:, 0:D], ones[:], bo[:], start=False, stop=True)
                    last.then_inc(v_ps, 1)
                pe.drain().then_inc(c_used, 1)

            def transpose(n, par):
                pe.wait_ge(y_ready, n + 1)
                pe.wait_ge(yT_ready, n * per_T)
                for t in range(TT):
                    for d in range(DC):
                        last = pe.transpose(psT[:, d * S + t * P:d * S + (t + 1) * P],
                                            y[par][:, t, d * P:(d + 1) * P], ident[:])
                last.then_inc(tr_ps, 1)

            def body(n, par):
                more = not (isinstance(n, int) and n == B - 1)
                if stage == 0:
                    pe.wait_ge(c_in[par], (n - par) * 8 + 16)
                    project(n, 0, cin[par], wk)
                transpose(n, par)
                if stage == 0:
                    values(n, cin[par])
                    pe.drain().then_inc(c_used, 1)
                if stage == 1 and more:
                    out_proj(n + 1, 1 - par)
                pe.wait_ge(yT_ready, n * per_T + per_T)
                if stage == 0:
                    project(n, 1, yT, wq)
                elif stage == 1:
                    project(n, 0, yT, wk)
                    project(n, 1, yT, wq)
                    values(n, yT)
                else:
                    for t in range(TT):
                        pe.wait_ge(v_free, n * VU + TT + t + 1)
                        for d in range(DC):
                            last = pe.matmul(psV[t][:, 0:E_N], yT[:, d, t * P:(t + 1) * P], wg[:, d, :],
                                             start=d == 0, stop=d == DC - 1)
                        last.then_inc(v_ps, 1)
                    if more:
                        out_proj(n + 1, 1 - par)
                    pe.wait_ge(gates_ready, n + 1)
                    for t in range(TT):
                        last = pe.transpose(psQ[0][0:E_N, t * P:(t + 1) * P], gate[par][:, t, 0, :], ident[:])
                    last.then_inc(gT_ps, 1)
                    pe.wait_ge(gT_ready, n + 1)
                    for t in range(TT):
                        pe.wait_ge(v_free, last_units(n) + t + 1)
                        pe.matmul(psV[t][:, 0:D], gT[:, t * P:(t + 1) * P], b2[:], start=True, stop=True
                                  ).then_inc(v_ps, 1)
                pe.drain().then_inc(yT_used, 1)

            if stage > 0:
                out_proj(0, 0)
            by_pairs(pe, body, peel_last=True)


def half_of(x):
    return x // 2


def quarter_of(x):
    return x // 4


def phase_attention(nc, c, causal, scr):
    SLOTS = 8
    LA = 2
    U = GH * TT
    NP_BUF = 8
    K6 = [c.sb(f"K6_{s}", [K_EXP, GH, S], BF16) for s in range(SLOTS)]
    Q6 = [c.sb(f"Q6_{s}", [K_EXP, GH, S], BF16) for s in range(SLOTS)]
    V = [c.sb(f"V_{s}", [P, TT, GH * HP]) for s in range(SLOTS)]
    NM_BUF = 4
    nm = [c.sb(f"nm{s}", [P, TT, GH]) for s in range(NM_BUF)]
    nr = c.sb("nr", [P, TT, GH])
    nparts = c.sb("nparts", [P, TT, NPART * GH], BF16)
    nrow = [c.sb(f"nrow{s}", [NPART * GH, S], BF16) for s in range(2)]
    prob = [c.sb(f"prob{s}", [P, S]) for s in range(NP_BUF)]
    oT = [c.sb(f"oT{s}", [P, S]) for s in range(2)]
    on = [c.sb(f"on{s}", [P, S]) for s in range(2)]
    identb = c.sb("identb", [P, P], BF16)
    ident = c.sb("ident", [P, P])
    one = c.sb("one", [P, 1, 1])
    pick = c.sb("pick", [P, GH])
    rc = [c.sb(f"rc{s}", [P, TT * GH]) for s in range(2)]
    rcx = [c.sb(f"rcx{s}", [P, TT * GH * HP]) for s in range(2)]
    cmq = c.sb("cmq", [P, P], BF16)
    cmk = c.sb("cmk", [P, P], BF16)
    NS, NE = 2, 4
    psS = [c.ps(f"psS{k}", [P, S]) for k in range(NS)]
    psE = [c.ps(f"psE{k}", [P, S]) for k in range(NE)]
    psO = c.ps("psO", [P, S])
    psM = c.ps("psM", [P, S])
    psMb = psM[:, :].bitcast(BF16)

    set_done, rows_set = c.sem("set_done"), c.sem("rows_set")
    g_in = [c.sem(f"g_in{s}") for s in range(SLOTS)]
    s_ps, s_free = c.sem("s_ps"), c.sem("s_free")
    e_ps, p_ready, pv_done = c.sem("e_ps"), c.sem("p_ready"), c.sem("pv_done")
    nparts_ready, nT_ps, nrow_ready = c.sem("nparts_ready"), c.sem("nT_ps"), c.sem("nrow_ready")
    nrow_in = [c.sem(f"nrow_in{s}") for s in range(2)]
    oT_ready, den_ps, on_ready, rc_ready = c.sem("oT_ready"), c.sem("den_ps"), c.sem("on_ready"), c.sem("rc_ready")
    one_set = c.sem("one_set")
    spread_ps, rcx_ready = c.sem("spread_ps"), c.sem("rcx_ready")
    o_out = [c.sem(f"o_out{s}") for s in range(2)]
    dve_own = c.sem("dve_own")
    N_LOAD = 3 if causal else 4

    def steps(eng, first, step):
        step(0, 0)
        with eng.Fori(0, 3) as i:
            for s in range(1, SLOTS + 1):
                step(i * SLOTS + s, s % SLOTS)
        for G in range(3 * SLOTS + 1, G_ALL):
            step(G, G % SLOTS)

    def last_of(G, k):
        return isinstance(G, int) and G + k >= G_ALL

    n_set = 10 if causal else 6

    with nc.Block() as block:

        @block.gpsimd
        def _(pool):
            pool.memset(identb[:], 0.0).then_inc(set_done, 1)
            pool.memset(ident[:], 0.0).then_inc(set_done, 1)
            pool.memset(pick[:], 0.0).then_inc(set_done, 1)
            pool.wait_ge(set_done, 3)
            pool.affine_select(out=ident[:], in_=ident[:], compare_op=ALU.not_equal, fill=1.0, base=0,
                               pattern=[[-1, P]], channel_multiplier=1).then_inc(set_done, 1)
            pool.affine_select(out=identb[:], in_=identb[:], compare_op=ALU.not_equal, fill=1.0, base=0,
                               pattern=[[-1, P]], channel_multiplier=1).then_inc(set_done, 1)
            pool.affine_select(out=pick[:], in_=pick[:], compare_op=ALU.not_equal, fill=1.0, base=-HD,
                               pattern=[[-HP, GH]], channel_multiplier=1).then_inc(set_done, 1)
            if causal:
                pool.memset(cmq[:], 0.0).then_inc(set_done, 1)
                pool.memset(cmk[:], 0.0).then_inc(set_done, 1)
                pool.wait_ge(set_done, 8)
                pool.affine_select(out=cmq[:], in_=cmq[:], compare_op=ALU.is_ge, fill=NEG, base=0,
                                   pattern=[[-1, P]], channel_multiplier=1).then_inc(set_done, 1)
                pool.affine_select(out=cmk[:], in_=cmk[:], compare_op=ALU.is_ge, fill=NEG, base=0,
                                   pattern=[[1, P]], channel_multiplier=-1).then_inc(set_done, 1)

            pool.memset(one[:], 1.0).then_inc(one_set, 1)
            pool.wait_ge(one_set, 1)
            with pool.Fori(0, G_ALL // 2) as i:
                for s in range(2):
                    pool.wait_ge(rc_ready, i * 2 + (s + 1))
                    pool.tensor_tensor(rcx[s][:].rearrange("p (h m) -> p h m", m=HP),
                                       rc[s][:].unsqueeze(2).to_broadcast([P, TT * GH, HP]),
                                       one[:].to_broadcast([P, TT * GH, HP]), ALU.mult).then_inc(rcx_ready, 1)

        @block.sync
        def _(sp):
            def load(G, s):
                if not (isinstance(G, int) and G < SLOTS):
                    sp.wait_ge(oT_ready, G - SLOTS + 1)
                g = s % NG
                blk, half = g // 2, g % 2
                row = (G - g) // 2 + blk if isinstance(G, int) else half_of(G - g) + blk
                for k, tile in ((0, K6[s]), (1, Q6[s])):
                    src = scr["qk"][ds(row, 1), k].rearrange("o t (d e h) n -> (o t d) e (h n)", d=HD, e=2)
                    sp.dma_start(tile[0:KM].rearrange("p h n -> p (h n)"), src[:, half, :]).then_inc(g_in[s], 16)
                b = (G - g) // NG if isinstance(G, int) else quarter_of(G - g)
                sp.dma_start(V[s][:], scr["v"][ds(b, 1), :, g * GH * HP:(g + 1) * GH * HP]
                             .rearrange("o (t p) c -> p (o t) c", p=P)).then_inc(g_in[s], 16)
                if not causal:
                    sp.dma_start(K6[s][KM:KM + 1, :, :],
                                 scr["mask"][ds(b, 1), :].unsqueeze(1).to_broadcast([1, GH, S])
                                 ).then_inc(g_in[s], 16)

            sp.wait_ge(rows_set, 1)
            for G in range(SLOTS):
                load(G, G)

            def maxima(G, s):
                sp.wait_ge(nrow_ready, G + 1)
                for r in range(NPART):
                    sp.dma_start(Q6[s][KM + 1 + r:KM + 2 + r, :, :],
                                 nrow[s % 2][r * GH:(r + 1) * GH, :]).then_inc(nrow_in[s % 2], 16)

            def result(G, s):
                sp.wait_ge(on_ready, 2 + G + 1)
                sp.dma_start(scr["o"][ds(G, 1)].rearrange("o p s -> p (o s)"), on[s % 2][:]
                             ).then_inc(o_out[s % 2], 16)

            maxima(0, 0)

            def step(G, s):
                if not last_of(G, 1):
                    maxima(G + 1, (s + 1) % SLOTS)
                if isinstance(G, int) and G == 0:
                    return
                result(G - 1, (s - 1) % SLOTS)
                if not last_of(G, SLOTS - 1):
                    load(G + SLOTS - 1, (s - 1) % SLOTS)

            steps(sp, 0, step)
            result(G_ALL - 1, (G_ALL - 1) % SLOTS)
            for k in range(2):
                sp.wait_ge(o_out[k], 16 * (G_ALL // 2))

        @block.tensor
        def _(pe):
            pe.wait_ge(set_done, n_set)
            pe.wait_ge(rows_set, 1)
            pe.sem_inc(s_free, NS)
            pe.sem_inc(on_ready, 2)

            def score(G, s, j):
                h, t = j // TT, j % TT
                bank = psS[j % NS]
                n = (t + 1) * P if causal else S
                pe.wait_ge(s_free, G * U + j + 1)
                last = pe.matmul(bank[:, 0:n], Q6[s][0:K_MAX, h, t * P:(t + 1) * P], K6[s][0:K_MAX, h, 0:n],
                                 start=True, stop=not causal)
                if causal:
                    last = pe.matmul(bank[:, t * P:n], identb[:], cmq[:], start=False, stop=True)
                last.then_inc(s_ps, 1)

            def shifted(G, s, j):
                t, h = j // GH, j % GH
                bank = psE[j % NE]
                q0 = t * P if causal else 0
                if not (isinstance(G, int) and G == 0 and j < NE):
                    pe.wait_ge(p_ready, G * U + j + 1 - NE)
                last = pe.matmul(bank[:, 0:S - q0], K6[s][0:K_EXP, h, t * P:(t + 1) * P], Q6[s][0:K_EXP, h, q0:S],
                                 start=True, stop=not causal)
                if causal:
                    last = pe.matmul(bank[:, 0:P], identb[:], cmk[:], start=False, stop=True)
                last.then_inc(e_ps, 1)

            def weigh(G, s, j):
                t, h = j // GH, j % GH
                q0 = t * P if causal else 0
                if j == 0:
                    pe.wait_ge(oT_ready, G)
                pe.wait_ge(p_ready, G * U + j + 1)
                pe.matmul(psO[h * HP:(h + 1) * HP, q0:S], V[s][:, t, h * HP:(h + 1) * HP],
                          prob[j % NP_BUF][:, 0:S - q0], start=t == 0, stop=t == TT - 1).then_inc(pv_done, 1)

            def maxima(G, s):
                pe.wait_ge(nparts_ready, G + 1)
                pe.wait_ge(on_ready, G)
                for t in range(TT):
                    last = pe.transpose(psMb[0:NPART * GH, t * P:(t + 1) * P], nparts[:, t, :], identb[:])
                last.then_inc(nT_ps, 1)

            def denominators(G, s):
                pe.wait_ge(oT_ready, G + 1)
                pe.wait_ge(nrow_ready, G + 3 if not last_of(G, 2) else G_ALL)
                if isinstance(G, int) and G > G_ALL - 3:
                    pe.wait_ge(on_ready, 2 + G)
                for t in range(TT):
                    last = pe.matmul(psM[:, t * GH:(t + 1) * GH], oT[s % 2][:, t * P:(t + 1) * P], pick[:],
                                     start=True, stop=True)
                last.then_inc(den_ps, 1)

            def spread(G, s):
                pe.wait_ge(rcx_ready, G + 1)
                for t in range(TT):
                    last = pe.matmul(psM[:, t * P:(t + 1) * P],
                                     rcx[s % 2][:, t * P:(t + 1) * P], ident[:],
                                     start=True, stop=True)
                last.then_inc(spread_ps, 1)

            for G in range(LA):
                pe.wait_ge(g_in[G], 16 * N_LOAD)
                for j in range(U):
                    score(G, G, j)
                    if G == 1 and j == 5:
                        maxima(0, 0)

            def step(G, s):
                if isinstance(G, int) and G == 0:
                    first = True
                else:
                    first = False
                pe.wait_ge(nrow_in[s % 2], (G - s % 2) * 24 + 48)
                more = not last_of(G, LA)
                s2 = (s + LA) % SLOTS
                if more:
                    pe.wait_ge(g_in[s2], loads_of(G + LA, s2))
                for j in range(U):
                    if more:
                        score(G + LA, s2, j)
                    shifted(G, s, j)
                    if j >= 2:
                        weigh(G, s, j - 2)
                    elif not first:
                        weigh(G - 1, (s - 1) % SLOTS, U - 2 + j)
                    if j == 2 and not last_of(G, 1):
                        maxima(G + 1, (s + 1) % SLOTS)
                    if j == 8 and not first:
                        denominators(G - 1, (s - 1) % SLOTS)
                    if j == 12 and not first:
                        spread(G - 1, (s - 1) % SLOTS)

            def loads_of(G, s):
                return (G - s) * (16 * N_LOAD // SLOTS) + 16 * N_LOAD

            steps(pe, 0, step)
            G, s = G_ALL - 1, (G_ALL - 1) % SLOTS
            weigh(G, s, U - 2)
            weigh(G, s, U - 1)
            denominators(G, s)
            spread(G, s)

        @block.scalar
        def _(act):
            def evacuate(G, s):
                act.wait_ge(pv_done, G * U + U)
                act.wait_ge(on_ready, G + 1)
                act.copy(oT[s % 2][:], psO[:]).then_inc(oT_ready, 1)

            def step(G, s):
                for j in range(U):
                    t = j // GH
                    n = S - t * P if causal else S
                    act.wait_ge(e_ps, G * U + j + 1)
                    if not (isinstance(G, int) and G == 0 and j < NP_BUF):
                        act.wait_ge(pv_done, G * U + j + 1 - NP_BUF)
                    act.activation(prob[j % NP_BUF][:, 0:n], psE[j % NE][:, 0:n], ACT.Exp).then_inc(p_ready, 1)
                    if j == 1 and not (isinstance(G, int) and G == 0):
                        evacuate(G - 1, (s - 1) % SLOTS)

            steps(act, 0, step)
            evacuate(G_ALL - 1, (G_ALL - 1) % SLOTS)

        @block.vector
        def _(dve):
            link = Chain(dve, dve_own)
            for s in range(SLOTS):
                dve.memset(K6[s][KM:K_EXP, :, :], 1.0)
                last = dve.memset(Q6[s][KM:K_EXP, :, :], 1.0)
            if causal:
                link(last)
                for s in range(SLOTS):
                    last = dve.memset(K6[s][KM:KM + 1, :, :], 0.0)
            last.then_inc(rows_set, 1)

            def top(G, s, j):
                h, t = j // TT, j % TT
                n = (t + 1) * P if causal else S
                dve.wait_ge(s_ps, G * U + j + 1)
                dve.tensor_reduce(nm[s % NM_BUF][:, t, h:h + 1], psS[j % NS][:, 0:n], axis=AX.X,
                                  op=ALU.max, negate=True).then_inc(s_free, 1)

            def shift_parts(G, s):
                m = nm[s % NM_BUF]
                np_ = nparts[:].rearrange("p t (r h) -> p r t h", r=NPART)
                dve.wait_ge(s_free, G * U + U + NS)
                dve.wait_ge(nT_ps, G)
                link(dve.tensor_copy(np_[:, 0], m[:]))
                link(dve.tensor_tensor(nr[:], m[:], np_[:, 0], ALU.subtract))
                link(dve.tensor_copy(np_[:, 1], nr[:]))
                dve.tensor_tensor(np_[:, 2], nr[:], np_[:, 1], ALU.subtract).then_inc(nparts_ready, 1)

            def shift_rows(G, s):
                dve.wait_ge(nT_ps, G + 1)
                if not (isinstance(G, int) and G < 2):
                    dve.wait_ge(nrow_in[s % 2], (G - s % 2) * 24)
                dve.tensor_copy(nrow[s % 2][:], psMb[0:NPART * GH, 0:S]).then_inc(nrow_ready, 1)

            def invert(G, s):
                dve.wait_ge(den_ps, G + 1)
                dve.reciprocal(rc[s % 2][:], psM[:, 0:TT * GH]).then_inc(rc_ready, 1)

            def scale(G, s):
                dve.wait_ge(spread_ps, G + 1)
                if not (isinstance(G, int) and G < 2):
                    dve.wait_ge(o_out[s % 2], (G - s % 2) * 8)
                dve.tensor_tensor(on[s % 2][:], oT[s % 2][:], psM[:], ALU.mult).then_inc(on_ready, 1)

            for G in range(LA):
                for j in range(U):
                    top(G, G, j)
                    if G == 1 and j == 2:
                        shift_parts(0, 0)
                    if G == 1 and j == 8:
                        shift_rows(0, 0)

            def step(G, s):
                if not last_of(G, 1):
                    shift_parts(G + 1, (s + 1) % SLOTS)
                for j in range(U):
                    if not last_of(G, LA):
                        top(G + LA, (s + LA) % SLOTS, j)
                    if j == 5 and not last_of(G, 1):
                        shift_rows(G + 1, (s + 1) % SLOTS)
                    if j == 9 and not (isinstance(G, int) and G == 0):
                        invert(G - 1, (s - 1) % SLOTS)
                    if j == 14 and not (isinstance(G, int) and G == 0):
                        scale(G - 1, (s - 1) % SLOTS)
                link.reset()

            link.reset()
            steps(dve, 0, step)
            invert(G_ALL - 1, (G_ALL - 1) % SLOTS)
            scale(G_ALL - 1, (G_ALL - 1) % SLOTS)


def phase_experts(nc, c, scr):
    w1h = c.sb("w1h", [P, E_N, 2, DC, FF], F16)
    w2h = c.sb("w2h", [P, E_N, 2, FC, D], F16)
    stage = [c.sb(f"stage{p}", [P, DC * FF]) for p in range(2)]
    gr = c.sb("gr", [P, NT, 2, E_N])
    xr = [c.sb(f"xr{p}", [P, TT, 2 * D], F16) for p in range(2)]
    zero = xr[0]
    seld = c.sb("seld", [P, NT * E_N], BF16)
    first = c.sb("first", [P, NT, E_N])
    second = c.sb("second", [P, NT, E_N])
    scan = [c.sb(f"scan{k}", [P, NT, E_N]) for k in range(2)]
    pos = c.sb("pos", [P, NT, E_N])
    tri, ones = c.sb("tri", [P, P], BF16), c.sb("ones", [P, P], BF16)
    NM = B * S // TE
    grid_i, grid = c.sb("grid_i", [P, NM], I32), c.sb("grid", [P, NM])
    tile_i, tile_f = c.sb("tile_i", [P, TILES], I32), c.sb("tile_f", [P, TILES])
    cmp = c.sb("cmp", [P, E_N, NM])
    cmp2 = c.sb("cmp2", [P, TILES, E_N])
    ends = [c.sb(f"ends{k}", [P, E_N]) for k in range(2)]
    count = c.sb("count", [P, E_N])
    start = c.sb("start", [P, E_N])
    ntile = c.sb("ntile", [P, E_N])
    emap_f, emap = c.sb("emap_f", [P, TILES]), c.sb("emap", [P, TILES], I32)
    slot_f, slot = c.sb("slot_f", [P, CHOSEN, NT]), c.sb("slot", [P, CHOSEN, NT], U32)
    gsel = c.sb("gsel", [P, CHOSEN, NT])
    identh = c.sb("identh", [P, P], F16)
    xt = [c.sb(f"xt{p}", [P, 2, 2 * D], F16) for p in range(2)]
    xT = [c.sb(f"xT{p}", [P, 2 * DC, TE], F16) for p in range(2)]
    b1 = [c.sb(f"b1_{p}", [P, FC]) for p in range(2)]
    hf = c.sb("hf", [P, FC, TE])
    hl = [c.sb(f"hl{p}", [P, 2, FC, TE], F16) for p in range(2)]
    yo = [c.sb(f"yo{p}", [P, 2, D]) for p in range(2)]
    psX = [c.ps(f"psX{p}", [P, 2 * DC * TE], F16) for p in range(2)]
    psH = [c.ps(f"psH{k}", [P, 2, TE]) for k in range(4)]
    psY = [c.ps(f"psY{k}", [P, 512]) for k in range(2)]
    FP = FC // 2
    PRODUCTS = ((0, 0), (0, 1), (1, 0))

    (gr_in, set_done, sel_ready, cum_ps, slot_ready, slot_out, xs_zero, xs_out, hi_done, w_ready, own, own_act,
     x_ps, x_ready, h_ps, h_free, hl_ready, y_ps, y_free, grid_set) = (
        c.sem(n) for n in ("gr_in", "set_done", "sel_ready", "cum_ps", "slot_ready", "slot_out", "xs_zero", "xs_out",
                           "hi_done", "w_ready", "own", "own_act", "x_ps", "x_ready", "h_ps", "h_free", "hl_ready",
                           "y_ps", "y_free", "grid_set"))
    w_in, xr_in, xt_in, y_out = ([c.sem(f"{n}{p}") for p in range(2)] for n in ("w_in", "xr_in", "xt_in", "y_out"))

    def tiles(eng, body):
        for s in range(2):
            body(s, s)
        with eng.Fori(1, TILES // 2) as i:
            for q in range(2):
                body(i * 2 + q, q)
        if TILES % 2:
            body(TILES - 1, 0)

    with nc.Block() as block:

        @block.sync
        def _(sp):
            sp.dma_start(gr[:].rearrange("p n r e -> p (n r e)").rearrange("p (b c) -> p b c", b=B),
                         scr["gates"].rearrange("b p t r e -> p b (t r e)")).then_inc(gr_in, 16)
            for e in range(E_N):
                for k in range(2):
                    if e > 0:
                        sp.wait_ge(w_ready, 2 * e + k - 1)
                    src = scr["w1"][e].rearrange("(c p) f -> p c f", p=P) if k == 0 else (
                        scr["w2"][e].rearrange("(c p) d -> p c d", p=P))
                    sp.dma_start(stage[k][:].rearrange("p (c f) -> p c f", c=DC if k == 0 else FC), src
                                 ).then_inc(w_in[k], 16)
            sp.wait_ge(slot_ready, 2)
            sp.dma_start(scr["slots"], slot[:]).then_inc(slot_out, 16)
            sp.dma_start(scr["gsel"], gsel[:]).then_inc(slot_out, 16)
            sp.wait_ge(xs_out, 16 * CHOSEN * NT)

            def load(s, q):
                e = sp.value_load(emap[0:1, ds(s, 1)], min_val=0, max_val=E_N - 1)
                if not (isinstance(s, int) and s < 2):
                    sp.wait_ge(x_ps, s - 1)
                    sp.wait_ge(h_free, (s - 1) * FC + 8)
                sp.dma_start(b1[q][:], scr["b1"][ds(e, 1)].rearrange("o p f -> p (o f)")).then_inc(xt_in[q], 16)
                sp.dma_start(xt[q][:], scr["xs"][ds(s * TE, TE)].rearrange("(h p) c -> p h c", p=P)
                             ).then_inc(xt_in[q], 16)

            def store(s, q):
                sp.wait_ge(y_free, s + 2)
                sp.dma_start(scr["ys"][ds(s * TE, TE)].rearrange("(h p) d -> p h d", p=P), yo[q][:]
                             ).then_inc(y_out[q], 16)

            def body(s, q):
                load(s, q)
                if not (isinstance(s, int) and s < 2):
                    store(s - 2, q)

            tiles(sp, body)
            store(TILES - 2, TILES % 2)
            store(TILES - 1, 1 - TILES % 2)
            sp.wait_ge(slot_out, 32)
            for q in range(2):
                sp.wait_ge(y_out[q], 16 * ((TILES + 1 - q) // 2))

        @block.gpsimd
        def _(pool):
            pool.memset(zero[:], 0.0).then_inc(grid_set, 1)
            pool.wait_ge(grid_set, 1)
            rows = TT * P
            for k in range(0, TILES * TE, rows):
                n = min(rows, TILES * TE - k)
                pool.dma_start(scr["xs"][k:k + n].rearrange("(t p) c -> p t c", p=P), zero[:, 0:n // P, :]
                               ).then_inc(xs_zero, 16)
            pool.memset(tri[:], 1.0).then_inc(set_done, 1)
            pool.memset(ones[:], 1.0).then_inc(set_done, 1)
            pool.memset(identh[:], 0.0).then_inc(set_done, 1)
            pool.iota(grid_i[:], pattern=[[TE, NM]], base=0, channel_multiplier=0).then_inc(set_done, 1)
            pool.iota(tile_i[:], pattern=[[1, TILES]], base=0, channel_multiplier=0).then_inc(set_done, 1)
            pool.wait_ge(set_done, 5)
            pool.affine_select(out=tri[:], in_=tri[:], compare_op=ALU.is_gt, fill=0.0, base=0,
                               pattern=[[1, P]], channel_multiplier=-1).then_inc(set_done, 1)
            pool.affine_select(out=identh[:], in_=identh[:], compare_op=ALU.not_equal, fill=1.0, base=0,
                               pattern=[[-1, P]], channel_multiplier=1).then_inc(set_done, 1)
            pool.tensor_copy(grid[:], grid_i[:]).then_inc(set_done, 1)
            pool.tensor_copy(tile_f[:], tile_i[:]).then_inc(set_done, 1)
            pool.wait_ge(xs_zero, 16 * len(range(0, TILES * TE, rows)))

            def rows_in(b):
                if b >= 2:
                    pool.wait_ge(xs_out, 16 * CHOSEN * TT * (b - 1))
                pool.dma_start(xr[b % 2][:], scr["xfs"][b].rearrange("(t p) c -> p t c", p=P)).then_inc(xr_in[b % 2], 16)

            rows_in(0)
            pool.wait_ge(slot_ready, 1)
            for b in range(B):
                if b + 1 < B:
                    rows_in(b + 1)
                pool.wait_ge(xr_in[b % 2], 16 * (b // 2 + 1))
                for t in range(TT):
                    for k in range(CHOSEN):
                        at = b * TT + t
                        pool.indirect_dma_start(scr["xs"], bass.IndirectOffsetOnAxis(slot[:, k, at:at + 1], 0),
                                                xr[b % 2][:, t, :], None).then_inc(xs_out, 16)

        @block.vector
        def _(dve):
            link = Chain(dve, own)
            dve.wait_ge(gr_in, 16)
            dve.wait_ge(set_done, 9)
            rank, gate = gr[:, :, 1, :], gr[:, :, 0, :]
            dve.tensor_scalar(seld[:].rearrange("p (n e) -> p n e", e=E_N), rank, CHOSEN - 0.5, None, ALU.is_lt
                              ).then_inc(sel_ready, 1)
            dve.tensor_scalar(first[:], rank, 0.5, None, ALU.is_lt)
            link(dve.tensor_scalar(second[:], rank, 1.0, None, ALU.is_equal))
            dve.wait_ge(cum_ps, 1)
            a = 0
            link(dve.tensor_copy(scan[0][:].rearrange("p n e -> p (n e)"), psY[1][:, 0:NT * E_N]))
            step = 1
            while step < NT:
                dve.tensor_copy(scan[1 - a][:, 0:step, :], scan[a][:, 0:step, :])
                link(dve.tensor_tensor(scan[1 - a][:, step:, :], scan[a][:, step:, :], scan[a][:, 0:NT - step, :], ALU.add))
                a, step = 1 - a, step * 2
            link(dve.tensor_copy(count[:], scan[a][:, NT - 1, :]))
            link(dve.tensor_tensor(pos[:].rearrange("p n e -> p (n e)"), scan[a][:].rearrange("p n e -> p (n e)"),
                                   psY[1][:, 0:NT * E_N], ALU.subtract))
            link(dve.tensor_tensor(pos[:].rearrange("p n e -> p (n e)"), pos[:].rearrange("p n e -> p (n e)"),
                                   psY[0][:, 0:NT * E_N], ALU.add))
            link(dve.tensor_tensor(cmp[:], count[:].unsqueeze(2).to_broadcast([P, E_N, NM]),
                                   grid[:].unsqueeze(1).to_broadcast([P, E_N, NM]), ALU.is_gt))
            link(dve.tensor_reduce(ntile[:], cmp[:], axis=AX.X, op=ALU.add))
            link(dve.tensor_copy(ends[0][:], ntile[:]))
            z, step = 0, 1
            while step < E_N:
                dve.tensor_copy(ends[1 - z][:, 0:step], ends[z][:, 0:step])
                link(dve.tensor_tensor(ends[1 - z][:, step:], ends[z][:, step:], ends[z][:, 0:E_N - step], ALU.add))
                z, step = 1 - z, step * 2
            link(dve.tensor_tensor(start[:], ends[z][:], ntile[:], ALU.subtract))
            link(dve.tensor_scalar(start[:], start[:], float(TE), None, ALU.mult))
            link(dve.tensor_tensor(pos[:], pos[:], start[:].unsqueeze(1).to_broadcast([P, NT, E_N]), ALU.add))
            for k, chosen in enumerate((first, second)):
                link(dve.tensor_tensor(scan[k][:], pos[:], chosen[:], ALU.mult))
                link(dve.tensor_reduce(slot_f[:, k, :], scan[k][:], axis=AX.X, op=ALU.add))
                link(dve.tensor_tensor(scan[k][:], gate, chosen[:], ALU.mult))
                link(dve.tensor_reduce(gsel[:, k, :], scan[k][:], axis=AX.X, op=ALU.add))
            dve.tensor_copy(slot[:], slot_f[:]).then_inc(slot_ready, 1)
            link(dve.tensor_tensor(cmp2[:], tile_f[:].unsqueeze(2).to_broadcast([P, TILES, E_N]),
                                   ends[z][:].unsqueeze(1).to_broadcast([P, TILES, E_N]), ALU.is_ge))
            link(dve.tensor_reduce(emap_f[:], cmp2[:], axis=AX.X, op=ALU.add))
            dve.tensor_scalar(emap[:], emap_f[:], float(E_N - 1), None, ALU.min).then_inc(slot_ready, 1)

            for e in range(E_N):
                for k, wh in enumerate((w1h, w2h)):
                    dve.wait_ge(hi_done, 2 * e + k + 1)
                    src = stage[k][:]
                    flat = wh[:, e].rearrange("p r c f -> p r (c f)")
                    dve.scalar_tensor_tensor(out=flat[:, 1, :], in0=src, scalar=WSCALE, in1=flat[:, 0, :],
                                             op0=ALU.mult, op1=ALU.subtract).then_inc(w_ready, 1)
            link.reset()

            def out_tile(s, q):
                dve.wait_ge(y_ps, s + 1)
                if not (isinstance(s, int) and s < 2):
                    dve.wait_ge(y_out[q], (s - q) * 8)
                dve.tensor_scalar(yo[q][:, 0, :], psY[0][:, 0:D], 1.0 / WSCALE, None, ALU.mult)
                dve.tensor_scalar(yo[q][:, 1, :], psY[1][:, 0:D], 1.0 / WSCALE, None, ALU.mult)
                dve.drain().then_inc(y_free, 1)

            dve.sem_inc(y_free, 1)

            def body(s, q):
                if not (isinstance(s, int) and s < 2):
                    dve.wait_ge(y_ps, s - 1)
                for f in range(FP):
                    two = slice(2 * f, 2 * f + 2)
                    dve.wait_ge(h_free, s * FC + 2 * f + 2 + 8)
                    link(dve.tensor_copy(hl[q][:, 0, two, :], hf[:, two, :]))
                    dve.tensor_tensor(hl[q][:, 1, two, :], hf[:, two, :], hl[q][:, 0, two, :], ALU.subtract
                                      ).then_inc(hl_ready, 1)
                    if f == 1 and not (isinstance(s, int) and s == 0):
                        out_tile(s - 1, 1 - q)
                link.reset()

            tiles(dve, body)
            out_tile(TILES - 1, 1 - TILES % 2)

        @block.scalar
        def _(act):
            for e in range(E_N):
                for k, wh in enumerate((w1h, w2h)):
                    act.wait_ge(w_in[k], 16 * (e + 1))
                    act.mul(wh[:, e, 0].rearrange("p c f -> p (c f)"), stage[k][:], WSCALE).then_inc(hi_done, 1)
            act.sem_inc(h_free, 8)

            def transposed(s, q):
                act.wait_ge(x_ps, s + 1)
                if not (isinstance(s, int) and s < 2):
                    act.wait_ge(h_ps, (s - 1) * FP)
                act.copy(xT[q][:].rearrange("p c t -> p (c t)"), psX[q][:]).then_inc(x_ready, 1)

            transposed(0, 0)

            def body(s, q):
                for f in range(FC):
                    act.wait_ge(h_ps, s * FP + f // 2 + 1)
                    if not (isinstance(s, int) and s == 0) and f % 2 == 0:
                        act.wait_ge(hl_ready, (s - 1) * FP + f // 2 + 1)
                    act.activation(hf[:, f, :], psH[f // 2][:, f % 2, :], ACT.Gelu_apprx_tanh, bias=b1[q][:, f:f + 1],
                                   scale=1.0 / WSCALE).then_inc(h_free, 1)
                    if f == 3 and not (isinstance(s, int) and s == TILES - 1):
                        transposed(s + 1, 1 - q)

            tiles(act, body)

        @block.tensor
        def _(pe):
            pe.wait_ge(set_done, 9)
            pe.wait_ge(sel_ready, 1)
            pe.matmul(psY[0][:, 0:NT * E_N], tri[:], seld[:], start=True, stop=True)
            pe.matmul(psY[1][:, 0:NT * E_N], ones[:], seld[:], start=True, stop=True).then_inc(cum_ps, 1)

            def transpose(s, q):
                pe.wait_ge(xt_in[q], (s - q) * 16 + 32)
                if not (isinstance(s, int) and s < 2):
                    pe.wait_ge(x_ready, s - 1)
                for ch in range(2 * DC):
                    for h in range(2):
                        last = pe.transpose(psX[q][:, ch * TE + h * P:ch * TE + (h + 1) * P],
                                            xt[q][:, h, ch * P:(ch + 1) * P], identh[:])
                last.then_inc(x_ps, 1)

            def hidden(s, q, e, f):
                pe.wait_ge(h_free, s * FC + 2 * f + 2)
                for j in range(2):
                    fc = 2 * f + j
                    n = 0
                    for wp, xp in PRODUCTS:
                        for d in range(DC):
                            last = pe.matmul(psH[f][:, j, :],
                                             w1h[:, ds(e, 1), wp, d, fc * P:(fc + 1) * P].rearrange("p o f -> p (o f)"),
                                             xT[q][:, xp * DC + d, :], start=n == 0, stop=n == len(PRODUCTS) * DC - 1)
                            n += 1
                last.then_inc(h_ps, 1)

            def output(s, q, e, f):
                pe.wait_ge(hl_ready, s * FP + f + 1)
                if f == 0:
                    pe.wait_ge(y_free, s + 1)
                for t in range(2):
                    for fc in (2 * f, 2 * f + 1):
                        for n, (wp, hp) in enumerate(PRODUCTS):
                            last = pe.matmul(psY[t][:, 0:D], hl[q][:, hp, fc, t * P:(t + 1) * P],
                                             w2h[:, ds(e, 1), wp, fc, :].rearrange("p o d -> p (o d)"),
                                             start=fc == 0 and n == 0, stop=fc == FC - 1 and n == len(PRODUCTS) - 1)
                if f == FP - 1:
                    last.then_inc(y_ps, 1)

            pe.wait_ge(slot_ready, 2)
            pe.wait_ge(w_ready, 2 * E_N)
            transpose(0, 0)

            def expert_of(s):
                return pe.value_load(emap[0:1, ds(s, 1)], min_val=0, max_val=E_N - 1)

            def body(s, q):
                pe.wait_ge(x_ready, s + 1)
                e = expert_of(s)
                if not (isinstance(s, int) and s == 0):
                    before = expert_of(s - 1)
                for f in range(FP):
                    hidden(s, q, e, f)
                    if f < 2:
                        if not (isinstance(s, int) and s == 0):
                            output(s - 1, 1 - q, before, f + 2)
                    else:
                        output(s, q, e, f - 2)
                    if f == 1 and not (isinstance(s, int) and s == TILES - 1):
                        transpose(s + 1, 1 - q)

            tiles(pe, body)
            e = expert_of(TILES - 1)
            for f in (2, 3):
                output(TILES - 1, 1 - TILES % 2, e, f)


def phase_last(nc, c, w, scr):
    wi = [c.sb(f"wi{k}", [P, DC * F2], I32) for k in range(3)]
    wgate, wup = c.sb("wgate", [P, DC, F2]), c.sb("wup", [P, DC, F2])
    wdown = c.sb("wdown", [P, F2C, D])
    wq, wk, wv = (c.sb(n, [P, DC, D]) for n in ("wq", "wk", "wv"))
    bq, bk, bv = c.sb("bq", [P, DC]), c.sb("bk", [P, DC]), c.sb("bv", [P, D])
    ident = c.sb("ident", [P, P])
    xin = [c.sb(f"xin{p}", [P, TT, D]) for p in range(2)]
    cin = [c.sb(f"cin{p}", [P, DC, S]) for p in range(2)]
    xo = [c.sb(f"xo{p}", [P, TT, D]) for p in range(2)]
    x3 = c.sb("x3", [P, TT, D])
    slots = c.sb("slots", [P, CHOSEN, NT], U32)
    gsel = c.sb("gsel", [P, CHOSEN, NT])
    yg = [c.sb(f"yg{p}", [P, TT, CHOSEN, D]) for p in range(2)]
    y = c.sb("y", [P, TT, D])
    yT = c.sb("yT", [P, DC, S])
    kT, qT = c.sb("kT", [P, DC, S]), c.sb("qT", [P, DC, S])
    vv = c.sb("vv", [P, TT, D])
    pr = c.sb("pr", [P, TT, S])
    pT = c.sb("pT", [P, TT, S])
    sg = c.sb("sg", [P, 2, S])
    hT = c.sb("hT", [P, F2C, S])
    stats, mv, rstd = c.sb("stats", [P, TT, 6]), c.sb("mv", [P, TT, 2]), c.sb("rstd", [P, TT])
    nmax, tot, rec = c.sb("nmax", [P, TT]), c.sb("tot", [P, TT]), c.sb("rec", [P, TT])
    psT = c.ps("psT", [P, 2 * S])
    psG = [c.ps(f"psG{k}", [P, S]) for k in range(2)]
    psU = [c.ps(f"psU{k}", [P, S]) for k in range(2)]
    psB = [c.ps(f"psB{k}", [P, S]) for k in range(2)]
    (const_in, set_done, w_ready, x_used, c_used, y_ready, t_ps, t_free, g_ps, g_free, u_ps, u_free, s_free, max_ready,
     b_ps, b_free, sg_ready, h_ready, xo_ready, dve_own, act_own, sum_ready) = (
        c.sem(n) for n in ("const_in", "set_done", "w_ready", "x_used", "c_used", "y_ready", "t_ps", "t_free", "g_ps",
                           "g_free", "u_ps", "u_free", "s_free", "max_ready", "b_ps", "b_free", "sg_ready",
                           "h_ready", "xo_ready", "dve_own", "act_own", "sum_ready"))
    x_in, c_in, x_out = ([c.sem(f"{n}{p}") for p in range(2)] for n in ("x_in", "c_in", "x_out"))
    var_ready, rstd_ready = c.sem("var_ready"), c.sem("rstd_ready")
    c.half_power = (c.sb("power", [P, TT]), c.sb("var", [P, TT]), c.sb("eps", [P, TT]), c.sem("pool_own"))
    NORMS = 2
    GU = 2 * DC + F2C
    UU = TT + F2C
    BU = 3 * TT
    TU = TT + 2
    consts = [(wi[0][:], w["gate"]), (wi[1][:], w["up"]), (wi[2][:], w["down"]), (wq[:], w["wq"]), (wk[:], w["wk"]),
              (wv[:], w["wv"]), (bq[:], w["bq"]), (bk[:], w["bk"]), (bv[:], w["bv"]), (slots[:], scr["slots"]),
              (gsel[:], scr["gsel"])]
    yg_in, yg_used = [c.sem(f"yg_in{p}") for p in range(2)], c.sem("yg_used")

    with nc.Block() as block:

        @block.sync
        def _(sp):
            for dst, src in consts:
                sp.dma_start(dst, src).then_inc(const_in, 16)
            sp.sem_inc(x_used, 2)
            sp.sem_inc(c_used, 2)

            def load(n, par):
                sp.wait_ge(x_used, n + 1)
                sp.dma_start(xin[par][:], scr["x2"][ds(n, 1)].rearrange("o (t p) d -> p (o t) d", p=P)
                             ).then_inc(x_in[par], 16)
                sp.wait_ge(c_used, n + 1)
                sp.dma_start(cin[par][:], scr["ctxT"][ds(n, 1)].rearrange("o (c p) s -> p (o c) s", p=P)
                             ).then_inc(c_in[par], 16)

            load(0, 0)

            def body(n, par):
                if not (isinstance(n, int) and n == B - 1):
                    load(n + 1, 1 - par)
                sp.wait_ge(xo_ready, n + 1)
                sp.dma_start(scr["out"][ds(n, 1)].rearrange("o (t p) d -> p (o t) d", p=P), xo[par][:]
                             ).then_inc(x_out[par], 16)

            by_pairs(sp, body, peel_last=True)
            for par in range(2):
                sp.wait_ge(x_out[par], 16 * (B // 2))

        @block.gpsimd
        def _(pool):
            pool.memset(ident[:], 0.0).then_inc(set_done, 1)
            pool.wait_ge(set_done, 1)
            pool.affine_select(out=ident[:], in_=ident[:], compare_op=ALU.not_equal, fill=1.0, base=0,
                               pattern=[[-1, P]], channel_multiplier=1).then_inc(set_done, 1)
            power, var, eps, own = c.half_power
            pool.memset(power[:], -0.5).then_inc(own, 1)
            pool.memset(eps[:], EPS).then_inc(own, 1)
            pool.wait_ge(own, 2)
            pool.wait_ge(const_in, 16 * len(consts))

            def gather(n):
                if n >= 2:
                    pool.wait_ge(yg_used, n - 1)
                for t in range(TT):
                    for k in range(CHOSEN):
                        at = n * TT + t
                        pool.indirect_dma_start(yg[n % 2][:, t, k, :], None, scr["y"],
                                                bass.IndirectOffsetOnAxis(slots[:, k, at:at + 1], 0)
                                                ).then_inc(yg_in[n % 2], 16)

            gather(0)
            for n in range(B):
                if n + 1 < B:
                    gather(n + 1)
                for k in range(n * NORMS, (n + 1) * NORMS):
                    pool.wait_ge(var_ready, k + 1)
                    pool.tensor_tensor(var[:], mv[:, :, 1], eps[:], ALU.add).then_inc(own, 1)
                    pool.wait_ge(own, k + 3)
                    pool.tensor_tensor(rstd[:], var[:], power[:], ALU.pow).then_inc(rstd_ready, 1)

        @block.vector
        def _(dve):
            link = Chain(dve, dve_own)
            dve.wait_ge(const_in, 16 * len(consts))
            dve.tensor_copy(wgate[:].rearrange("p c f -> p (c f)"), wi[0][:])
            dve.tensor_copy(wup[:].rearrange("p c f -> p (c f)"), wi[1][:])
            dve.tensor_copy(wdown[:].rearrange("p c d -> p (c d)"), wi[2][:]).then_inc(w_ready, 1)

            norms = [0]

            def norm(n, src):
                for t in range(TT):
                    last = dve.bn_stats(stats[:, t, :], src[:, t, :])
                link(last)
                for t in range(TT):
                    last = dve.bn_aggr(mv[:, t, :], stats[:, t, :])
                last.then_inc(var_ready, 1)
                norms[0] += 1
                dve.wait_ge(rstd_ready, n * NORMS + norms[0])
                for t in range(TT):
                    last = dve.tensor_scalar(y[:, t, :], src[:, t, :], mv[:, t, 0:1], rstd[:, t:t + 1],
                                             ALU.subtract, ALU.mult)
                last.then_inc(y_ready, 1)

            def body(n, par):
                    dve.wait_ge(x_in[par], (n - par) * 8 + 16)
                    dve.wait_ge(yg_in[par], (n - par) * (8 * CHOSEN * TT) + 16 * CHOSEN * TT)
                    for k in range(CHOSEN):
                        for t in range(TT):
                            g = gsel[:, k:k + 1, ds(n * TT + t, 1)].rearrange("p k t -> p (k t)")
                            last = dve.scalar_tensor_tensor(out=xin[par][:, t, :], in0=yg[par][:, t, k, :], scalar=g,
                                                            in1=xin[par][:, t, :], op0=ALU.mult, op1=ALU.add)
                        link(last)
                    dve.sem_inc(yg_used, 1)
                    dve.wait_ge(t_ps, n * TU)
                    norm(n, xin[par])
                    for t in range(TT):
                        dve.wait_ge(b_ps, n * BU + t + 1)
                        dve.tensor_tensor(vv[:, t, :], psB[t % 2][:, 0:D], bv[:], ALU.add).then_inc(b_free, 1)
                    for t in range(TT):
                        dve.wait_ge(u_ps, n * UU + t + 1)
                        dve.tensor_reduce(nmax[:, t:t + 1], psU[t % 2][:], axis=AX.X, op=ALU.max, negate=True
                                          ).then_inc(max_ready, 1)
                    dve.wait_ge(sum_ready, n * TT + TT)
                    link(dve.reciprocal(rec[:], tot[:]))
                    link(dve.tensor_scalar(rec[:], rec[:], 1.0 / 16.0, None, ALU.mult))
                    for t in range(TT):
                        dve.wait_ge(b_ps, n * BU + TT + t + 1)
                        dve.scalar_tensor_tensor(out=x3[:, t, :], in0=psB[t % 2][:, 0:D], scalar=rec[:, t:t + 1],
                                                 in1=xin[par][:, t, :], op0=ALU.mult, op1=ALU.add).then_inc(b_free, 1)
                    dve.drain().then_inc(x_used, 1)
                    norm(n, x3)
                    for f in range(F2C):
                        dve.wait_ge(u_ps, n * UU + TT + f + 1)
                        dve.wait_ge(sg_ready, n * F2C + f + 1)
                        dve.scalar_tensor_tensor(out=hT[:, f, :], in0=psU[f % 2][:], scalar=SCALE2, in1=sg[:, f % 2, :],
                                                 op0=ALU.mult, op1=ALU.mult).then_inc(u_free, 1)
                    dve.wait_ge(x_out[par], (n - par) * 8)
                    for t in range(TT):
                        dve.wait_ge(b_ps, n * BU + 2 * TT + t + 1)
                        dve.scalar_tensor_tensor(out=xo[par][:, t, :], in0=psB[t % 2][:, 0:D], scalar=SCALE2,
                                                 in1=x3[:, t, :], op0=ALU.mult, op1=ALU.add).then_inc(b_free, 1)
                    dve.drain().then_inc(xo_ready, 1)
                    link.reset()
                    norms[0] = 0

            by_pairs(dve, body)

        @block.scalar
        def _(act):
            act.wait_ge(const_in, 16 * len(consts))

            def body(n, par):
                    for u in range(DC):
                        act.wait_ge(g_ps, n * GU + u + 1)
                        act.activation(kT[:, u, :], psG[u][:], ACT.Identity, bias=bk[:, u:u + 1]).then_inc(g_free, 1)
                    act.wait_ge(t_ps, n * TU + 1)
                    act.copy(yT[:].rearrange("p c s -> p (c s)"), psT[:]).then_inc(t_free, 1)
                    for u in range(DC):
                        act.wait_ge(g_ps, n * GU + DC + u + 1)
                        act.activation(qT[:, u, :], psG[u][:], ACT.Identity, bias=bq[:, u:u + 1]).then_inc(g_free, 1)
                    for t in range(TT):
                        act.wait_ge(max_ready, n * TT + t + 1)
                        act.activation(pr[:, t, :], psU[t % 2][:], ACT.Exp, bias=nmax[:, t:t + 1],
                                       accum_out=tot[:, t:t + 1]).then_inc(s_free, 1)
                    act.drain().then_inc(sum_ready, TT)
                    for t in range(TT):
                        act.wait_ge(t_ps, n * TU + 1 + t + 1)
                        act.copy(pT[:, :, t * P:(t + 1) * P], psT[:, (t % 2) * S:(t % 2 + 1) * S]
                                 .rearrange("p (k q) -> p k q", k=TT)).then_inc(t_free, 1)
                    act.wait_ge(t_ps, n * TU + TU)
                    act.copy(yT[:].rearrange("p c s -> p (c s)"), psT[:]).then_inc(t_free, 1)
                    for f in range(F2C):
                        act.wait_ge(g_ps, n * GU + 2 * DC + f + 1)
                        if f >= 2:
                            act.wait_ge(u_free, n * F2C + f - 1)
                        act.activation(sg[:, f % 2, :], psG[f % 2][:], ACT.Silu, scale=SCALE2).then_inc(g_free, 1)
                        act.drain().then_inc(sg_ready, 1)

            by_pairs(act, body)

        @block.tensor
        def _(pe):
            pe.wait_ge(const_in, 16 * len(consts))
            pe.wait_ge(w_ready, 1)
            pe.wait_ge(set_done, 2)
            pe.sem_inc(g_free, 2)
            pe.sem_inc(b_free, 2)

            def wide(n, j, bank, wt, u, src):
                for d in range(DC):
                    last = pe.matmul(bank[:], wt[:, d, u * P:(u + 1) * P], src[:, d, :], start=d == 0, stop=d == DC - 1)
                return last

            def body(n, par):
                    pe.wait_ge(c_in[par], (n - par) * 8 + 16)
                    for u in range(DC):
                        pe.wait_ge(g_free, n * GU + u + 1)
                        wide(n, u, psG[u], wk, u, cin[par]).then_inc(g_ps, 1)
                    for t in range(TT):
                        pe.wait_ge(b_free, n * BU + t + 1)
                        for d in range(DC):
                            last = pe.matmul(psB[t % 2][:, 0:D], cin[par][:, d, t * P:(t + 1) * P], wv[:, d, :],
                                             start=d == 0, stop=d == DC - 1)
                        last.then_inc(b_ps, 1)
                    pe.drain().then_inc(c_used, 1)

                    def transpose_y(k):
                        pe.wait_ge(y_ready, n * 2 + k + 1)
                        pe.wait_ge(t_free, n * TU + k * (TT + 1))
                        for t in range(TT):
                            for d in range(DC):
                                last = pe.transpose(psT[:, d * S + t * P:d * S + (t + 1) * P],
                                                    y[:, t, d * P:(d + 1) * P], ident[:])
                        last.then_inc(t_ps, 1)

                    transpose_y(0)
                    pe.wait_ge(t_free, n * TU + 1)
                    for u in range(DC):
                        pe.wait_ge(g_free, n * GU + DC + u + 1)
                        wide(n, u, psG[u], wq, u, yT).then_inc(g_ps, 1)
                    pe.wait_ge(g_free, n * GU + 2 * DC + 2)
                    for t in range(TT):
                        pe.wait_ge(s_free, n * TT + t - 1) if t >= 2 else pe.wait_ge(u_free, n * F2C)
                        for d in range(DC):
                            last = pe.matmul(psU[t % 2][:], qT[:, d, t * P:(t + 1) * P], kT[:, d, :],
                                             start=d == 0, stop=d == DC - 1)
                        last.then_inc(u_ps, 1)
                    for t in range(TT):
                        pe.wait_ge(s_free, n * TT + t + 1)
                        pe.wait_ge(t_free, n * TU + 1 + max(t - 1, 0))
                        for k in range(TT):
                            last = pe.transpose(psT[:, (t % 2) * S + k * P:(t % 2) * S + (k + 1) * P],
                                                pr[:, t, k * P:(k + 1) * P], ident[:])
                        last.then_inc(t_ps, 1)
                    for t in range(TT):
                        pe.wait_ge(t_free, n * TU + 1 + t + 1)
                        pe.wait_ge(b_free, n * BU + TT + t + 1)
                        for k in range(TT):
                            last = pe.matmul(psB[t % 2][:, 0:D], pT[:, k, t * P:(t + 1) * P], vv[:, k, :],
                                             start=k == 0, stop=k == TT - 1)
                        last.then_inc(b_ps, 1)
                    transpose_y(1)
                    pe.wait_ge(t_free, n * TU + TU)
                    for f in range(F2C):
                        pe.wait_ge(g_free, n * GU + 2 * DC + f + 1)
                        wide(n, f, psG[f % 2], wgate, f, yT).then_inc(g_ps, 1)
                        if f < 2:
                            pe.wait_ge(s_free, n * TT + TT)
                        else:
                            pe.wait_ge(u_free, n * F2C + f - 1)
                        wide(n, f, psU[f % 2], wup, f, yT).then_inc(u_ps, 1)
                    pe.wait_ge(u_free, n * F2C + F2C)
                    for t in range(TT):
                        pe.wait_ge(b_free, n * BU + 2 * TT + t + 1)
                        for f in range(F2C):
                            last = pe.matmul(psB[t % 2][:, 0:D], hT[:, f, t * P:(t + 1) * P], wdown[:, f, :],
                                             start=f == 0, stop=f == F2C - 1)
                        last.then_inc(b_ps, 1)

            by_pairs(pe, body)


def phase_mask(nc, c, mask, dst):
    m8, row = c.sb("m8", [B, S], U8), c.sb("row", [B, S], BF16)
    m_in, m_ready, m_out = c.sem("in"), c.sem("ready"), c.sem("out")
    with nc.Block() as block:

        @block.sync
        def _(sp):
            sp.dma_start(m8[:], mask).then_inc(m_in, 16)
            sp.wait_ge(m_ready, 1)
            sp.dma_start(dst, row[:]).then_inc(m_out, 16)
            sp.wait_ge(m_out, 16)

        @block.vector
        def _(dve):
            dve.wait_ge(m_in, 16)
            dve.tensor_scalar(row[:], m8[:], 1.0, -NEG, ALU.subtract, ALU.mult).then_inc(m_ready, 1)


def build(nc, a, out):
    def scratch(name, shape, dt=F32):
        return nc.dram_tensor(f"s_{name}", shape, dt).ap()

    qk0, qk1 = (scratch(f"qk{k}", [B * DC, 2, NTERM, P, S], BF16) for k in range(2))
    v0, v1 = (scratch(f"v{k}", [B, S, H * HP]) for k in range(2))
    o0, o1 = (scratch(f"o{k}", [G_ALL, P, S]) for k in range(2))
    mask = scratch("mask", [B, S], BF16)
    x1, y1, base = (scratch(n, [B, S, D]) for n in ("x1", "y1", "base"))
    xfs = scratch("xfs", [B, S, 2 * D], F16)
    gates = scratch("gates", [B, P, TT, 2, E_N])
    xs = scratch("xs", [TILES * TE, 2 * D], F16)
    ys = scratch("ys", [TILES * TE, D])
    slots = scratch("slots", [P, CHOSEN, NT], U32)
    gsel = scratch("gsel", [P, CHOSEN, NT])

    def chunks(ap):
        return ap.rearrange("(c p) n -> p c n", p=P)

    def phase(tag, run, *args):
        with ExitStack() as stack:
            c = Ctx(nc, tag, stack)
            run(nc, c, *args)
            for sem in c.sems:
                nc.sync.sem_clear(sem)
            nc.all_engine_barrier()

    phase("mask", phase_mask, a["mask"], mask)
    phase("t0", phase_tokens, 0,
          {"wk": chunks(a["wk0"]), "wq": chunks(a["wq0"]), "wv": chunks(a["wv0"]), "bk": a["bk0"], "bq": a["bq0"],
           "bv": a["bv0"].partition_broadcast(P)},
          {"x_src": a["x"], "c_src": a["ctxT"], "qk": qk0, "v": v0})
    phase("a0", phase_attention, False, {"qk": qk0, "v": v0, "mask": mask, "o": o0})
    phase("t1", phase_tokens, 1,
          {"wk": chunks(a["wk1"]), "wq": chunks(a["wq1"]), "wv": chunks(a["wv1"]), "wo": chunks(a["wo0"]),
           "bo": a["bo0"], "lng": a["g1"], "lnb": a["be1"]},
          {"x_src": a["x"], "c_src": o0, "x_dst": x1, "y_dst": y1, "qk": qk1, "v": v1})
    phase("a1", phase_attention, True, {"qk": qk1, "v": v1, "o": o1})
    phase("t2", phase_tokens, 2,
          {"wo": chunks(a["wo1"]), "lngr": a["g2"].partition_broadcast(P), "lnbr": a["be2"].partition_broadcast(P),
           "wg": chunks(a["wg"]), "b2": a["b2"]},
          {"x_src": x1, "y_src": y1, "c_src": o1, "x_dst": base, "xfs": xfs, "gates": gates})
    phase("ex", phase_experts, {"w1": a["w1"], "w2": a["w2"], "b1": a["b1"], "xfs": xfs, "gates": gates, "xs": xs,
                                "ys": ys, "slots": slots, "gsel": gsel})
    phase("la", phase_last,
          {"gate": chunks(a["gate"]), "up": chunks(a["up"]), "down": chunks(a["down"]), "wq": chunks(a["wq2"]),
           "wk": chunks(a["wk2"]), "wv": chunks(a["wv2"]), "bq": a["bq2"], "bk": a["bk2"],
           "bv": a["bv2"].partition_broadcast(P)},
          {"x2": base, "ctxT": a["ctxT"], "y": ys, "slots": slots, "gsel": gsel, "out": out})


def kernel(**inputs):
    import concourse.bacc as bacc
    from concourse.bass_utils import run_bass_kernel_spmd

    t = {k: np.asarray(v) for k, v in inputs.items()}
    order = np.array([(blk * 8 + h) * HD + d for blk in range(DC) for d in range(HD) for h in range(8)])

    def cols(v):
        return v.reshape(-1, P).T

    def padded(wt):
        out = np.zeros((H, HP, D), wt.dtype)
        out[:, :HD] = wt.reshape(H, HD, D)
        return out.reshape(H * HP, D)

    qkv = t["L0_ffn_w_qkv"]
    arrays = {
        "x": t["x"], "ctxT": t["ctx_1024"].transpose(0, 2, 1),
        "mask": t["mask_Bx1xS2_bf1"].reshape(B, S).view(np.uint8),
        "wk0": t["L0_xattn_Wk"].T[:, order], "wq0": t["L0_xattn_Wq"].T[:, order], "wv0": t["L0_xattn_Wv"].T,
        "bk0": cols(t["L0_xattn_bk"][order]), "bq0": cols(t["L0_xattn_bq"][order]), "bv0": t["L0_xattn_bv"],
        "wo0": padded(t["L0_xattn_Wo"].T), "bo0": t["L0_xattn_bo"].reshape(1, D),
        "g1": cols(t["L0_ffn_ln1_g"]), "be1": cols(t["L0_ffn_ln1_b"]),
        "g2": t["L0_ffn_ln2_g"], "be2": t["L0_ffn_ln2_b"],
        "wq1": qkv[:, 0:D][:, order], "wk1": qkv[:, D:2 * D][:, order], "wv1": qkv[:, 2 * D:],
        "wo1": padded(t["L0_ffn_w_o"]), "wg": t["L0_ffn_w_gate"],
        "w1": t["L0_ffn_w1"], "w2": t["L0_ffn_w2"], "b1": t["L0_ffn_b1"].reshape(E_N, FC, P).transpose(0, 2, 1),
        "b2": t["L0_ffn_b2"],
        "wq2": t["L1_xattn_Wq"], "wk2": t["L1_xattn_Wk"], "wv2": t["L1_xattn_Wv"],
        "bq2": cols(t["L1_xattn_bq"]), "bk2": cols(t["L1_xattn_bk"]), "bv2": t["L1_xattn_bv"],
        "gate": t["L1_ffn_w_gate"].T, "up": t["L1_ffn_w_up"].T, "down": t["L1_ffn_w_down"].T,
    }
    nc = bacc.Bacc("TRN2", target_bir_lowering=False, num_devices=1)
    feed, args = {}, {}
    for name, v in arrays.items():
        feed[f"in_{name}"] = np.ascontiguousarray(v)
        args[name] = nc.dram_tensor(f"in_{name}", v.shape, mybir.dt.from_np(v.dtype), kind="ExternalInput").ap()
    out = nc.dram_tensor("out_x", (B, S, D), F32, kind="ExternalOutput").ap()
    build(nc, args, out)
    return run_bass_kernel_spmd(nc, [feed], core_ids=[0]).results[0]["out_x"]
```

```python
import numpy as np
import concourse.bass as bass
from concourse import mybir
from contextlib import ExitStack

F32 = mybir.dt.float32
BF16 = mybir.dt.bfloat16
I32 = mybir.dt.int32
U8 = mybir.dt.uint8
U32 = mybir.dt.uint32
F16 = mybir.dt.float16
ALU = mybir.AluOpType
ACT = mybir.ActivationFunctionType
AX = mybir.AxisListType
ds = bass.ds

P = 128
B, S, D = 8, 512, 256
TT = S // P
DC = D // P
H, HD = 16, 16
HP = 32
GH = 4
NG = H // GH
G_ALL = B * NG
EPS = 1e-5
NEG = -1e30
E_N, FF = 8, 1024
FC = FF // P
NT = B * TT
TE = 256
CHOSEN = 2
TILES = CHOSEN * B * S // TE + E_N - 1
WSCALE = 64.0
F2 = 768
F2C = F2 // P
SCALE2 = 1.0 / 127.0
NPART = 3
NTERM = 6
KM = NTERM * HD
K_MAX = KM + 1
K_EXP = KM + 1 + NPART


class Chain:

    def __init__(self, eng, sem):
        self.eng, self.sem, self.n = eng, sem, 0

    def __call__(self, ins):
        self.n += 1
        ins.then_inc(self.sem, 1)
        self.eng.wait_ge(self.sem, self.n)

    def reset(self):
        self.eng.sem_clear(self.sem)
        self.n = 0


def by_pairs(eng, body, peel_last=False):
    for par in range(2):
        body(par, par)
    with eng.Fori(1, B // 2 - peel_last) as i:
        for par in range(2):
            body(i * 2 + par, par)
    if peel_last:
        for par in range(2):
            body(B - 2 + par, par)


def inverse_deviations(pool, c, mv, rstd, var_ready, rstd_ready, times):
    power, var, eps, own = c.half_power
    pool.memset(power[:], -0.5).then_inc(own, 1)
    pool.memset(eps[:], EPS).then_inc(own, 1)
    pool.wait_ge(own, 2)
    with pool.Fori(0, times) as k:
        pool.wait_ge(var_ready, k + 1)
        pool.tensor_tensor(var[:], mv[:, :, 1], eps[:], ALU.add).then_inc(own, 1)
        pool.wait_ge(own, k + 3)
        pool.tensor_tensor(rstd[:], var[:], power[:], ALU.pow).then_inc(rstd_ready, 1)


class Ctx:

    def __init__(self, nc, tag, stack):
        self.nc, self.tag, self.stack, self.sems = nc, tag, stack, []

    def sb(self, name, shape, dt=F32):
        return self.stack.enter_context(self.nc.sbuf_tensor(f"{self.tag}_{name}", shape, dt))

    def ps(self, name, shape, dt=F32):
        return self.stack.enter_context(self.nc.psum_tensor(f"{self.tag}_{name}", shape, dt))

    def sem(self, name):
        self.sems.append(self.stack.enter_context(self.nc.semaphore(f"{self.tag}_{name}")))
        return self.sems[-1]


def phase_tokens(nc, c, stage, w, scr):
    xin = [c.sb(f"xin{p}", [P, TT, D]) for p in range(2)]
    cin = [c.sb(f"cin{p}", [P, DC, S] if stage == 0 else [P, NG, S]) for p in range(2)]
    y = [c.sb(f"y{p}", [P, TT, D]) for p in range(2)]
    y0 = [c.sb(f"y0{p}", [P, TT, D]) for p in range(2)]
    XS = 2 if stage == 1 else 1
    XL = 2 if stage == 2 else 1
    yT = c.sb("yT", [P, DC, S])
    stats = c.sb("stats", [P, TT, 6])
    mv = c.sb("mv", [P, TT, 2])
    rstd = c.sb("rstd", [P, TT])
    xo = [c.sb(f"xo{p}", [P, TT, D]) for p in range(2)]
    ident = c.sb("ident", [P, P])
    psT = c.ps("psT", [P, DC * S])
    psQ = [c.ps(f"psQ{k}", [P, S]) for k in range(2)]
    NV = TT
    psV = [c.ps(f"psV{k}", [P, 512]) for k in range(NV)]
    if stage < 2:
        full = c.sb("full", [P, 2, DC, S])
        rest = c.sb("rest", [P, DC, S])
        parts = [c.sb(f"parts{p}", [P, 2, NPART, DC, S], BF16) for p in range(2)]
        vaug = [c.sb(f"vaug{p}", [P, TT, H, HP]) for p in range(2)]
        wk, wq, wv = (c.sb(n, [P, DC, D]) for n in ("wk", "wq", "wv"))
        bv = c.sb("bv", [P, D])
        bk, bq = c.sb("bk", [P, DC]), c.sb("bq", [P, DC])
    if stage == 2:
        wg = c.sb("wg", [P, DC, E_N])
        lg = c.sb("lg", [P, TT, E_N])
        lmax = c.sb("lmax", [P, TT])
        ex = c.sb("ex", [P, TT, E_N])
        gt = c.sb("gt", [P, TT, E_N, E_N])
        eq = c.sb("eq", [P, TT, E_N, E_N])
        lower = c.sb("lower", [P, E_N, E_N])
        tot = c.sb("tot", [P, TT])
        gate = [c.sb(f"gate{p}", [P, TT, 2, E_N]) for p in range(2)]
        gT = c.sb("gT", [E_N, S])
        b2 = c.sb("b2", [E_N, D])
        lngr, lnbr = c.sb("lngr", [P, D]), c.sb("lnbr", [P, D])
        xfs = [c.sb(f"xfs{p}", [P, TT, 2, D], F16) for p in range(2)]
    if stage > 0:
        wo = c.sb("wo", [P, NG, D])
        lng, lnb = c.sb("lng", [P, DC]), c.sb("lnb", [P, DC])
    if stage == 1:
        bo = c.sb("bo", [1, D])
    ones = c.sb("ones", [1, P])

    n_const = [0]
    const_in = c.sem("const_in")
    set_done = c.sem("set_done")
    x_in = [c.sem(f"x_in{p}") for p in range(2)]
    c_in = [c.sem(f"c_in{p}") for p in range(2)]
    x_used, c_used = c.sem("x_used"), c.sem("c_used")
    y_ready, tr_ps, yT_ready = c.sem("y_ready"), c.sem("tr_ps"), c.sem("yT_ready")
    q_ps, q_free, v_ps, v_free = c.sem("q_ps"), c.sem("q_free"), c.sem("v_ps"), c.sem("v_free")
    full_ready, split_done = c.sem("full_ready"), c.sem("split_done")
    v_ready = c.sem("v_ready")
    qk_out = [c.sem(f"qk_out{p}") for p in range(2)]
    v_out = [c.sem(f"v_out{p}") for p in range(2)]
    x_out = [c.sem(f"x_out{p}") for p in range(2)]
    xo_ready, gates_ready, logit_ready, exp_ready = (
        c.sem("xo_ready"), c.sem("gates_ready"), c.sem("logit_ready"), c.sem("exp_ready"))
    yT_used = c.sem("yT_used")
    y0_ready = c.sem("y0_ready")
    var_ready, rstd_ready = c.sem("var_ready"), c.sem("rstd_ready")
    c.half_power = (c.sb("power", [P, TT]), c.sb("var", [P, TT]), c.sb("eps", [P, TT]), c.sem("pool_own"))
    NORMS = 2 if stage == 1 else 1
    dve_own, act_own = c.sem("dve_own"), c.sem("act_own")
    QK = 4
    VU = {0: TT, 1: 2 * TT, 2: 3 * TT}[stage]

    def projected(n):
        return 0 if isinstance(n, int) and n == 0 else n * VU - TT

    def last_units(n):
        if stage == 0:
            return n * VU
        return n * VU + (VU - TT if isinstance(n, int) and n == B - 1 else VU)

    QKD = 2 * DC
    consts = []
    if stage < 2:
        consts += [(wk, w["wk"]), (wq, w["wq"]), (wv, w["wv"])]
        if stage == 0:
            consts += [(bk, w["bk"]), (bq, w["bq"])]
    if stage > 0:
        consts += [(wo, w["wo"])]
    if stage == 1:
        consts += [(bo, w["bo"]), (lng, w["lng"]), (lnb, w["lnb"])]
    if stage == 2:
        consts += [(wg, w["wg"]), (b2, w["b2"]), (lngr, w["lngr"]), (lnbr, w["lnbr"])]
    hi_ready, xfs_ready, gT_ps, gT_ready = c.sem("hi_ready"), c.sem("xfs_ready"), c.sem("gT_ps"), c.sem("gT_ready")
    if stage == 0:
        consts += [(bv, w["bv"])]
    n_consts = len(consts)

    with nc.Block() as block:

        @block.sync
        def _(sp):
            for tile, src in consts:
                sp.dma_start(tile[:], src).then_inc(const_in, 16)

            def load(n, par):
                sp.wait_ge(x_used, n + 1)
                sp.dma_start(xin[par][:], scr["x_src"][ds(n, 1)].rearrange("o (t p) d -> p (o t) d", p=P)
                             ).then_inc(x_in[par], 16)
                if stage == 2:
                    sp.dma_start(y0[par][:], scr["y_src"][ds(n, 1)].rearrange("o (t p) d -> p (o t) d", p=P)
                                 ).then_inc(x_in[par], 16)
                sp.wait_ge(c_used, n + 1)
                if stage == 0:
                    src = scr["c_src"][ds(n, 1)].rearrange("o (c p) s -> p (o c) s", p=P)
                else:
                    src = scr["c_src"][ds(n * NG, NG)].rearrange("g p s -> p g s")
                sp.dma_start(cin[par][:], src).then_inc(c_in[par], 16)

            def store_x(n, par):
                sp.wait_ge(xo_ready, n + 1)
                sp.dma_start(scr["x_dst"][ds(n, 1)].rearrange("o (t p) d -> p (o t) d", p=P), xo[par][:]
                             ).then_inc(x_out[par], 16)

            def store(n, par):
                if stage == 1:
                    store_x(n, par)
                if stage == 1:
                    sp.wait_ge(y0_ready, n + 1)
                    sp.dma_start(scr["y_dst"][ds(n, 1)].rearrange("o (t p) d -> p (o t) d", p=P), y0[par][:]
                                 ).then_inc(x_out[par], 16)
                if stage == 2:
                    sp.wait_ge(xfs_ready, n + 1)
                    sp.dma_start(scr["xfs"][ds(n, 1)].rearrange("o (t p) c -> p (o t) c", p=P),
                                 xfs[par][:].rearrange("p t r d -> p t (r d)")).then_inc(v_out[par], 16)
                    sp.wait_ge(gates_ready, n + 1)
                    sp.dma_start(scr["gates"][ds(n, 1)].rearrange("o p t r e -> p (o t r e)"),
                                 gate[par][:].rearrange("p t r e -> p (t r e)")).then_inc(qk_out[par], 16)
                    store_x(n, par)
                    return
                for k in range(2):
                    sp.wait_ge(split_done, n * 2 + k + 1)
                    for blk in range(DC):
                        sp.dma_start(scr["qk"][ds(n * DC + blk, 1), k].rearrange("o t p s -> p (o t) s"),
                                     parts[par][:, k, :, blk, :]).then_inc(qk_out[par], 16)
                sp.wait_ge(v_ready, n + 1)
                sp.dma_start(scr["v"][ds(n, 1)].rearrange("o (t p) c -> p (o t) c", p=P),
                             vaug[par][:].rearrange("p t h c -> p t (h c)")).then_inc(v_out[par], 16)

            sp.sem_inc(x_used, 2)
            sp.sem_inc(c_used, 2)
            load(0, 0)
            load(1, 1)

            def body(n, par):
                if not (isinstance(n, int) and n >= B - 2):
                    load(n + 2, par)
                store(n, par)

            by_pairs(sp, body, peel_last=True)
            for par in range(2):
                if stage < 2:
                    sp.wait_ge(qk_out[par], 16 * QKD * (B // 2))
                else:
                    sp.wait_ge(qk_out[par], 16 * (B // 2))
                sp.wait_ge(v_out[par], 16 * (B // 2))
                if stage > 0:
                    sp.wait_ge(x_out[par], 16 * XS * (B // 2))

        @block.gpsimd
        def _(pool):
            pool.memset(ident[:], 0.0).then_inc(set_done, 1)
            pool.wait_ge(set_done, 1)
            pool.affine_select(out=ident[:], in_=ident[:], compare_op=ALU.not_equal, fill=1.0, base=0,
                               pattern=[[-1, P]], channel_multiplier=1).then_inc(set_done, 1)
            pool.memset(ones[:], 1.0).then_inc(set_done, 1)
            if stage < 2:
                for p in range(2):
                    pool.memset(vaug[p][:], 0.0).then_inc(set_done, 1)
                pool.wait_ge(set_done, 5)
                for p in range(2):
                    pool.memset(vaug[p][:, :, :, HD:HD + 1], 1.0).then_inc(set_done, 1)
            else:
                pool.memset(lower[:], 0.0).then_inc(set_done, 1)
                pool.wait_ge(set_done, 4)
                pool.affine_select(out=lower[:], in_=lower[:], compare_op=ALU.is_ge, fill=1.0, base=0,
                                   pattern=[[-1, E_N], [1, E_N]], channel_multiplier=0).then_inc(set_done, 1)
            inverse_deviations(pool, c, mv, rstd, var_ready, rstd_ready, B * NORMS)

        n_set = 7 if stage < 2 else 5

        @block.vector
        def _(dve):
            link = Chain(dve, dve_own)
            dve.wait_ge(set_done, n_set)
            dve.wait_ge(const_in, 16 * n_consts)

            def norm(k, src, dst):
                for t in range(TT):
                    last = dve.bn_stats(stats[:, t, :], src[:, t, :])
                link(last)
                for t in range(TT):
                    last = dve.bn_aggr(mv[:, t, :], stats[:, t, :])
                last.then_inc(var_ready, 1)
                dve.wait_ge(rstd_ready, k + 1)
                for t in range(TT):
                    last = dve.tensor_scalar(dst[:, t, :], src[:, t, :], mv[:, t, 0:1], rstd[:, t:t + 1],
                                             ALU.subtract, ALU.mult)
                return last

            def split(n, par, k):
                dve.wait_ge(full_ready, n * QK + DC * (k + 1))
                dve.wait_ge(split_done, n * 2 + k)
                a = parts[par]
                link(dve.tensor_tensor(rest[:], full[:, k], a[:, k, 0], ALU.subtract))
                link(dve.tensor_copy(a[:, k, 1], rest[:]))
                dve.tensor_tensor(a[:, k, 2], rest[:], a[:, k, 1], ALU.subtract).then_inc(split_done, 1)

            def values(n, par):
                dve.wait_ge(v_out[par], (n - par) * 8)
                for t in range(TT):
                    dve.wait_ge(v_ps, last_units(n) + t + 1)
                    src = psV[t][:, 0:D].rearrange("p (h d) -> p h d", h=H)
                    dst = vaug[par][:, t, :, 0:HD]
                    if stage == 0:
                        last = dve.tensor_tensor(dst, src, bv[:].rearrange("p (h d) -> p h d", h=H), ALU.add)
                    else:
                        last = dve.tensor_copy(dst, src)
                    last.then_inc(v_free, 1)
                dve.drain().then_inc(v_ready, 1)

            def front(n, par, between=None):
                dve.wait_ge(x_in[par], (n - par) * (8 * XL) + 16 * XL)
                src = xin[par]
                if stage > 0:
                    dve.wait_ge(x_out[par], (n - par) * (8 * XS))
                    for t in range(TT):
                        dve.wait_ge(v_ps, projected(n) + t + 1)
                        last = dve.tensor_tensor(xo[par][:, t, :], psV[t][:, 0:D],
                                                 (y0 if stage == 2 else xin)[par][:, t, :], ALU.add)
                        last.then_inc(v_free, 1)
                    src = xo[par]
                    dve.wait_ge(v_free, projected(n) + TT + NV)
                if stage == 1:
                    dve.sem_inc(xo_ready, 1)
                    dve.sem_inc(x_used, 1)
                    link(norm(n * NORMS, src, y0[par]))
                    dve.sem_inc(y0_ready, 1)
                    if between:
                        between()
                    src = y0[par]
                if not (isinstance(n, int) and n < 2):
                    dve.wait_ge(tr_ps, n - 1)
                last = norm(n * NORMS + NORMS - 1, src, y[par])
                if stage == 2:
                    link(last)
                    link(dve.tensor_tensor(y[par][:], y[par][:], lngr[:].unsqueeze(1).to_broadcast([P, TT, D]),
                                           ALU.mult))
                    last = dve.tensor_tensor(y[par][:], y[par][:], lnbr[:].unsqueeze(1).to_broadcast([P, TT, D]),
                                             ALU.add)
                link(last)
                dve.sem_inc(y_ready, 1)
                if stage == 0:
                    dve.sem_inc(x_used, 1)
                if stage == 2:
                    link(dve.tensor_tensor(xo[par][:], xo[par][:], xin[par][:], ALU.add))
                    dve.sem_inc(x_used, 1)

            def body(n, par):
                more = not (isinstance(n, int) and n == B - 1)
                if stage == 2:
                    experts(n, par)
                if more:
                    front(n + 1, 1 - par, (lambda: values(n, par)) if stage == 1 else None)
                elif stage == 1:
                    values(n, par)
                if stage == 2:
                    dve.wait_ge(hi_ready, n + 1)
                    dve.tensor_tensor(xfs[par][:, :, 1, :], y[par][:], xfs[par][:, :, 0, :], ALU.subtract
                                      ).then_inc(xfs_ready, 1)
                    for t in range(TT):
                        dve.wait_ge(v_ps, last_units(n) + t + 1)
                        dve.tensor_tensor(xo[par][:, t, :], psV[t][:, 0:D], xo[par][:, t, :], ALU.add
                                          ).then_inc(v_free, 1)
                    dve.drain().then_inc(xo_ready, 1)
                else:
                    dve.wait_ge(qk_out[par], (n - par) * (8 * QKD))
                    split(n, par, 0)
                    if stage == 0:
                        values(n, par)
                        split(n, par, 1)
                    else:
                        split(n, par, 1)
                link.reset()

            def experts(n, par):
                for t in range(TT):
                    dve.wait_ge(v_ps, n * VU + TT + t + 1)
                    last = dve.tensor_copy(lg[:, t, :], psV[t][:, 0:E_N])
                    last.then_inc(v_free, 1)
                dve.wait_ge(v_free, n * VU + 2 * TT + NV)
                link(dve.tensor_reduce(lmax[:], lg[:], axis=AX.X, op=ALU.max))
                dve.tensor_tensor(ex[:], lg[:], lmax[:, :].unsqueeze(2).to_broadcast([P, TT, E_N]), ALU.subtract
                                  ).then_inc(logit_ready, 1)
                mine = lg[:, :, :].unsqueeze(3).to_broadcast([P, TT, E_N, E_N])
                other = lg[:, :, :].unsqueeze(2).to_broadcast([P, TT, E_N, E_N])
                dve.tensor_tensor(gt[:], other, mine, ALU.is_gt)
                link(dve.tensor_tensor(eq[:], other, mine, ALU.is_equal))
                for t in range(TT):
                    last = dve.tensor_tensor(eq[:, t], eq[:, t], lower[:], ALU.mult)
                link(last)
                link(dve.tensor_tensor(gt[:], gt[:], eq[:], ALU.add))
                dve.wait_ge(qk_out[par], (n - par) * 8)
                rank = gate[par][:, :, 1, :]
                link(dve.tensor_reduce(rank, gt[:], axis=AX.X, op=ALU.add))
                dve.wait_ge(exp_ready, n + 1)
                for t in range(TT):
                    last = dve.scalar_tensor_tensor(out=ex[:, t, :], in0=gate[par][:, t, 1, :], scalar=CHOSEN - 0.5,
                                                    in1=ex[:, t, :], op0=ALU.is_lt, op1=ALU.mult)
                link(last)
                link(dve.tensor_reduce(tot[:], ex[:], axis=AX.X, op=ALU.add))
                link(dve.reciprocal(tot[:], tot[:]))
                dve.tensor_tensor(gate[par][:, :, 0, :], ex[:], tot[:, :].unsqueeze(2).to_broadcast([P, TT, E_N]),
                                  ALU.mult).then_inc(gates_ready, 1)

            front(0, 0)
            link.reset()
            by_pairs(dve, body, peel_last=True)

        @block.scalar
        def _(act):
            link = Chain(act, act_own)
            act.wait_ge(const_in, 16 * n_consts)
            act.wait_ge(set_done, n_set)
            if stage == 0:
                link(act.mul(bq[:], bq[:], 0.25))

            def project(n, par, k, scale, bias):
                if not (isinstance(n, int) and n == 0):
                    act.wait_ge(split_done, n * 2 - 1 + k)
                for u in range(DC):
                    act.wait_ge(q_ps, n * QK + DC * k + u + 1)
                    dst = full[:, k, u, :]
                    if bias is None:
                        ins = act.mul(dst, psQ[u][:], scale)
                    else:
                        ins = act.activation(dst, psQ[u][:], ACT.Identity, bias=bias[:, u:u + 1], scale=scale)
                    ins.then_inc(q_free, 1)
                act.wait_ge(q_free, n * QK + DC * (k + 1) + 2)
                act.wait_ge(qk_out[par], (n - par) * (8 * QKD))
                for u in range(DC):
                    act.copy(parts[par][:, k, 0, u, :], full[:, k, u, :]).then_inc(full_ready, 1)

            def transposed(n, par):
                act.wait_ge(tr_ps, n + 1)
                act.wait_ge(yT_used, n)
                if stage != 1:
                    act.copy(yT[:].rearrange("p c s -> p (c s)"), psT[:]).then_inc(yT_ready, 1)
                else:
                    for u in range(DC):
                        act.activation(yT[:, u, :], psT[:, u * S:(u + 1) * S], ACT.Identity,
                                       bias=lnb[:, u:u + 1], scale=lng[:, u:u + 1]).then_inc(yT_ready, 1)

            def body(n, par):
                    if stage == 0:
                        project(n, par, 0, 1.0, bk)
                        transposed(n, par)
                        project(n, par, 1, 0.25, bq)
                    elif stage == 1:
                        transposed(n, par)
                        project(n, par, 0, 1.0, None)
                        project(n, par, 1, 0.25, None)
                    else:
                        act.wait_ge(y_ready, n + 1)
                        act.wait_ge(v_out[par], (n - par) * 8)
                        act.copy(xfs[par][:, :, 0, :], y[par][:]).then_inc(hi_ready, 1)
                        transposed(n, par)
                        act.wait_ge(logit_ready, n + 1)
                        act.activation(ex[:], ex[:], ACT.Exp).then_inc(exp_ready, 1)
                        act.wait_ge(gT_ps, n + 1)
                        act.wait_ge(yT_used, n)
                        act.copy(gT[:], psQ[0][0:E_N, :]).then_inc(gT_ready, 1)

            by_pairs(act, body)

        @block.tensor
        def _(pe):
            pe.wait_ge(const_in, 16 * n_consts)
            pe.wait_ge(set_done, n_set)
            pe.sem_inc(q_free, 2)
            pe.sem_inc(v_free, NV)
            per_T = DC if stage == 1 else 1

            def project(n, k, src, wt):
                for u in range(DC):
                    pe.wait_ge(q_free, n * QK + DC * k + u + 1)
                    for d in range(DC):
                        last = pe.matmul(psQ[u][:], wt[:, d, u * P:(u + 1) * P], src[:, d, :],
                                         start=d == 0, stop=d == DC - 1)
                    last.then_inc(q_ps, 1)

            def values(n, src):
                for t in range(TT):
                    pe.wait_ge(v_free, last_units(n) + t + 1)
                    for d in range(DC):
                        last = pe.matmul(psV[t][:, 0:D], src[:, d, t * P:(t + 1) * P], wv[:, d, :],
                                         start=d == 0, stop=d == DC - 1)
                    last.then_inc(v_ps, 1)
                return last

            def out_proj(n, par):
                pe.wait_ge(c_in[par], (n - par) * 8 + 16)
                for t in range(TT):
                    pe.wait_ge(v_free, projected(n) + t + 1)
                    for g in range(NG):
                        last = pe.matmul(psV[t][:, 0:D], cin[par][:, g, t * P:(t + 1) * P], wo[:, g, :],
                                         start=g == 0, stop=stage == 2 and g == NG - 1)
                    if stage == 1:
                        last = pe.matmul(psV[t][:, 0:D], ones[:], bo[:], start=False, stop=True)
                    last.then_inc(v_ps, 1)
                pe.drain().then_inc(c_used, 1)

            def transpose(n, par):
                pe.wait_ge(y_ready, n + 1)
                pe.wait_ge(yT_ready, n * per_T)
                for t in range(TT):
                    for d in range(DC):
                        last = pe.transpose(psT[:, d * S + t * P:d * S + (t + 1) * P],
                                            y[par][:, t, d * P:(d + 1) * P], ident[:])
                last.then_inc(tr_ps, 1)

            def body(n, par):
                more = not (isinstance(n, int) and n == B - 1)
                if stage == 0:
                    pe.wait_ge(c_in[par], (n - par) * 8 + 16)
                    project(n, 0, cin[par], wk)
                transpose(n, par)
                if stage == 0:
                    values(n, cin[par])
                    pe.drain().then_inc(c_used, 1)
                if stage == 1 and more:
                    out_proj(n + 1, 1 - par)
                pe.wait_ge(yT_ready, n * per_T + per_T)
                if stage == 0:
                    project(n, 1, yT, wq)
                elif stage == 1:
                    values(n, yT)
                    project(n, 0, yT, wk)
                    project(n, 1, yT, wq)
                else:
                    for t in range(TT):
                        pe.wait_ge(v_free, n * VU + TT + t + 1)
                        for d in range(DC):
                            last = pe.matmul(psV[t][:, 0:E_N], yT[:, d, t * P:(t + 1) * P], wg[:, d, :],
                                             start=d == 0, stop=d == DC - 1)
                        last.then_inc(v_ps, 1)
                    if more:
                        out_proj(n + 1, 1 - par)
                    pe.wait_ge(gates_ready, n + 1)
                    for t in range(TT):
                        last = pe.transpose(psQ[0][0:E_N, t * P:(t + 1) * P], gate[par][:, t, 0, :], ident[:])
                    last.then_inc(gT_ps, 1)
                    pe.wait_ge(gT_ready, n + 1)
                    for t in range(TT):
                        pe.wait_ge(v_free, last_units(n) + t + 1)
                        pe.matmul(psV[t][:, 0:D], gT[:, t * P:(t + 1) * P], b2[:], start=True, stop=True
                                  ).then_inc(v_ps, 1)
                pe.drain().then_inc(yT_used, 1)

            if stage > 0:
                out_proj(0, 0)
            by_pairs(pe, body, peel_last=True)


def half_of(x):
    return x // 2


def quarter_of(x):
    return x // 4


def phase_attention(nc, c, causal, scr):
    SLOTS = 8
    LA = 2
    U = GH * TT
    NP_BUF = 8
    K6 = [c.sb(f"K6_{s}", [K_EXP, GH, S], BF16) for s in range(SLOTS)]
    Q6 = [c.sb(f"Q6_{s}", [K_EXP, GH, S], BF16) for s in range(SLOTS)]
    V = [c.sb(f"V_{s}", [P, TT, GH * HP]) for s in range(SLOTS)]
    NM_BUF = 4
    nm = [c.sb(f"nm{s}", [P, TT, GH]) for s in range(NM_BUF)]
    nr = c.sb("nr", [P, TT, GH])
    nparts = c.sb("nparts", [P, TT, NPART * GH], BF16)
    nrow = [c.sb(f"nrow{s}", [NPART * GH, S], BF16) for s in range(2)]
    prob = [c.sb(f"prob{s}", [P, S]) for s in range(NP_BUF)]
    oT = [c.sb(f"oT{s}", [P, S]) for s in range(2)]
    on = [c.sb(f"on{s}", [P, S]) for s in range(2)]
    identb = c.sb("identb", [P, P], BF16)
    ident = c.sb("ident", [P, P])
    one = c.sb("one", [P, 1, 1])
    pick = c.sb("pick", [P, GH])
    rc = [c.sb(f"rc{s}", [P, TT * GH]) for s in range(2)]
    rcx = [c.sb(f"rcx{s}", [P, TT * GH * HP]) for s in range(2)]
    cmq = c.sb("cmq", [P, P], BF16)
    cmk = c.sb("cmk", [P, P], BF16)
    NS, NE = 4, 2
    psS_all = c.ps("psS", [P, NS, S])
    psS = [psS_all[:, k] for k in range(NS)]
    rowc = c.sb("rowc", [1 + NPART, GH, S], BF16)
    psE = [c.ps(f"psE{k}", [P, S]) for k in range(NE)]
    psO = c.ps("psO", [P, S])
    psM = c.ps("psM", [P, S])
    psMb = psM[:, :].bitcast(BF16)

    set_done, rows_set, rows_in = c.sem("set_done"), c.sem("rows_set"), [c.sem(f"rows_in{s}") for s in range(SLOTS)]
    g_in = [c.sem(f"g_in{s}") for s in range(SLOTS)]
    s_ps, s_free = c.sem("s_ps"), c.sem("s_free")
    e_ps, p_ready, pv_done = c.sem("e_ps"), c.sem("p_ready"), c.sem("pv_done")
    nparts_ready, nT_ps, nrow_ready = c.sem("nparts_ready"), c.sem("nT_ps"), c.sem("nrow_ready")
    nrow_in = [c.sem(f"nrow_in{s}") for s in range(2)]
    oT_ready, den_ps, on_ready, rc_ready = c.sem("oT_ready"), c.sem("den_ps"), c.sem("on_ready"), c.sem("rc_ready")
    one_set = c.sem("one_set")
    spread_ps, rcx_ready = c.sem("spread_ps"), c.sem("rcx_ready")
    o_out = [c.sem(f"o_out{s}") for s in range(2)]
    dve_own, part_done = c.sem("dve_own"), c.sem("part_done")
    PART_AT = (0, 2, 4, 6)
    ZROWS = TILES * TE // G_ALL
    ZR = 3
    if causal:
        zero = c.sb("zero", [ZROWS // ZR, ZR * 2 * D], F16)
        zero_set, zero_out = c.sem("zero_set"), c.sem("zero_out")
    N_LOAD = 2 * NPART + (1 if causal else 2)

    def steps(eng, first, step):
        step(0, 0)
        with eng.Fori(0, 3) as i:
            for s in range(1, SLOTS + 1):
                step(i * SLOTS + s, s % SLOTS)
        for G in range(3 * SLOTS + 1, G_ALL):
            step(G, G % SLOTS)

    def last_of(G, k):
        return isinstance(G, int) and G + k >= G_ALL

    n_set = 10 if causal else 6

    with nc.Block() as block:

        @block.gpsimd
        def _(pool):
            pool.memset(identb[:], 0.0).then_inc(set_done, 1)
            pool.memset(ident[:], 0.0).then_inc(set_done, 1)
            pool.memset(pick[:], 0.0).then_inc(set_done, 1)
            pool.wait_ge(set_done, 3)
            pool.affine_select(out=ident[:], in_=ident[:], compare_op=ALU.not_equal, fill=1.0, base=0,
                               pattern=[[-1, P]], channel_multiplier=1).then_inc(set_done, 1)
            pool.affine_select(out=identb[:], in_=identb[:], compare_op=ALU.not_equal, fill=1.0, base=0,
                               pattern=[[-1, P]], channel_multiplier=1).then_inc(set_done, 1)
            pool.affine_select(out=pick[:], in_=pick[:], compare_op=ALU.not_equal, fill=1.0, base=-HD,
                               pattern=[[-HP, GH]], channel_multiplier=1).then_inc(set_done, 1)
            if causal:
                pool.memset(zero[:], 0.0).then_inc(zero_set, 1)
                pool.memset(cmq[:], 0.0).then_inc(set_done, 1)
                pool.memset(cmk[:], 0.0).then_inc(set_done, 1)
                pool.wait_ge(set_done, 8)
                pool.affine_select(out=cmq[:], in_=cmq[:], compare_op=ALU.is_ge, fill=NEG, base=0,
                                   pattern=[[-1, P]], channel_multiplier=1).then_inc(set_done, 1)
                pool.affine_select(out=cmk[:], in_=cmk[:], compare_op=ALU.is_ge, fill=NEG, base=0,
                                   pattern=[[1, P]], channel_multiplier=-1).then_inc(set_done, 1)

            pool.memset(one[:], 1.0).then_inc(one_set, 1)
            pool.wait_ge(one_set, 1)
            with pool.Fori(0, G_ALL // 2) as i:
                for s in range(2):
                    pool.wait_ge(rc_ready, i * 2 + (s + 1))
                    pool.tensor_tensor(rcx[s][:].rearrange("p (h m) -> p h m", m=HP),
                                       rc[s][:].unsqueeze(2).to_broadcast([P, TT * GH, HP]),
                                       one[:].to_broadcast([P, TT * GH, HP]), ALU.mult).then_inc(rcx_ready, 1)

        @block.sync
        def _(sp):
            def load(G, s):
                if not (isinstance(G, int) and G < SLOTS):
                    sp.wait_ge(oT_ready, G - SLOTS + 1)
                g = s % NG
                blk, half = g // 2, g % 2
                row = (G - g) // 2 + blk if isinstance(G, int) else half_of(G - g) + blk
                at = 0
                for r in range(NPART):
                    m = NPART - r
                    src = scr["qk"][ds(row, 1), 0, 0:m].rearrange("o t (d e h) n -> (o t d) e (h n)", d=HD, e=2)
                    sp.dma_start(K6[s][at:at + m * HD].rearrange("p h n -> p (h n)"), src[:, half, :]
                                 ).then_inc(g_in[s], 16)
                    src = scr["qk"][ds(row, 1), 1, r].rearrange("o (d e h) n -> (o d) e (h n)", d=HD, e=2)
                    sp.dma_start(Q6[s][at:at + m * HD].rearrange("p h n -> p (h n)"),
                                 src[:, half, :].unsqueeze(0).to_broadcast([m, HD, GH * S])
                                 ).then_inc(g_in[s], 16)
                    at += m * HD
                b = (G - g) // NG if isinstance(G, int) else quarter_of(G - g)
                sp.dma_start(V[s][:], scr["v"][ds(b, 1), :, g * GH * HP:(g + 1) * GH * HP]
                             .rearrange("o (t p) c -> p (o t) c", p=P)).then_inc(g_in[s], 16)
                if not causal:
                    sp.dma_start(K6[s][KM:KM + 1, :, :],
                                 scr["mask"][ds(b, 1), :].unsqueeze(1).to_broadcast([1, GH, S])
                                 ).then_inc(g_in[s], 16)

            for G in range(SLOTS // 2):
                load(G, G)

            def maxima(G, s):
                sp.wait_ge(nrow_ready, G + 1)
                for r in range(NPART):
                    sp.dma_start(Q6[s][KM + 1 + r:KM + 2 + r, :, :],
                                 nrow[s % 2][r * GH:(r + 1) * GH, :]).then_inc(nrow_in[s % 2], 16)

            def result(G, s):
                sp.wait_ge(on_ready, 2 + G + 1)
                sp.dma_start(scr["o"][ds(G, 1)].rearrange("o p s -> p (o s)"), on[s % 2][:]
                             ).then_inc(o_out[s % 2], 16)

            maxima(0, 0)
            for G in range(SLOTS // 2, SLOTS):
                load(G, G)
            if causal:
                sp.wait_ge(zero_set, 1)

            def step(G, s):
                if not last_of(G, 1):
                    maxima(G + 1, (s + 1) % SLOTS)
                if causal:
                    sp.dma_start(scr["xs"][ds(G * ZROWS, ZROWS)].rearrange("(p r) c -> p (r c)", r=ZR), zero[:]
                                 ).then_inc(zero_out, 16)
                if isinstance(G, int) and G == 0:
                    return
                result(G - 1, (s - 1) % SLOTS)
                if not last_of(G, SLOTS - 1):
                    load(G + SLOTS - 1, (s - 1) % SLOTS)

            steps(sp, 0, step)
            result(G_ALL - 1, (G_ALL - 1) % SLOTS)
            for k in range(2):
                sp.wait_ge(o_out[k], 16 * (G_ALL // 2))
            if causal:
                sp.wait_ge(zero_out, 16 * G_ALL)

        @block.tensor
        def _(pe):
            pe.wait_ge(set_done, n_set)
            pe.sem_inc(s_free, NS)
            pe.sem_inc(on_ready, 2)

            def score(G, s, j):
                h, t = j // TT, j % TT
                bank = psS[j % NS]
                n = (t + 1) * P if causal else S
                pe.wait_ge(s_free, G * U + j + 1)
                last = pe.matmul(bank[:, 0:n], Q6[s][0:K_MAX, h, t * P:(t + 1) * P], K6[s][0:K_MAX, h, 0:n],
                                 start=True, stop=not causal)
                if causal:
                    last = pe.matmul(bank[:, t * P:n], identb[:], cmq[:], start=False, stop=True)
                last.then_inc(s_ps, 1)

            def shifted(G, s, j):
                t, h = j // GH, j % GH
                bank = psE[j % NE]
                q0 = t * P if causal else 0
                if not (isinstance(G, int) and G == 0 and j < NE):
                    pe.wait_ge(p_ready, G * U + j + 1 - NE)
                last = pe.matmul(bank[:, 0:S - q0], K6[s][0:K_EXP, h, t * P:(t + 1) * P], Q6[s][0:K_EXP, h, q0:S],
                                 start=True, stop=not causal)
                if causal:
                    last = pe.matmul(bank[:, 0:P], identb[:], cmk[:], start=False, stop=True)
                last.then_inc(e_ps, 1)

            def weigh(G, s, j):
                t, h = j // GH, j % GH
                q0 = t * P if causal else 0
                if j == 0:
                    pe.wait_ge(oT_ready, G)
                pe.wait_ge(p_ready, G * U + j + 1)
                pe.matmul(psO[h * HP:(h + 1) * HP, q0:S], V[s][:, t, h * HP:(h + 1) * HP],
                          prob[j % NP_BUF][:, 0:S - q0], start=t == 0, stop=t == TT - 1).then_inc(pv_done, 1)

            def maxima(G, s):
                pe.wait_ge(nparts_ready, G + 1)
                if isinstance(G, int) and G == 1:
                    pe.wait_ge(nrow_ready, 1)
                elif not (isinstance(G, int) and G == 0):
                    pe.wait_ge(rc_ready, G - 1)
                for t in range(TT):
                    last = pe.transpose(psMb[0:NPART * GH, t * P:(t + 1) * P], nparts[:, t, :], identb[:])
                last.then_inc(nT_ps, 1)

            def denominators(G, s):
                pe.wait_ge(oT_ready, G + 1)
                pe.wait_ge(on_ready, 2 + G)
                for t in range(TT):
                    last = pe.matmul(psM[:, t * GH:(t + 1) * GH], oT[s % 2][:, t * P:(t + 1) * P], pick[:],
                                     start=True, stop=True)
                last.then_inc(den_ps, 1)

            def spread(G, s):
                pe.wait_ge(rcx_ready, G + 1)
                if not last_of(G, 2):
                    pe.wait_ge(nrow_ready, G + 3)
                for t in range(TT):
                    last = pe.matmul(psM[:, t * P:(t + 1) * P],
                                     rcx[s % 2][:, t * P:(t + 1) * P], ident[:],
                                     start=True, stop=True)
                last.then_inc(spread_ps, 1)

            for G in range(LA):
                pe.wait_ge(g_in[G], 16 * N_LOAD)
                pe.wait_ge(rows_in[G], 32)
                for j in range(U):
                    score(G, G, j)
                    if G == 1 and j == 5:
                        maxima(0, 0)

            def step(G, s):
                if isinstance(G, int) and G == 0:
                    first = True
                else:
                    first = False
                pe.wait_ge(nrow_in[s % 2], (G - s % 2) * 24 + 48)
                more = not last_of(G, LA)
                s2 = (s + LA) % SLOTS
                if more:
                    pe.wait_ge(g_in[s2], loads_of(G + LA, s2))
                    pe.wait_ge(rows_in[s2], 32)
                for j in range(U):
                    if more:
                        score(G + LA, s2, j)
                    shifted(G, s, j)
                    if j >= 3:
                        weigh(G, s, j - 3)
                    elif j < 2 and not first:
                        weigh(G - 1, (s - 1) % SLOTS, U - 3 + 2 * j)
                        if j == 0:
                            weigh(G - 1, (s - 1) % SLOTS, U - 2)
                    if j == 4 and not first:
                        denominators(G - 1, (s - 1) % SLOTS)
                    if j == 8 and not last_of(G, 1):
                        maxima(G + 1, (s + 1) % SLOTS)
                    if j == 12 and not first:
                        spread(G - 1, (s - 1) % SLOTS)

            def loads_of(G, s):
                return (G - s) * (16 * N_LOAD // SLOTS) + 16 * N_LOAD

            steps(pe, 0, step)
            G, s = G_ALL - 1, (G_ALL - 1) % SLOTS
            for j in range(U - 3, U):
                weigh(G, s, j)
            denominators(G, s)
            spread(G, s)

        @block.scalar
        def _(act):
            def evacuate(G, s):
                act.wait_ge(pv_done, G * U + U)
                act.wait_ge(on_ready, G + 1)
                act.copy(oT[s % 2][:], psO[:]).then_inc(oT_ready, 1)

            def step(G, s):
                for j in range(U):
                    t = j // GH
                    n = S - t * P if causal else S
                    act.wait_ge(e_ps, G * U + j + 1)
                    if not (isinstance(G, int) and G == 0 and j < NP_BUF):
                        act.wait_ge(pv_done, G * U + j + 1 - NP_BUF)
                    act.activation(prob[j % NP_BUF][:, 0:n], psE[j % NE][:, 0:n], ACT.Exp).then_inc(p_ready, 1)
                    if j == 1 and not (isinstance(G, int) and G == 0):
                        evacuate(G - 1, (s - 1) % SLOTS)

            act.wait_ge(rows_set, 1)
            k0 = 0 if causal else 1
            for s in range(SLOTS):
                act.dma_start(K6[s][KM + k0:K_EXP, :, :], rowc[k0:, :, :]).then_inc(rows_in[s], 16)
                act.dma_start(Q6[s][KM:KM + 1, :, :], rowc[1:2, :, :]).then_inc(rows_in[s], 16)

            steps(act, 0, step)
            evacuate(G_ALL - 1, (G_ALL - 1) % SLOTS)

        @block.vector
        def _(dve):
            link = Chain(dve, dve_own)
            last = dve.memset(rowc[:], 1.0)
            if causal:
                link(last)
                last = dve.memset(rowc[0:1], 0.0)
            last.then_inc(rows_set, 1)

            def top(G, s, j):
                h, t = j // TT, j % TT
                n = (t + 1) * P if causal else S
                if not causal and j % 2 == 0:
                    return
                dve.wait_ge(s_ps, G * U + j + 1)
                if causal:
                    dve.tensor_reduce(nm[s % NM_BUF][:, t, h:h + 1], psS[j % NS][:, 0:n], axis=AX.X,
                                      op=ALU.max, negate=True).then_inc(s_free, 1)
                elif j % 2:
                    dve.tensor_reduce(nm[s % NM_BUF][:, t - 1:t + 1, h], psS_all[:, (j - 1) % NS:j % NS + 1, :],
                                      axis=AX.X, op=ALU.max, negate=True).then_inc(s_free, 2)

            def shift_part(G, s, k):
                m = nm[s % NM_BUF]
                np_ = nparts[:].rearrange("p t (r h) -> p r t h", r=NPART)
                if k == 0:
                    dve.wait_ge(s_free, G * U + U + NS)
                    dve.wait_ge(nT_ps, G)
                    dve.tensor_copy(np_[:, 0], m[:]).then_inc(part_done, 1)
                    return
                dve.wait_ge(part_done, G * NPART + k)
                if k == 1:
                    dve.tensor_tensor(nr[:], m[:], np_[:, 0], ALU.subtract).then_inc(part_done, 1)
                elif k == 2:
                    dve.tensor_copy(np_[:, 1], nr[:]).then_inc(part_done, 1)
                else:
                    dve.tensor_tensor(np_[:, 2], nr[:], np_[:, 1], ALU.subtract).then_inc(nparts_ready, 1)

            def shift_rows(G, s):
                dve.wait_ge(nT_ps, G + 1)
                if not (isinstance(G, int) and G < 2):
                    dve.wait_ge(nrow_in[s % 2], (G - s % 2) * 24)
                dve.tensor_copy(nrow[s % 2][:], psMb[0:NPART * GH, 0:S]).then_inc(nrow_ready, 1)

            def invert(G, s):
                dve.wait_ge(den_ps, G + 1)
                dve.reciprocal(rc[s % 2][:], psM[:, 0:TT * GH]).then_inc(rc_ready, 1)

            def scale(G, s):
                dve.wait_ge(spread_ps, G + 1)
                if not (isinstance(G, int) and G < 2):
                    dve.wait_ge(o_out[s % 2], (G - s % 2) * 8)
                dve.tensor_tensor(on[s % 2][:], oT[s % 2][:], psM[:], ALU.mult).then_inc(on_ready, 1)

            for G in range(LA):
                for j in range(U):
                    top(G, G, j)
                    if G == 1 and j < 4:
                        shift_part(0, 0, j)
                    if G == 1 and j == 7:
                        shift_rows(0, 0)

            def step(G, s):
                first = isinstance(G, int) and G == 0
                for j in range(U):
                    if j in PART_AT and not last_of(G, 1):
                        shift_part(G + 1, (s + 1) % SLOTS, PART_AT.index(j))
                    if not last_of(G, LA):
                        top(G + LA, (s + LA) % SLOTS, j)
                    if j == 5 and not first:
                        invert(G - 1, (s - 1) % SLOTS)
                    if j == 9 and not last_of(G, 1):
                        shift_rows(G + 1, (s + 1) % SLOTS)
                    if j == 14 and not first:
                        scale(G - 1, (s - 1) % SLOTS)

            link.reset()
            steps(dve, 0, step)
            invert(G_ALL - 1, (G_ALL - 1) % SLOTS)
            scale(G_ALL - 1, (G_ALL - 1) % SLOTS)


def phase_gates(nc, c, w, scr):
    xin, yin, y, base, ob = ([c.sb(f"{n}{p}", [P, TT, D]) for p in range(2)] for n in ("xin", "yin", "y", "base", "ob"))
    cin = [c.sb(f"cin{p}", [P, NG, S]) for p in range(2)]
    xres = c.sb("xres", [P, TT, D])
    yT = c.sb("yT", [P, DC, S])
    stats, mv, rstd = c.sb("stats", [P, TT, 6]), c.sb("mv", [P, TT, 2]), c.sb("rstd", [P, TT])
    c.half_power = (c.sb("power", [P, TT]), c.sb("var", [P, TT]), c.sb("eps", [P, TT]), c.sem("pool_own"))
    ident = c.sb("ident", [P, P])
    wo, wg, b2 = c.sb("wo", [P, NG, D]), c.sb("wg", [P, DC, E_N]), c.sb("b2", [E_N, D])
    lng, lnb = c.sb("lng", [P, D]), c.sb("lnb", [P, D])
    lg, ex = c.sb("lg", [P, TT, E_N]), c.sb("ex", [P, TT, E_N])
    lmax, tot = c.sb("lmax", [P, TT]), c.sb("tot", [P, TT])
    gt, eq = c.sb("gt", [P, TT, E_N, E_N]), c.sb("eq", [P, TT, E_N, E_N])
    lower = c.sb("lower", [P, E_N, E_N])
    gate = [c.sb(f"gate{p}", [P, TT, 2, E_N]) for p in range(2)]
    gT = c.sb("gT", [E_N, S])
    xfs = [c.sb(f"xfs{p}", [P, TT, 2, D], F16) for p in range(2)]
    psT, psG = c.ps("psT", [P, DC * S]), c.ps("psG", [P, S])
    psL = c.ps("psL", [P, 512])
    psV = [c.ps(f"psV{t}", [P, 512]) for t in range(TT)]

    const_in, set_done = c.sem("const_in"), c.sem("set_done")
    x_in, c_in, xfs_out, gate_out, ob_out = ([c.sem(f"{n}{p}") for p in range(2)] for n in (
        "x_in", "c_in", "xfs_out", "gate_out", "ob_out"))
    (c_used, x_used, v_ps, v_free, var_ready, rstd_ready, y_ready, hi_ready, xfs_ready, tr_ps, yT_ready, logit_ready,
     exp_ready, gates_ready, gT_ps, gT_ready, ob_ready, pe_done, own, l_ps, l_free) = (
        c.sem(n) for n in ("c_used", "x_used", "v_ps", "v_free", "var_ready", "rstd_ready", "y_ready", "hi_ready",
                           "xfs_ready", "tr_ps", "yT_ready", "logit_ready", "exp_ready", "gates_ready", "gT_ps",
                           "gT_ready", "ob_ready", "pe_done", "own", "l_ps",
                           "l_free"))
    consts = ((wo, w["wo"]), (wg, w["wg"]), (b2, w["b2"]), (lng, w["lng"]), (lnb, w["lnb"]))

    def is_(n, *values):
        return isinstance(n, int) and n in values

    def v_proj(n):
        return n * TT if is_(n, 0, 1) else (n - 1) * (2 * TT)

    def v_b2(n):
        return n * (2 * TT) + TT * (1 if is_(n, B - 1) else 2 if is_(n, B - 2) else 3)

    def bodies(eng, body):
        for n in range(2):
            body(n, n % 2)
        with eng.Fori(1, B // 2 - 1) as i:
            for par in range(2):
                body(i * 2 + par, par)
        for n in range(B - 2, B + 1):
            body(n, n % 2)

    with nc.Block() as block:

        @block.sync
        def _(sp):
            def load(n, par):
                if not is_(n, 0, 1):
                    sp.wait_ge(x_used, n - 1)
                    sp.wait_ge(c_used, n - 1)
                sp.dma_start(cin[par][:], scr["o"][ds(n * NG, NG)].rearrange("g p s -> p g s")).then_inc(c_in[par], 16)
                for tile, src in ((yin, scr["y1"]), (xin, scr["x1"])):
                    sp.dma_start(tile[par][:], src[ds(n, 1)].rearrange("o (t p) d -> p (o t) d", p=P)
                                 ).then_inc(x_in[par], 16)

            for tile, src in consts:
                sp.dma_start(tile[:], src).then_inc(const_in, 16)
            load(0, 0)
            load(1, 1)

            def body(n, par):
                if not is_(n, B - 2, B - 1, B):
                    load(n + 2, par)
                if not is_(n, B):
                    sp.wait_ge(xfs_ready, n + 1)
                    sp.dma_start(scr["xfs"][ds(n, 1)].rearrange("o (t p) c -> p (o t) c", p=P),
                                 xfs[par][:].rearrange("p t r d -> p t (r d)")).then_inc(xfs_out[par], 16)
                if not is_(n, 0):
                    sp.wait_ge(gates_ready, n)
                    sp.dma_start(scr["gates"][ds(n - 1, 1)].rearrange("o p t r e -> p (o t r e)"),
                                 gate[1 - par][:].rearrange("p t r e -> p (t r e)")).then_inc(gate_out[1 - par], 16)
                    sp.wait_ge(ob_ready, n)
                    sp.dma_start(scr["base"][ds(n - 1, 1)].rearrange("o (t p) d -> p (o t) d", p=P), ob[1 - par][:]
                                 ).then_inc(ob_out[1 - par], 16)

            bodies(sp, body)
            for par in range(2):
                for out in (xfs_out, gate_out, ob_out):
                    sp.wait_ge(out[par], 16 * (B // 2))

        @block.gpsimd
        def _(pool):
            pool.memset(ident[:], 0.0).then_inc(set_done, 1)
            pool.memset(lower[:], 0.0).then_inc(set_done, 1)
            pool.wait_ge(set_done, 2)
            pool.affine_select(out=ident[:], in_=ident[:], compare_op=ALU.not_equal, fill=1.0, base=0,
                               pattern=[[-1, P]], channel_multiplier=1).then_inc(set_done, 1)
            pool.affine_select(out=lower[:], in_=lower[:], compare_op=ALU.is_ge, fill=1.0, base=0,
                               pattern=[[-1, E_N], [1, E_N]], channel_multiplier=0).then_inc(set_done, 1)
            inverse_deviations(pool, c, mv, rstd, var_ready, rstd_ready, B)

        @block.vector
        def _(dve):
            link = Chain(dve, own)
            dve.wait_ge(set_done, 4)
            dve.wait_ge(const_in, 16 * len(consts))

            def front(n, par, b2_of_last):
                dve.wait_ge(x_in[par], (n - par) * 16 + 32)
                for t in range(TT):
                    dve.wait_ge(v_ps, v_proj(n) + t + 1)
                    dve.tensor_tensor(xres[:, t, :], psV[t][:, 0:D], yin[par][:, t, :], ALU.add).then_inc(v_free, 1)
                dve.wait_ge(v_free, v_proj(n) + TT + TT)
                for t in range(TT):
                    last = dve.bn_stats(stats[:, t, :], xres[:, t, :])
                link(last)
                for t in range(TT):
                    last = dve.bn_aggr(mv[:, t, :], stats[:, t, :])
                last.then_inc(var_ready, 1)
                if not is_(n, 0, 1):
                    dve.wait_ge(tr_ps, n - 1)
                dve.wait_ge(rstd_ready, n + 1)
                yn = y[par]
                for t in range(TT):
                    last = dve.tensor_scalar(yn[:, t, :], xres[:, t, :], mv[:, t, 0:1], rstd[:, t:t + 1],
                                             ALU.subtract, ALU.mult)
                link(last)
                link(dve.tensor_tensor(yn[:], yn[:], lng[:].unsqueeze(1).to_broadcast([P, TT, D]), ALU.mult))
                dve.tensor_tensor(yn[:], yn[:], lnb[:].unsqueeze(1).to_broadcast([P, TT, D]), ALU.add
                                  ).then_inc(y_ready, 1)
                b2_of_last()
                link(dve.tensor_tensor(base[par][:], xres[:], xin[par][:], ALU.add))
                dve.sem_inc(x_used, 1)
                dve.wait_ge(hi_ready, n + 1)
                dve.tensor_tensor(xfs[par][:, :, 1, :], yn[:], xfs[par][:, :, 0, :], ALU.subtract
                                  ).then_inc(xfs_ready, 1)

            def experts(n, par):
                dve.wait_ge(l_ps, n + 1)
                dve.tensor_copy(lg[:].rearrange("p t e -> p (t e)"), psL[:, 0:TT * E_N]).then_inc(l_free, 1)
                dve.wait_ge(l_free, n + 1)
                link(dve.tensor_reduce(lmax[:], lg[:], axis=AX.X, op=ALU.max))
                dve.tensor_tensor(ex[:], lg[:], lmax[:, :].unsqueeze(2).to_broadcast([P, TT, E_N]), ALU.subtract
                                  ).then_inc(logit_ready, 1)
                mine = lg[:, :, :].unsqueeze(3).to_broadcast([P, TT, E_N, E_N])
                other = lg[:, :, :].unsqueeze(2).to_broadcast([P, TT, E_N, E_N])
                dve.tensor_tensor(gt[:], other, mine, ALU.is_gt)
                link(dve.tensor_tensor(eq[:], other, mine, ALU.is_equal))
                for t in range(TT):
                    last = dve.tensor_tensor(eq[:, t], eq[:, t], lower[:], ALU.mult)
                link(last)
                link(dve.tensor_tensor(gt[:], gt[:], eq[:], ALU.add))
                dve.wait_ge(gate_out[par], (n - par) * 8)
                link(dve.tensor_reduce(gate[par][:, :, 1, :], gt[:], axis=AX.X, op=ALU.add))
                dve.wait_ge(exp_ready, n + 1)
                for t in range(TT):
                    last = dve.scalar_tensor_tensor(out=ex[:, t, :], in0=gate[par][:, t, 1, :], scalar=CHOSEN - 0.5,
                                                    in1=ex[:, t, :], op0=ALU.is_lt, op1=ALU.mult)
                link(last)
                link(dve.tensor_reduce(tot[:], ex[:], axis=AX.X, op=ALU.add))
                link(dve.reciprocal(tot[:], tot[:]))
                dve.tensor_tensor(gate[par][:, :, 0, :], ex[:], tot[:, :].unsqueeze(2).to_broadcast([P, TT, E_N]),
                                  ALU.mult).then_inc(gates_ready, 1)

            def add_b2(n, par):
                dve.wait_ge(ob_out[par], (n - par) * 8)
                for t in range(TT):
                    dve.wait_ge(v_ps, v_b2(n) + t + 1)
                    dve.tensor_tensor(ob[par][:, t, :], psV[t][:, 0:D], base[par][:, t, :], ALU.add
                                      ).then_inc(v_free, 1)
                dve.drain().then_inc(ob_ready, 1)

            front(0, 0, lambda: None)
            link.reset()

            def body(n, par):
                if not is_(n, 0):
                    experts(n - 1, 1 - par)
                sums = (lambda: None) if is_(n, 0) else (lambda: add_b2(n - 1, 1 - par))
                if is_(n, B - 1, B):
                    sums()
                else:
                    front(n + 1, 1 - par, sums)
                dve.drain()
                link.reset()

            bodies(dve, body)

        @block.scalar
        def _(act):
            def high(n, par):
                act.wait_ge(y_ready, n + 1)
                act.wait_ge(xfs_out[par], (n - par) * 8)
                act.copy(xfs[par][:, :, 0, :], y[par][:]).then_inc(hi_ready, 1)

            high(0, 0)

            def body(n, par):
                if not is_(n, 0):
                    act.wait_ge(logit_ready, n)
                    act.activation(ex[:], ex[:], ACT.Exp).then_inc(exp_ready, 1)
                    act.wait_ge(gT_ps, n)
                    act.wait_ge(pe_done, n)
                    act.copy(gT[:], psG[0:E_N, :]).then_inc(gT_ready, 1)
                if not is_(n, B):
                    act.wait_ge(tr_ps, n + 1)
                    act.wait_ge(pe_done, n)
                    act.copy(yT[:].rearrange("p c s -> p (c s)"), psT[:]).then_inc(yT_ready, 1)
                if not is_(n, B - 1, B):
                    high(n + 1, 1 - par)

            bodies(act, body)

        @block.tensor
        def _(pe):
            pe.wait_ge(const_in, 16 * len(consts))
            pe.wait_ge(set_done, 4)
            pe.sem_inc(v_free, TT)

            def project(n, par):
                pe.wait_ge(c_in[par], (n - par) * 8 + 16)
                for t in range(TT):
                    pe.wait_ge(v_free, v_proj(n) + t + 1)
                    for g in range(NG):
                        last = pe.matmul(psV[t][:, 0:D], cin[par][:, g, t * P:(t + 1) * P], wo[:, g, :],
                                         start=g == 0, stop=g == NG - 1)
                    last.then_inc(v_ps, 1)
                pe.drain().then_inc(c_used, 1)

            project(0, 0)

            def body(n, par):
                if not is_(n, B - 1, B):
                    project(n + 1, 1 - par)
                if not is_(n, 0):
                    pe.wait_ge(gates_ready, n)
                    for t in range(TT):
                        last = pe.transpose(psG[0:E_N, t * P:(t + 1) * P], gate[1 - par][:, t, 0, :], ident[:])
                    last.then_inc(gT_ps, 1)
                if not is_(n, B):
                    pe.wait_ge(y_ready, n + 1)
                    pe.wait_ge(yT_ready, n)
                    for t in range(TT):
                        for d in range(DC):
                            last = pe.transpose(psT[:, d * S + t * P:d * S + (t + 1) * P],
                                                y[par][:, t, d * P:(d + 1) * P], ident[:])
                    last.then_inc(tr_ps, 1)
                if not is_(n, 0):
                    pe.wait_ge(gT_ready, n)
                    for t in range(TT):
                        pe.wait_ge(v_free, v_b2(n - 1) + t + 1)
                        pe.matmul(psV[t][:, 0:D], gT[:, t * P:(t + 1) * P], b2[:], start=True, stop=True
                                  ).then_inc(v_ps, 1)
                if not is_(n, B):
                    pe.wait_ge(yT_ready, n + 1)
                    if not is_(n, 0):
                        pe.wait_ge(l_free, n)
                    for t in range(TT):
                        for d in range(DC):
                            last = pe.matmul(psL[:, t * E_N:(t + 1) * E_N], yT[:, d, t * P:(t + 1) * P], wg[:, d, :],
                                             start=d == 0, stop=d == DC - 1)
                    last.then_inc(l_ps, 1)
                pe.drain().then_inc(pe_done, 1)

            bodies(pe, body)


def phase_experts(nc, c, scr):
    w1h = c.sb("w1h", [P, E_N, 2, DC, FF], F16)
    w2h = c.sb("w2h", [P, E_N, 2, FC, D], F16)
    stage = [c.sb(f"stage{p}", [P, DC * FF]) for p in range(2)]
    gr = c.sb("gr", [P, NT, 2, E_N])
    seld = c.sb("seld", [P, NT * E_N], BF16)
    first = c.sb("first", [P, NT, E_N])
    second = c.sb("second", [P, NT, E_N])
    scan = [c.sb(f"scan{k}", [P, NT, E_N]) for k in range(2)]
    pos = c.sb("pos", [P, NT, E_N])
    tri, ones = c.sb("tri", [P, P], BF16), c.sb("ones", [P, P], BF16)
    NM = B * S // TE
    grid_i, grid = c.sb("grid_i", [P, NM], I32), c.sb("grid", [P, NM])
    tile_i, tile_f = c.sb("tile_i", [P, TILES], I32), c.sb("tile_f", [P, TILES])
    cmp = c.sb("cmp", [P, E_N, NM])
    cmp2 = c.sb("cmp2", [P, TILES, E_N])
    ends = [c.sb(f"ends{k}", [P, E_N]) for k in range(2)]
    count = c.sb("count", [P, E_N])
    start = c.sb("start", [P, E_N])
    ntile = c.sb("ntile", [P, E_N])
    emap_f, emap = c.sb("emap_f", [P, TILES]), c.sb("emap", [P, TILES], I32)
    slot_f, slot = c.sb("slot_f", [P, CHOSEN, NT]), c.sb("slot", [P, CHOSEN, NT], U32)
    gsel = c.sb("gsel", [P, CHOSEN, NT])
    identh = c.sb("identh", [P, P], F16)
    xt = [c.sb(f"xt{p}", [P, 2, 2 * D], F16) for p in range(2)]
    xT = [c.sb(f"xT{p}", [P, 2 * DC, TE], F16) for p in range(2)]
    b1 = [c.sb(f"b1_{p}", [P, FC]) for p in range(2)]
    hf = c.sb("hf", [P, FC, TE])
    hl = [c.sb(f"hl{p}", [P, 2, FC, TE], F16) for p in range(2)]
    yo = [c.sb(f"yo{p}", [P, 2, D]) for p in range(2)]
    hb = hf[:].rearrange("p f t -> p (f t)").bitcast(F16)
    ROW = TT * 2 * D
    xr = [c.sb(f"xr{p}", [P, ROW], F16)[:] for p in range(2)] + [hb[:, k * ROW:(k + 1) * ROW] for k in range(2)] + [
        hl[q][:, r].rearrange("p f t -> p (f t)") for q in range(2) for r in range(2)]
    psX = [c.ps(f"psX{p}", [P, 2 * DC * TE], F16) for p in range(2)]
    psH = [c.ps(f"psH{k}", [P, 2, TE]) for k in range(4)]
    psY = [c.ps(f"psY{k}", [P, 512]) for k in range(2)]
    FP = FC // 2
    PRODUCTS = ((0, 0), (0, 1), (1, 0))

    (gr_in, set_done, sel_ready, cum_ps, slot_ready, slot_out, xs_out, hi_done, w_ready, own, own_act,
     x_ps, x_ready, h_ps, h_free, hl_ready, y_ps, y_free) = (
        c.sem(n) for n in ("gr_in", "set_done", "sel_ready", "cum_ps", "slot_ready", "slot_out", "xs_out",
                           "hi_done", "w_ready", "own", "own_act", "x_ps", "x_ready", "h_ps", "h_free", "hl_ready",
                           "y_ps", "y_free"))
    w_in, xt_in, y_out = ([c.sem(f"{n}{p}") for p in range(2)] for n in ("w_in", "xt_in", "y_out"))
    xr_in = [c.sem(f"xr_in{b}") for b in range(B)]

    def tiles(eng, body):
        for s in range(2):
            body(s, s)
        with eng.Fori(1, TILES // 2) as i:
            for q in range(2):
                body(i * 2 + q, q)
        if TILES % 2:
            body(TILES - 1, 0)

    with nc.Block() as block:

        @block.sync
        def _(sp):
            sp.dma_start(gr[:].rearrange("p n r e -> p (n r e)").rearrange("p (b c) -> p b c", b=B),
                         scr["gates"].rearrange("b p t r e -> p b (t r e)")).then_inc(gr_in, 16)
            for b in range(B):
                sp.dma_start(xr[b].rearrange("p (t c) -> p t c", t=TT), scr["xfs"][b].rearrange("(t p) c -> p t c", p=P)
                             ).then_inc(xr_in[b], 16)
            for e in range(E_N):
                for k in range(2):
                    if e > 0:
                        sp.wait_ge(w_ready, 2 * e + k - 1)
                    src = scr["w1"][e].rearrange("(c p) f -> p c f", p=P) if k == 0 else (
                        scr["w2"][e].rearrange("(c p) d -> p c d", p=P))
                    sp.dma_start(stage[k][:].rearrange("p (c f) -> p c f", c=DC if k == 0 else FC), src
                                 ).then_inc(w_in[k], 16)
            sp.wait_ge(slot_ready, 2)
            sp.dma_start(scr["slots"], slot[:]).then_inc(slot_out, 16)
            sp.dma_start(scr["gsel"], gsel[:]).then_inc(slot_out, 16)
            sp.wait_ge(xs_out, 16 * CHOSEN * NT)

            def load(s, q):
                e = sp.value_load(emap[0:1, ds(s, 1)], min_val=0, max_val=E_N - 1)
                if not (isinstance(s, int) and s < 2):
                    sp.wait_ge(x_ps, s - 1)
                    sp.wait_ge(h_free, (s - 1) * FC + 8)
                sp.dma_start(b1[q][:], scr["b1"][ds(e, 1)].rearrange("o p f -> p (o f)")).then_inc(xt_in[q], 16)
                sp.dma_start(xt[q][:], scr["xs"][ds(s * TE, TE)].rearrange("(h p) c -> p h c", p=P)
                             ).then_inc(xt_in[q], 16)

            def store(s, q):
                sp.wait_ge(y_free, s + 2)
                sp.dma_start(scr["ys"][ds(s * TE, TE)].rearrange("(h p) d -> p h d", p=P), yo[q][:]
                             ).then_inc(y_out[q], 16)

            def body(s, q):
                load(s, q)
                if not (isinstance(s, int) and s < 2):
                    store(s - 2, q)

            tiles(sp, body)
            store(TILES - 2, TILES % 2)
            store(TILES - 1, 1 - TILES % 2)
            sp.wait_ge(slot_out, 32)
            for q in range(2):
                sp.wait_ge(y_out[q], 16 * ((TILES + 1 - q) // 2))

        @block.gpsimd
        def _(pool):
            pool.memset(tri[:], 1.0).then_inc(set_done, 1)
            pool.memset(ones[:], 1.0).then_inc(set_done, 1)
            pool.memset(identh[:], 0.0).then_inc(set_done, 1)
            pool.iota(grid_i[:], pattern=[[TE, NM]], base=0, channel_multiplier=0).then_inc(set_done, 1)
            pool.iota(tile_i[:], pattern=[[1, TILES]], base=0, channel_multiplier=0).then_inc(set_done, 1)
            pool.wait_ge(set_done, 5)
            pool.affine_select(out=tri[:], in_=tri[:], compare_op=ALU.is_gt, fill=0.0, base=0,
                               pattern=[[1, P]], channel_multiplier=-1).then_inc(set_done, 1)
            pool.affine_select(out=identh[:], in_=identh[:], compare_op=ALU.not_equal, fill=1.0, base=0,
                               pattern=[[-1, P]], channel_multiplier=1).then_inc(set_done, 1)
            pool.tensor_copy(grid[:], grid_i[:]).then_inc(set_done, 1)
            pool.tensor_copy(tile_f[:], tile_i[:]).then_inc(set_done, 1)

            pool.wait_ge(slot_ready, 1)
            for b in range(B):
                pool.wait_ge(xr_in[b], 16)
                for t in range(TT):
                    for k in range(CHOSEN):
                        at = b * TT + t
                        pool.indirect_dma_start(scr["xs"], bass.IndirectOffsetOnAxis(slot[:, k, at:at + 1], 0),
                                                xr[b][:, t * 2 * D:(t + 1) * 2 * D], None).then_inc(xs_out, 16)

        @block.vector
        def _(dve):
            link = Chain(dve, own)
            dve.wait_ge(gr_in, 16)
            dve.wait_ge(set_done, 9)
            rank, gate = gr[:, :, 1, :], gr[:, :, 0, :]
            dve.tensor_scalar(seld[:].rearrange("p (n e) -> p n e", e=E_N), rank, CHOSEN - 0.5, None, ALU.is_lt
                              ).then_inc(sel_ready, 1)
            dve.tensor_scalar(first[:], rank, 0.5, None, ALU.is_lt)
            link(dve.tensor_scalar(second[:], rank, 1.0, None, ALU.is_equal))
            dve.wait_ge(cum_ps, 1)
            a = 0
            link(dve.tensor_copy(scan[0][:].rearrange("p n e -> p (n e)"), psY[1][:, 0:NT * E_N]))
            step = 1
            while step < NT:
                dve.tensor_copy(scan[1 - a][:, 0:step, :], scan[a][:, 0:step, :])
                link(dve.tensor_tensor(scan[1 - a][:, step:, :], scan[a][:, step:, :], scan[a][:, 0:NT - step, :], ALU.add))
                a, step = 1 - a, step * 2
            link(dve.tensor_copy(count[:], scan[a][:, NT - 1, :]))
            link(dve.tensor_tensor(pos[:].rearrange("p n e -> p (n e)"), scan[a][:].rearrange("p n e -> p (n e)"),
                                   psY[1][:, 0:NT * E_N], ALU.subtract))
            link(dve.tensor_tensor(pos[:].rearrange("p n e -> p (n e)"), pos[:].rearrange("p n e -> p (n e)"),
                                   psY[0][:, 0:NT * E_N], ALU.add))
            link(dve.tensor_tensor(cmp[:], count[:].unsqueeze(2).to_broadcast([P, E_N, NM]),
                                   grid[:].unsqueeze(1).to_broadcast([P, E_N, NM]), ALU.is_gt))
            link(dve.tensor_reduce(ntile[:], cmp[:], axis=AX.X, op=ALU.add))
            link(dve.tensor_copy(ends[0][:], ntile[:]))
            z, step = 0, 1
            while step < E_N:
                dve.tensor_copy(ends[1 - z][:, 0:step], ends[z][:, 0:step])
                link(dve.tensor_tensor(ends[1 - z][:, step:], ends[z][:, step:], ends[z][:, 0:E_N - step], ALU.add))
                z, step = 1 - z, step * 2
            link(dve.tensor_tensor(start[:], ends[z][:], ntile[:], ALU.subtract))
            link(dve.tensor_scalar(start[:], start[:], float(TE), None, ALU.mult))
            link(dve.tensor_tensor(pos[:], pos[:], start[:].unsqueeze(1).to_broadcast([P, NT, E_N]), ALU.add))
            for k, chosen in enumerate((first, second)):
                link(dve.tensor_tensor(scan[k][:], pos[:], chosen[:], ALU.mult))
                link(dve.tensor_reduce(slot_f[:, k, :], scan[k][:], axis=AX.X, op=ALU.add))
                link(dve.tensor_tensor(scan[k][:], gate, chosen[:], ALU.mult))
                link(dve.tensor_reduce(gsel[:, k, :], scan[k][:], axis=AX.X, op=ALU.add))
            dve.tensor_copy(slot[:], slot_f[:]).then_inc(slot_ready, 1)
            link(dve.tensor_tensor(cmp2[:], tile_f[:].unsqueeze(2).to_broadcast([P, TILES, E_N]),
                                   ends[z][:].unsqueeze(1).to_broadcast([P, TILES, E_N]), ALU.is_ge))
            link(dve.tensor_reduce(emap_f[:], cmp2[:], axis=AX.X, op=ALU.add))
            dve.tensor_scalar(emap[:], emap_f[:], float(E_N - 1), None, ALU.min).then_inc(slot_ready, 1)

            for e in range(E_N):
                for k, wh in enumerate((w1h, w2h)):
                    dve.wait_ge(hi_done, 2 * e + k + 1)
                    src = stage[k][:]
                    flat = wh[:, e].rearrange("p r c f -> p r (c f)")
                    dve.scalar_tensor_tensor(out=flat[:, 1, :], in0=src, scalar=WSCALE, in1=flat[:, 0, :],
                                             op0=ALU.mult, op1=ALU.subtract).then_inc(w_ready, 1)
            link.reset()

            def out_tile(s, q):
                dve.wait_ge(y_ps, s + 1)
                if not (isinstance(s, int) and s < 2):
                    dve.wait_ge(y_out[q], (s - q) * 8)
                dve.tensor_scalar(yo[q][:, 0, :], psY[0][:, 0:D], 1.0 / WSCALE, None, ALU.mult)
                dve.tensor_scalar(yo[q][:, 1, :], psY[1][:, 0:D], 1.0 / WSCALE, None, ALU.mult)
                dve.drain().then_inc(y_free, 1)

            dve.sem_inc(y_free, 1)

            def body(s, q):
                if not (isinstance(s, int) and s < 2):
                    dve.wait_ge(y_ps, s - 1)
                for f in range(FP):
                    two = slice(2 * f, 2 * f + 2)
                    dve.wait_ge(h_free, s * FC + 2 * f + 2 + 8)
                    link(dve.tensor_copy(hl[q][:, 0, two, :], hf[:, two, :]))
                    dve.tensor_tensor(hl[q][:, 1, two, :], hf[:, two, :], hl[q][:, 0, two, :], ALU.subtract
                                      ).then_inc(hl_ready, 1)
                    if f == 1 and not (isinstance(s, int) and s == 0):
                        out_tile(s - 1, 1 - q)
                link.reset()

            tiles(dve, body)
            out_tile(TILES - 1, 1 - TILES % 2)

        @block.scalar
        def _(act):
            for e in range(E_N):
                for k, wh in enumerate((w1h, w2h)):
                    act.wait_ge(w_in[k], 16 * (e + 1))
                    act.mul(wh[:, e, 0].rearrange("p c f -> p (c f)"), stage[k][:], WSCALE).then_inc(hi_done, 1)
            act.wait_ge(xs_out, 16 * CHOSEN * NT)
            act.sem_inc(h_free, 8)

            def transposed(s, q):
                act.wait_ge(x_ps, s + 1)
                if not (isinstance(s, int) and s < 2):
                    act.wait_ge(h_ps, (s - 1) * FP)
                act.copy(xT[q][:].rearrange("p c t -> p (c t)"), psX[q][:]).then_inc(x_ready, 1)

            transposed(0, 0)

            def body(s, q):
                for f in range(FC):
                    act.wait_ge(h_ps, s * FP + f // 2 + 1)
                    if not (isinstance(s, int) and s == 0) and f % 2 == 0:
                        act.wait_ge(hl_ready, (s - 1) * FP + f // 2 + 1)
                    act.activation(hf[:, f, :], psH[f // 2][:, f % 2, :], ACT.Gelu_apprx_tanh, bias=b1[q][:, f:f + 1],
                                   scale=1.0 / WSCALE).then_inc(h_free, 1)
                    if f == 3 and not (isinstance(s, int) and s == TILES - 1):
                        transposed(s + 1, 1 - q)

            tiles(act, body)

        @block.tensor
        def _(pe):
            pe.wait_ge(set_done, 9)
            pe.wait_ge(sel_ready, 1)
            pe.matmul(psY[0][:, 0:NT * E_N], tri[:], seld[:], start=True, stop=True)
            pe.matmul(psY[1][:, 0:NT * E_N], ones[:], seld[:], start=True, stop=True).then_inc(cum_ps, 1)

            def transpose(s, q):
                pe.wait_ge(xt_in[q], (s - q) * 16 + 32)
                if not (isinstance(s, int) and s < 2):
                    pe.wait_ge(x_ready, s - 1)
                for ch in range(2 * DC):
                    for h in range(2):
                        last = pe.transpose(psX[q][:, ch * TE + h * P:ch * TE + (h + 1) * P],
                                            xt[q][:, h, ch * P:(ch + 1) * P], identh[:])
                last.then_inc(x_ps, 1)

            def hidden(s, q, e, f):
                pe.wait_ge(h_free, s * FC + 2 * f + 2)
                for j in range(2):
                    fc = 2 * f + j
                    n = 0
                    for wp, xp in PRODUCTS:
                        for d in range(DC):
                            last = pe.matmul(psH[f][:, j, :],
                                             w1h[:, ds(e, 1), wp, d, fc * P:(fc + 1) * P].rearrange("p o f -> p (o f)"),
                                             xT[q][:, xp * DC + d, :], start=n == 0, stop=n == len(PRODUCTS) * DC - 1)
                            n += 1
                last.then_inc(h_ps, 1)

            def output(s, q, e, f):
                pe.wait_ge(hl_ready, s * FP + f + 1)
                if f == 0:
                    pe.wait_ge(y_free, s + 1)
                for t in range(2):
                    for fc in (2 * f, 2 * f + 1):
                        for n, (wp, hp) in enumerate(PRODUCTS):
                            last = pe.matmul(psY[t][:, 0:D], hl[q][:, hp, fc, t * P:(t + 1) * P],
                                             w2h[:, ds(e, 1), wp, fc, :].rearrange("p o d -> p (o d)"),
                                             start=fc == 0 and n == 0, stop=fc == FC - 1 and n == len(PRODUCTS) - 1)
                if f == FP - 1:
                    last.then_inc(y_ps, 1)

            pe.wait_ge(slot_ready, 2)
            pe.wait_ge(w_ready, 2 * E_N)
            transpose(0, 0)

            def expert_of(s):
                return pe.value_load(emap[0:1, ds(s, 1)], min_val=0, max_val=E_N - 1)

            def body(s, q):
                pe.wait_ge(x_ready, s + 1)
                e = expert_of(s)
                if not (isinstance(s, int) and s == 0):
                    before = expert_of(s - 1)
                for f in range(FP):
                    hidden(s, q, e, f)
                    if f < 2:
                        if not (isinstance(s, int) and s == 0):
                            output(s - 1, 1 - q, before, f + 2)
                    else:
                        output(s, q, e, f - 2)
                    if f == 1 and not (isinstance(s, int) and s == TILES - 1):
                        transpose(s + 1, 1 - q)

            tiles(pe, body)
            e = expert_of(TILES - 1)
            for f in (2, 3):
                output(TILES - 1, 1 - TILES % 2, e, f)


def phase_last(nc, c, w, scr):
    WS = 16.0
    YS = 4.0
    QS, KS = WS * YS, WS
    IS = 2.0 ** -14
    HS = 2.0 ** -4
    PRODUCTS = ((0, 0), (0, 1), (1, 0))
    wi = c.sb("wi", [P, DC * F2], I32)
    wf = c.sb("wf", [P, DC * F2])
    wgate, wup = (c.sb(n, [P, 2, DC, F2], F16) for n in ("wgate", "wup"))
    wdown = c.sb("wdown", [P, 2, F2C, D], F16)
    wq, wk, wv = (c.sb(n, [P, 2, DC, D], F16) for n in ("wq", "wk", "wv"))
    bq, bk, bv = c.sb("bq", [P, DC]), c.sb("bk", [P, DC]), c.sb("bv", [P, D])
    identh = c.sb("identh", [P, P], F16)
    xin, cin, xo, x3 = ([c.sb(f"{n}{p}", shape) for p in range(2)] for n, shape in (
        ("xin", [P, TT, D]), ("cin", [P, DC, S]), ("xo", [P, TT, D]), ("x3_", [P, TT, D])))
    slots = c.sb("slots", [P, CHOSEN, NT], U32)
    gsel = c.sb("gsel", [P, CHOSEN, NT])
    yg = [c.sb(f"yg{p}", [P, TT, CHOSEN, D]) for p in range(2)]
    ya, yf = c.sb("ya", [P, TT, D]), c.sb("yf", [P, TT, D])
    yap, yfp = c.sb("yap", [P, 2, TT, D], F16), c.sb("yfp", [P, 2, TT, D], F16)
    yT = c.sb("yT", [P, 2, DC, S], F16)
    ctx = [c.sb(f"ctx{p}", [P, 2, DC, S], F16) for p in range(2)]
    kT = [c.sb(f"kT{p}", [P, 2, DC, S], F16) for p in range(2)]
    qT = c.sb("qT", [P, 2, DC, S], F16)
    vf = c.sb("vf", [P, TT, D])
    vv = [c.sb(f"vv{p}", [P, 2, TT, D], F16) for p in range(2)]
    pr = c.sb("pr", [P, TT, S])
    pp = c.sb("pp", [P, 2, TT, S], F16)
    pT = c.sb("pT", [P, 2, TT, S], F16)
    sg = c.sb("sg", [P, 2, S])
    hf = c.sb("hf", [P, 2, S])
    hT = c.sb("hT", [P, 2, F2C, S], F16)
    stats, mv, rstd = c.sb("stats", [P, TT, 6]), c.sb("mv", [P, TT, 2]), c.sb("rstd", [P, TT])
    power, var, eps = c.sb("power", [P, TT]), c.sb("var", [P, TT]), c.sb("eps", [P, TT])
    top, nmax, tot, rec = (c.sb(n, [P, TT]) for n in ("top", "nmax", "tot", "rec"))
    psT = c.ps("psT", [P, 4 * S], F16)
    psG = [c.ps(f"psG{k}", [P, S]) for k in range(2)]
    psU = [c.ps(f"psU{k}", [P, S]) for k in range(2)]
    psB = [c.ps(f"psB{k}", [P, S]) for k in range(2)]

    const_in, wi_in = c.sem("const_in"), c.sem("wi_in")
    x_in, c_in, yg_in, x_out = ([c.sem(f"{n}{p}") for p in range(2)] for n in ("x_in", "c_in", "yg_in", "x_out"))
    t_ps, g_ps, u_ps, b_ps = (c.sem(n) for n in ("t_ps", "g_ps", "u_ps", "b_ps"))
    t_free, exp_done, ph_ready, kqh_ready, ctxh_ready, vh_ready, yah_ready, yfh_ready, silu_done, hh_ready, wh_ready = (
        c.sem(n) for n in ("t_free", "exp_done", "ph_ready", "kqh_ready", "ctxh_ready", "vh_ready", "yah_ready",
                           "yfh_ready", "silu_done", "hh_ready", "wh_ready"))
    max_ready, pl_ready, kq_ready, ctx_ready, v_ready, ya_ready, yf_ready, hl_ready, w_ready = (
        c.sem(n) for n in ("max_ready", "pl_ready", "kq_ready", "ctx_ready", "v_ready", "ya_ready", "yf_ready",
                           "hl_ready", "w_ready"))
    wf_ready, vf_ready, yaf_ready, yff_ready, h_ready, b_free, x_used, yg_used, xo_ready = (
        c.sem(n) for n in ("wf_ready", "vf_ready", "yaf_ready", "yff_ready", "h_ready", "b_free", "x_used",
                           "yg_used", "xo_ready"))
    set_done, bias_ready, var_ready, rstd_ready, dve_own, pool_own = (
        c.sem(n) for n in ("set_done", "bias_ready", "var_ready", "rstd_ready", "dve_own", "pool_own"))
    n_const = 5

    def is_(n, *values):
        return isinstance(n, int) and n in values

    def bodies(eng, body):
        for n in range(2):
            body(n, n % 2)
        with eng.Fori(1, B // 2 - 1) as i:
            for par in range(2):
                body(i * 2 + par, par)
        for n in range(B - 2, B + 1):
            body(n, n % 2)

    def t_att(n):
        return 0 if is_(n, 0) else n * 6 - 1

    def t_ffn(m):
        return m * 6 + (5 if is_(m, B - 1) else 6)

    def t_prob(n):
        return n * 6 + 1

    def b_val(n):
        return n * 4 if is_(n, 0, 1) else n * 12 - 12

    def b_att(n):
        return 8 if is_(n, 0) else n * 12 + (0 if is_(n, B - 1) else 4)

    def b_down(m):
        return m * 12 + (8 if is_(m, B - 1) else 16 if is_(m, B - 2) else 20)

    GU = 2 * DC + F2C
    UU = TT + F2C

    def g_key(n):
        return 0 if is_(n, 0) else 4 if is_(n, 1) else n * GU - 12

    def g_gate(m):
        return m * GU + (8 if is_(m, B - 2) else 4 if is_(m, B - 1) else 10)

    def g_query(n):
        return 2 if is_(n, 0) else 6 if is_(n, 1) else n * GU - 4

    def u_score(n):
        return 0 if is_(n, 0) else n * UU - F2C

    def u_up(m):
        return m * UU + (TT if is_(m, B - 1) else 2 * TT)

    with nc.Block() as block:

        @block.sync
        def _(sp):
            for dst, src in ((bq[:], w["bq"]), (bk[:], w["bk"]), (bv[:], w["bv"]), (slots[:], scr["slots"]),
                             (gsel[:], scr["gsel"])):
                sp.dma_start(dst, src).then_inc(const_in, 16)
            for k, name in enumerate(("wq", "wk", "wv")):
                sp.dma_start(pr[:, k, :].rearrange("p (c d) -> p c d", c=DC), w[name]).then_inc(const_in, 16)

            def load_c(n, par):
                if not is_(n, 0, 1):
                    sp.wait_ge(ctx_ready, n - 1)
                sp.dma_start(cin[par][:], scr["ctxT"][ds(n, 1)].rearrange("o (c p) s -> p (o c) s", p=P)
                             ).then_inc(c_in[par], 16)

            def load_x(n, par):
                if not is_(n, 0, 1):
                    sp.wait_ge(x_used, n - 1)
                sp.dma_start(xin[par][:], scr["x2"][ds(n, 1)].rearrange("o (t p) d -> p (o t) d", p=P)
                             ).then_inc(x_in[par], 16)

            load_c(0, 0)
            load_x(0, 0)
            load_c(1, 1)
            load_x(1, 1)
            for k, name in enumerate(("gate", "up", "down")):
                if k > 0:
                    sp.wait_ge(wf_ready, k)
                sp.dma_start(wi[:].rearrange("p (c f) -> p c f", c=DC if k < 2 else F2C), 
                             w[name]).then_inc(wi_in, 16)

            def body(n, par):
                if not is_(n, B - 2, B - 1, B):
                    load_c(n + 2, par)
                    load_x(n + 2, par)
                if not is_(n, 0):
                    sp.wait_ge(xo_ready, n)
                    sp.dma_start(scr["out"][ds(n - 1, 1)].rearrange("o (t p) d -> p (o t) d", p=P), xo[1 - par][:]
                                 ).then_inc(x_out[1 - par], 16)

            bodies(sp, body)
            for par in range(2):
                sp.wait_ge(x_out[par], 16 * (B // 2))

        @block.gpsimd
        def _(pool):
            pool.memset(identh[:], 0.0).then_inc(set_done, 1)
            pool.wait_ge(set_done, 1)
            pool.affine_select(out=identh[:], in_=identh[:], compare_op=ALU.not_equal, fill=1.0, base=0,
                               pattern=[[-1, P]], channel_multiplier=1).then_inc(set_done, 1)
            pool.memset(power[:], -0.5).then_inc(pool_own, 1)
            pool.memset(eps[:], EPS).then_inc(pool_own, 1)
            pool.wait_ge(pool_own, 2)
            pool.wait_ge(const_in, 16 * (n_const + 3))

            def gather(n):
                if n >= 2:
                    pool.wait_ge(yg_used, n - 1)
                for t in range(TT):
                    for k in range(CHOSEN):
                        at = n * TT + t
                        pool.indirect_dma_start(yg[n % 2][:, t, k, :], None, scr["y"],
                                                bass.IndirectOffsetOnAxis(slots[:, k, at:at + 1], 0)
                                                ).then_inc(yg_in[n % 2], 16)

            def deviations(k):
                pool.wait_ge(var_ready, k + 1)
                pool.tensor_tensor(var[:], mv[:, :, 1], eps[:], ALU.add).then_inc(pool_own, 1)
                pool.wait_ge(pool_own, k + 3)
                pool.tensor_tensor(rstd[:], var[:], power[:], ALU.pow).then_inc(rstd_ready, 1)

            gather(0)
            deviations(0)
            gather(1)
            for n in range(B):
                if n + 2 < B:
                    gather(n + 2)
                for k in range(2 * n + 1, min(2 * n + 3, 2 * B)):
                    deviations(k)

        @block.vector
        def _(dve):
            link = Chain(dve, dve_own)
            dve.wait_ge(const_in, 16 * (n_const + 3))
            dve.tensor_scalar(bq[:], bq[:], QS, None, ALU.mult)
            dve.tensor_scalar(bk[:], bk[:], KS, None, ALU.mult)
            link(dve.tensor_scalar(bv[:], bv[:], KS, None, ALU.mult))
            dve.sem_inc(bias_ready, 1)

            def low(dst, src, scale, high):
                return dve.scalar_tensor_tensor(out=dst, in0=src, scalar=scale, in1=high, op0=ALU.mult,
                                                op1=ALU.subtract)

            def stats_of(src):
                for t in range(TT):
                    last = dve.bn_stats(stats[:, t, :], src[:, t, :])
                link(last)
                for t in range(TT):
                    last = dve.bn_aggr(mv[:, t, :], stats[:, t, :])
                last.then_inc(var_ready, 1)

            def normed(k, src, dst):
                dve.wait_ge(rstd_ready, k + 1)
                for t in range(TT):
                    last = dve.tensor_scalar(dst[:, t, :], src[:, t, :], mv[:, t, 0:1], rstd[:, t:t + 1],
                                             ALU.subtract, ALU.mult)
                return last

            def combine(n, par, k):
                if k == 0:
                    dve.wait_ge(x_in[par], (n - par) * 8 + 16)
                    dve.wait_ge(yg_in[par], (n - par) * (8 * CHOSEN * TT) + 16 * CHOSEN * TT)
                for t in range(TT):
                    g = gsel[:, k:k + 1, ds(n * TT + t, 1)].rearrange("p k t -> p (k t)")
                    last = dve.scalar_tensor_tensor(out=xin[par][:, t, :], in0=yg[par][:, t, k, :], scalar=g,
                                                    in1=xin[par][:, t, :], op0=ALU.mult, op1=ALU.add)
                link(last)
                if k == CHOSEN - 1:
                    dve.sem_inc(yg_used, 1)

            def att_norm(n, par):
                k = 0 if is_(n, 0) else n * 2 - 1
                normed(k, xin[par], ya).then_inc(yaf_ready, 1)

            def att_norm_low(n):
                dve.wait_ge(yah_ready, n + 1)
                low(yap[:, 1], ya[:], YS, yap[:, 0]).then_inc(ya_ready, 1)

            def context_low(n, par):
                dve.wait_ge(ctxh_ready, n + 1)
                dve.tensor_tensor(ctx[par][:, 1], cin[par][:], ctx[par][:, 0], ALU.subtract).then_inc(ctx_ready, 1)

            def keys_low(n, par):
                for u in range(DC):
                    dve.wait_ge(kqh_ready, n * 4 + u + 1)
                    dve.scalar_tensor_tensor(out=kT[par][:, 1, u, :], in0=psG[u][:], scalar=bk[:, u:u + 1],
                                             in1=kT[par][:, 0, u, :], op0=ALU.add, op1=ALU.subtract
                                             ).then_inc(kq_ready, 1)

            def queries_low(n):
                for u in range(DC):
                    dve.wait_ge(kqh_ready, n * 4 + 2 + u + 1)
                    dve.scalar_tensor_tensor(out=qT[:, 1, u, :], in0=psG[u][:], scalar=bq[:, u:u + 1],
                                             in1=qT[:, 0, u, :], op0=ALU.add, op1=ALU.subtract
                                             ).then_inc(kq_ready, 1)

            def values(n):
                for t in range(TT):
                    dve.wait_ge(b_ps, b_val(n) + t + 1)
                    dve.tensor_tensor(vf[:, t, :], psB[t % 2][:, 0:D], bv[:], ALU.add).then_inc(b_free, 1)
                dve.wait_ge(b_free, b_val(n) + TT)
                dve.sem_inc(vf_ready, 1)

            def values_low(n, par):
                dve.wait_ge(vh_ready, n + 1)
                dve.tensor_tensor(vv[par][:, 1], vf[:], vv[par][:, 0], ALU.subtract).then_inc(v_ready, 1)

            def maximum(n, t):
                dve.wait_ge(u_ps, u_score(n) + t + 1)
                link(dve.tensor_reduce(top[:, t:t + 1], psU[t % 2][:], axis=AX.X, op=ALU.max, negate=True))
                dve.tensor_scalar(nmax[:, t:t + 1], top[:, t:t + 1], 1.0 / (QS * KS), None, ALU.mult
                                  ).then_inc(max_ready, 1)

            def prob_low(n, t):
                dve.wait_ge(ph_ready, n * TT + t + 1)
                dve.tensor_tensor(pp[:, 1, t, :], pr[:, t, :], pp[:, 0, t, :], ALU.subtract).then_inc(pl_ready, 1)

            def hidden(m, f):
                dve.wait_ge(u_ps, u_up(m) + f + 1)
                dve.wait_ge(silu_done, m * F2C + f + 1)
                if f >= 2:
                    dve.wait_ge(hl_ready, m * F2C + f - 1)
                dve.scalar_tensor_tensor(out=hf[:, f % 2, :], in0=psU[f % 2][:], scalar=SCALE2 / IS / YS * HS,
                                         in1=sg[:, f % 2, :], op0=ALU.mult, op1=ALU.mult).then_inc(h_ready, 1)

            def hidden_low(m, f):
                dve.wait_ge(hh_ready, m * F2C + f + 1)
                dve.tensor_tensor(hT[:, 1, f, :], hf[:, f % 2, :], hT[:, 0, f, :], ALU.subtract
                                  ).then_inc(hl_ready, 1)

            def attended(n, par):
                dve.wait_ge(exp_done, n * TT + TT)
                link(dve.reciprocal(rec[:], tot[:]))
                link(dve.tensor_scalar(rec[:], rec[:], 1.0 / 16.0 / KS, None, ALU.mult))
                for t in range(TT):
                    dve.wait_ge(b_ps, b_att(n) + t + 1)
                    dve.scalar_tensor_tensor(out=x3[par][:, t, :], in0=psB[t % 2][:, 0:D], scalar=rec[:, t:t + 1],
                                             in1=xin[par][:, t, :], op0=ALU.mult, op1=ALU.add).then_inc(b_free, 1)
                dve.wait_ge(b_free, b_att(n) + TT)
                dve.sem_inc(x_used, 1)
                stats_of(x3[par])

            def ffn_norm(n, par):
                k = n * 2 + (1 if is_(n, B - 1) else 2)
                normed(k, x3[par], yf).then_inc(yff_ready, 1)

            def ffn_norm_low(n):
                dve.wait_ge(yfh_ready, n + 1)
                low(yfp[:, 1], yf[:], YS, yfp[:, 0]).then_inc(yf_ready, 1)

            def down(m, par, tiles):
                if 0 in tiles:
                    dve.wait_ge(x_out[par], (m - par) * 8)
                for t in tiles:
                    dve.wait_ge(b_ps, b_down(m) + t + 1)
                    dve.scalar_tensor_tensor(out=xo[par][:, t, :], in0=psB[t % 2][:, 0:D], scalar=SCALE2 / IS / HS,
                                             in1=x3[par][:, t, :], op0=ALU.mult, op1=ALU.add).then_inc(b_free, 1)
                if TT - 1 in tiles:
                    dve.drain().then_inc(xo_ready, 1)

            for k, wt in enumerate((wq, wk, wv)):
                dve.wait_ge(wh_ready, k + 1)
                low(wt[:, 1].rearrange("p c d -> p (c d)"), pr[:, k, :], WS, wt[:, 0].rearrange("p c d -> p (c d)")
                    ).then_inc(w_ready, 1)
            context_low(0, 0)
            combine(0, 0, 0)
            combine(0, 0, 1)
            stats_of(xin[0])
            att_norm(0, 0)
            att_norm_low(0)
            context_low(1, 1)
            keys_low(0, 0)
            values(0)
            values_low(0, 0)
            queries_low(0)
            dve.wait_ge(w_ready, 3)
            link.reset()

            def int_weights(k):
                dve.wait_ge(wi_in, 16 * (k + 1))
                if k > 0:
                    dve.wait_ge(w_ready, 3 + k)
                link(dve.tensor_scalar(wf[:], wi[:], IS, None, ALU.mult))
                dve.sem_inc(wf_ready, 1)
                dve.wait_ge(wh_ready, 3 + k + 1)
                flat = (wgate, wup, wdown)[k][:].rearrange("p r c f -> p r (c f)")
                dve.tensor_tensor(flat[:, 1], wf[:], flat[:, 0], ALU.subtract).then_inc(w_ready, 1)

            def body(n, par):
                front, att, ffn = not is_(n, B - 1, B), not is_(n, B), not is_(n, 0)
                if att:
                    maximum(n, 0)
                    maximum(n, 1)
                if front:
                    keys_low(n + 1, 1 - par)
                if att:
                    prob_low(n, 0)
                    maximum(n, 2)
                    prob_low(n, 1)
                    maximum(n, 3)
                if front:
                    values(n + 1)
                if att:
                    prob_low(n, 2)
                    prob_low(n, 3)
                if front:
                    values_low(n + 1, 1 - par)
                pieces = [lambda: combine(n + 1, 1 - par, 0), lambda: combine(n + 1, 1 - par, 1),
                          lambda: stats_of(xin[1 - par]), lambda: att_norm(n + 1, 1 - par),
                          lambda: att_norm_low(n + 1)]
                for f in range(F2C):
                    if ffn:
                        hidden(n - 1, f)
                        if f > 0:
                            hidden_low(n - 1, f - 1)
                    if front and f < len(pieces):
                        pieces[f]()
                    if is_(n, 0) and f < 3:
                        int_weights(f)
                if ffn:
                    hidden_low(n - 1, F2C - 1)
                if att:
                    attended(n, par)
                    if not is_(n, B - 2, B - 1):
                        context_low(n + 2, par)
                    ffn_norm(n, par)
                if ffn:
                    down(n - 1, 1 - par, (0, 1))
                if att:
                    ffn_norm_low(n)
                if front:
                    queries_low(n + 1)
                if ffn:
                    down(n - 1, 1 - par, (2, 3))
                dve.drain()
                link.reset()

            bodies(dve, body)

        @block.scalar
        def _(act):
            act.wait_ge(const_in, 16 * (n_const + 3))

            def flat(tile):
                return tile.rearrange("p a b -> p (a b)")

            def context_high(n, par):
                act.wait_ge(c_in[par], (n - par) * 8 + 16)
                if not is_(n, 0, 1):
                    act.wait_ge(b_ps, b_val(n - 2) + TT)
                act.copy(flat(ctx[par][:, 0]), flat(cin[par][:])).then_inc(ctxh_ready, 1)

            def keys_high(n, par):
                for u in range(DC):
                    act.wait_ge(g_ps, g_key(n) + u + 1)
                    act.activation(kT[par][:, 0, u, :], psG[u][:], ACT.Identity, bias=bk[:, u:u + 1]
                                   ).then_inc(kqh_ready, 1)

            def queries_high(n):
                if not is_(n, 0):
                    act.wait_ge(u_ps, u_score(n - 1) + TT)
                for u in range(DC):
                    act.wait_ge(g_ps, g_query(n) + u + 1)
                    act.activation(qT[:, 0, u, :], psG[u][:], ACT.Identity, bias=bq[:, u:u + 1]
                                   ).then_inc(kqh_ready, 1)

            def values_high(n, par):
                act.wait_ge(vf_ready, n + 1)
                act.copy(flat(vv[par][:, 0]), flat(vf[:])).then_inc(vh_ready, 1)

            def transposed(unit):
                act.wait_ge(t_ps, unit + 1)
                act.copy(yT[:].rearrange("p r c s -> p (r c s)"), psT[:]).then_inc(t_free, 1)

            def att_transposed(n):
                if not is_(n, 0, 1):
                    act.wait_ge(u_ps, u_up(n - 2) + F2C)
                transposed(t_att(n))

            def ffn_transposed(m):
                act.wait_ge(g_ps, g_query(m if is_(m, B - 1) else m + 1) + DC)
                transposed(t_ffn(m))

            def exponential(n, t):
                act.wait_ge(max_ready, n * TT + t + 1)
                if not is_(n, 0):
                    act.wait_ge(pl_ready, n * TT)
                act.activation(pr[:, t, :], psU[t % 2][:], ACT.Exp, bias=nmax[:, t:t + 1], scale=1.0 / (QS * KS),
                               accum_out=tot[:, t:t + 1]).then_inc(exp_done, 1)

            def prob_high(n, t):
                act.wait_ge(exp_done, n * TT + t + 1)
                if not is_(n, 0):
                    act.wait_ge(t_ps, t_prob(n - 1) + TT)
                act.copy(pp[:, 0, t, :], pr[:, t, :]).then_inc(ph_ready, 1)

            def prob_transposed(n, t):
                act.wait_ge(t_ps, t_prob(n) + t + 1)
                if not is_(n, 0):
                    act.wait_ge(b_ps, b_att(n - 1) + TT)
                act.copy(pT[:, :, :, t * P:(t + 1) * P].rearrange("p r k q -> p (r k) q"),
                         psT[:, (t % 2) * 2 * S:(t % 2 + 1) * 2 * S].rearrange("p (k q) -> p k q", q=P)
                         ).then_inc(t_free, 1)

            def silu(m, f):
                act.wait_ge(g_ps, g_gate(m) + f + 1)
                if f >= 2:
                    act.wait_ge(h_ready, m * F2C + f - 1)
                elif not is_(m, 0):
                    act.wait_ge(h_ready, m * F2C)
                act.activation(sg[:, f % 2, :], psG[f % 2][:], ACT.Silu, scale=SCALE2 / IS / YS
                               ).then_inc(silu_done, 1)

            def hidden_high(m, f):
                act.wait_ge(h_ready, m * F2C + f + 1)
                if not is_(m, 0):
                    act.wait_ge(b_ps, b_down(m - 1) + TT)
                act.copy(hT[:, 0, f, :], hf[:, f % 2, :]).then_inc(hh_ready, 1)

            def att_norm_high(n):
                act.wait_ge(yaf_ready, n + 1)
                if not is_(n, 0):
                    act.wait_ge(t_ps, t_att(n - 1) + 1)
                act.mul(flat(yap[:, 0]), flat(ya[:]), YS).then_inc(yah_ready, 1)

            def ffn_norm_high(n):
                act.wait_ge(yff_ready, n + 1)
                if not is_(n, 0):
                    act.wait_ge(t_ps, t_ffn(n - 1) + 1)
                act.mul(flat(yfp[:, 0]), flat(yf[:]), YS).then_inc(yfh_ready, 1)

            for k, wt in enumerate((wq, wk, wv)):
                act.mul(flat(wt[:, 0]), pr[:, k, :], WS).then_inc(wh_ready, 1)
            act.wait_ge(bias_ready, 1)
            context_high(0, 0)
            att_norm_high(0)
            context_high(1, 1)
            keys_high(0, 0)
            values_high(0, 0)
            att_transposed(0)
            queries_high(0)
            act.wait_ge(w_ready, 3)

            def body(n, par):
                front, att, ffn = not is_(n, B - 1, B), not is_(n, B), not is_(n, 0)
                if att:
                    exponential(n, 0)
                    exponential(n, 1)
                if front:
                    keys_high(n + 1, 1 - par)
                if att:
                    prob_high(n, 0)
                    exponential(n, 2)
                    prob_high(n, 1)
                    exponential(n, 3)
                if ffn:
                    ffn_transposed(n - 1)
                if att:
                    prob_high(n, 2)
                    prob_high(n, 3)
                if front:
                    values_high(n + 1, 1 - par)
                for f in range(F2C):
                    if ffn:
                        silu(n - 1, f)
                        if f > 0:
                            hidden_high(n - 1, f - 1)
                    if is_(n, 0) and f < 3:
                        act.wait_ge(wf_ready, f + 1)
                        act.copy(flat((wgate, wup, wdown)[f][:, 0]), wf[:]).then_inc(wh_ready, 1)
                    if f == 4 and front:
                        att_norm_high(n + 1)
                    if att and f in (1, 2):
                        prob_transposed(n, 2 * f - 2)
                        prob_transposed(n, 2 * f - 1)
                if ffn:
                    hidden_high(n - 1, F2C - 1)
                if not is_(n, B - 2, B - 1, B):
                    context_high(n + 2, par)
                if front:
                    att_transposed(n + 1)
                if att:
                    ffn_norm_high(n)
                if front:
                    queries_high(n + 1)

            bodies(act, body)

        @block.tensor
        def _(pe):
            pe.wait_ge(set_done, 2)
            pe.wait_ge(w_ready, 3)

            def wide(bank, wt, u, src):
                i = 0
                for wp, xp in PRODUCTS:
                    for d in range(DC):
                        last = pe.matmul(bank[:], wt[:, wp, d, u * P:(u + 1) * P], src[:, xp, d, :],
                                         start=i == 0, stop=i == len(PRODUCTS) * DC - 1)
                        i += 1
                return last

            def tall(bank, lhs, rhs, chunks, t):
                i = 0
                for lp, rp in PRODUCTS:
                    for d in range(chunks):
                        last = pe.matmul(bank[:, 0:rhs.shape[-1]], lhs[:, lp, d, t * P:(t + 1) * P], rhs[:, rp, d, :],
                                         start=i == 0, stop=i == len(PRODUCTS) * chunks - 1)
                        i += 1
                return last

            def keys(n, par):
                pe.wait_ge(ctx_ready, n + 1)
                for u in range(DC):
                    if not is_(n, 0):
                        pe.wait_ge(kq_ready, n * 4 - 1 + u)
                    wide(psG[u], wk, u, ctx[par]).then_inc(g_ps, 1)

            def queries(n):
                pe.wait_ge(t_free, t_att(n) + 1)
                for u in range(DC):
                    if is_(n, 0, 1):
                        pe.wait_ge(kq_ready, n * 4 + u + 1)
                    else:
                        pe.wait_ge(silu_done, (n - 2) * F2C + F2C - 1 + u)
                    wide(psG[u], wq, u, yT).then_inc(g_ps, 1)

            def values(n, par):
                for t in range(TT):
                    if not (is_(n, 0) and t < 2):
                        pe.wait_ge(b_free, b_val(n) + t - 1)
                    tall(psB[t % 2], ctx[par], wv, DC, t).then_inc(b_ps, 1)

            def transpose(parts, unit, ready, count):
                pe.wait_ge(ready, count)
                if not is_(unit, 0):
                    pe.wait_ge(t_free, unit)
                for r in range(2):
                    for d in range(DC):
                        for t in range(TT):
                            at = (r * DC + d) * S + t * P
                            last = pe.transpose(psT[:, at:at + P], parts[:, r, t, d * P:(d + 1) * P], identh[:])
                last.then_inc(t_ps, 1)

            def score(n, par, t):
                if t == 0:
                    pe.wait_ge(kq_ready, n * 4 + 4)
                    if not is_(n, 0, 1):
                        pe.wait_ge(h_ready, (n - 1) * F2C)
                    elif is_(n, 1):
                        pe.wait_ge(exp_done, TT)
                if t >= 2:
                    pe.wait_ge(exp_done, n * TT + t - 1)
                tall(psU[t % 2], qT, kT[par], DC, t).then_inc(u_ps, 1)

            def prob_transpose(n, t):
                pe.wait_ge(pl_ready, n * TT + t + 1)
                pe.wait_ge(t_free, t_prob(n) + max(t - 1, 0))
                for r in range(2):
                    for k in range(TT):
                        at = (t % 2) * 2 * S + (r * TT + k) * P
                        last = pe.transpose(psT[:, at:at + P], pp[:, r, t, k * P:(k + 1) * P], identh[:])
                last.then_inc(t_ps, 1)

            def weigh(n, par):
                pe.wait_ge(v_ready, n + 1)
                for t in range(TT):
                    pe.wait_ge(t_free, t_prob(n) + t + 1)
                    pe.wait_ge(b_free, b_att(n) + t - 1)
                    tall(psB[t % 2], pT, vv[par], TT, t).then_inc(b_ps, 1)

            def gate_up(m, f):
                if f == 0:
                    pe.wait_ge(t_free, t_ffn(m) + 1)
                    if is_(m, 0):
                        pe.wait_ge(w_ready, 5)
                if f >= 2 or is_(m, B - 1):
                    pe.wait_ge(silu_done, m * F2C + f - 1)
                elif is_(m, B - 2):
                    pe.wait_ge(kq_ready, 4 * (B - 1) + 3 + f)
                else:
                    pe.wait_ge(kq_ready, m * 4 + 9 + f)
                wide(psG[f % 2], wgate, f, yT).then_inc(g_ps, 1)
                if f >= 2 or is_(m, B - 1):
                    pe.wait_ge(h_ready, m * F2C + f - 1)
                else:
                    pe.wait_ge(exp_done, m * TT + TT + 3 + f)
                wide(psU[f % 2], wup, f, yT).then_inc(u_ps, 1)

            def down(m, tiles):
                if 0 in tiles:
                    pe.wait_ge(hl_ready, m * F2C + F2C)
                    if is_(m, 0):
                        pe.wait_ge(w_ready, 6)
                for t in tiles:
                    pe.wait_ge(b_free, b_down(m) + t - 1)
                    tall(psB[t % 2], hT, wdown, F2C, t).then_inc(b_ps, 1)

            keys(0, 0)
            values(0, 0)
            transpose(yap, 0, ya_ready, 1)
            queries(0)

            def body(n, par):
                front, att, ffn = not is_(n, B - 1, B), not is_(n, B), not is_(n, 0)
                if att:
                    score(n, par, 0)
                    score(n, par, 1)
                if front:
                    keys(n + 1, 1 - par)
                if att:
                    score(n, par, 2)
                    score(n, par, 3)
                if ffn:
                    transpose(yfp, t_ffn(n - 1), yf_ready, n)
                if front:
                    values(n + 1, 1 - par)
                for f in range(F2C):
                    if ffn:
                        gate_up(n - 1, f)
                    if att and f in (1, 2):
                        prob_transpose(n, 2 * f - 2)
                        prob_transpose(n, 2 * f - 1)
                if att:
                    weigh(n, par)
                if front:
                    transpose(yap, t_att(n + 1), ya_ready, n + 2)
                if ffn:
                    down(n - 1, (0, 1))
                if front:
                    queries(n + 1)
                if ffn:
                    down(n - 1, (2, 3))

            bodies(pe, body)


def phase_mask(nc, c, mask, dst):
    m8, row = c.sb("m8", [B, S], U8), c.sb("row", [B, S], BF16)
    m_in, m_ready, m_out = c.sem("in"), c.sem("ready"), c.sem("out")
    with nc.Block() as block:

        @block.sync
        def _(sp):
            sp.dma_start(m8[:], mask).then_inc(m_in, 16)
            sp.wait_ge(m_ready, 1)
            sp.dma_start(dst, row[:]).then_inc(m_out, 16)
            sp.wait_ge(m_out, 16)

        @block.vector
        def _(dve):
            dve.wait_ge(m_in, 16)
            dve.tensor_scalar(row[:], m8[:], 1.0, -NEG, ALU.subtract, ALU.mult).then_inc(m_ready, 1)


def build(nc, a, out):
    def scratch(name, shape, dt=F32):
        return nc.dram_tensor(f"s_{name}", shape, dt).ap()

    qk0, qk1 = (scratch(f"qk{k}", [B * DC, 2, NPART, P, S], BF16) for k in range(2))
    v0, v1 = (scratch(f"v{k}", [B, S, H * HP]) for k in range(2))
    o0, o1 = (scratch(f"o{k}", [G_ALL, P, S]) for k in range(2))
    mask = scratch("mask", [B, S], BF16)
    x1, y1, base = (scratch(n, [B, S, D]) for n in ("x1", "y1", "base"))
    xfs = scratch("xfs", [B, S, 2 * D], F16)
    gates = scratch("gates", [B, P, TT, 2, E_N])
    xs = scratch("xs", [TILES * TE, 2 * D], F16)
    ys = scratch("ys", [TILES * TE, D])
    slots = scratch("slots", [P, CHOSEN, NT], U32)
    gsel = scratch("gsel", [P, CHOSEN, NT])

    def chunks(ap):
        return ap.rearrange("(c p) n -> p c n", p=P)

    def phase(tag, run, *args):
        with ExitStack() as stack:
            c = Ctx(nc, tag, stack)
            run(nc, c, *args)
            for sem in c.sems:
                nc.sync.sem_clear(sem)
            nc.all_engine_barrier()

    phase("mask", phase_mask, a["mask"], mask)
    phase("t0", phase_tokens, 0,
          {"wk": chunks(a["wk0"]), "wq": chunks(a["wq0"]), "wv": chunks(a["wv0"]), "bk": a["bk0"], "bq": a["bq0"],
           "bv": a["bv0"].partition_broadcast(P)},
          {"x_src": a["x"], "c_src": a["ctxT"], "qk": qk0, "v": v0})
    phase("a0", phase_attention, False, {"qk": qk0, "v": v0, "mask": mask, "o": o0})
    phase("t1", phase_tokens, 1,
          {"wk": chunks(a["wk1"]), "wq": chunks(a["wq1"]), "wv": chunks(a["wv1"]), "wo": chunks(a["wo0"]),
           "bo": a["bo0"], "lng": a["g1"], "lnb": a["be1"]},
          {"x_src": a["x"], "c_src": o0, "x_dst": x1, "y_dst": y1, "qk": qk1, "v": v1})
    phase("a1", phase_attention, True, {"qk": qk1, "v": v1, "o": o1, "xs": xs})
    phase("t2", phase_gates,
          {"wo": chunks(a["wo1"]), "lng": a["g2"].partition_broadcast(P), "lnb": a["be2"].partition_broadcast(P),
           "wg": chunks(a["wg"]), "b2": a["b2"]},
          {"x1": x1, "y1": y1, "o": o1, "base": base, "xfs": xfs, "gates": gates})
    phase("ex", phase_experts, {"w1": a["w1"], "w2": a["w2"], "b1": a["b1"], "xfs": xfs, "gates": gates, "xs": xs,
                                "ys": ys, "slots": slots, "gsel": gsel})
    phase("la", phase_last,
          {"gate": chunks(a["gate"]), "up": chunks(a["up"]), "down": chunks(a["down"]), "wq": chunks(a["wq2"]),
           "wk": chunks(a["wk2"]), "wv": chunks(a["wv2"]), "bq": a["bq2"], "bk": a["bk2"],
           "bv": a["bv2"].partition_broadcast(P)},
          {"x2": base, "ctxT": a["ctxT"], "y": ys, "slots": slots, "gsel": gsel, "out": out})


def kernel(**inputs):
    import concourse.bacc as bacc
    from concourse.bass_utils import run_bass_kernel_spmd

    t = {k: np.asarray(v) for k, v in inputs.items()}
    order = np.array([(blk * 8 + h) * HD + d for blk in range(DC) for d in range(HD) for h in range(8)])

    def cols(v):
        return v.reshape(-1, P).T

    def padded(wt):
        out = np.zeros((H, HP, D), wt.dtype)
        out[:, :HD] = wt.reshape(H, HD, D)
        return out.reshape(H * HP, D)

    qkv = t["L0_ffn_w_qkv"]
    arrays = {
        "x": t["x"], "ctxT": t["ctx_1024"].transpose(0, 2, 1),
        "mask": t["mask_Bx1xS2_bf1"].reshape(B, S).view(np.uint8),
        "wk0": t["L0_xattn_Wk"].T[:, order], "wq0": t["L0_xattn_Wq"].T[:, order], "wv0": t["L0_xattn_Wv"].T,
        "bk0": cols(t["L0_xattn_bk"][order]), "bq0": cols(t["L0_xattn_bq"][order]), "bv0": t["L0_xattn_bv"],
        "wo0": padded(t["L0_xattn_Wo"].T), "bo0": t["L0_xattn_bo"].reshape(1, D),
        "g1": cols(t["L0_ffn_ln1_g"]), "be1": cols(t["L0_ffn_ln1_b"]),
        "g2": t["L0_ffn_ln2_g"], "be2": t["L0_ffn_ln2_b"],
        "wq1": qkv[:, 0:D][:, order], "wk1": qkv[:, D:2 * D][:, order], "wv1": qkv[:, 2 * D:],
        "wo1": padded(t["L0_ffn_w_o"]), "wg": t["L0_ffn_w_gate"],
        "w1": t["L0_ffn_w1"], "w2": t["L0_ffn_w2"], "b1": t["L0_ffn_b1"].reshape(E_N, FC, P).transpose(0, 2, 1),
        "b2": t["L0_ffn_b2"],
        "wq2": t["L1_xattn_Wq"], "wk2": t["L1_xattn_Wk"], "wv2": t["L1_xattn_Wv"],
        "bq2": cols(t["L1_xattn_bq"]), "bk2": cols(t["L1_xattn_bk"]), "bv2": t["L1_xattn_bv"],
        "gate": t["L1_ffn_w_gate"].T, "up": t["L1_ffn_w_up"].T, "down": t["L1_ffn_w_down"].T,
    }
    nc = bacc.Bacc("TRN2", target_bir_lowering=False, num_devices=1)
    feed, args = {}, {}
    for name, v in arrays.items():
        feed[f"in_{name}"] = np.ascontiguousarray(v)
        args[name] = nc.dram_tensor(f"in_{name}", v.shape, mybir.dt.from_np(v.dtype), kind="ExternalInput").ap()
    out = nc.dram_tensor("out_x", (B, S, D), F32, kind="ExternalOutput").ap()
    build(nc, args, out)
    return run_bass_kernel_spmd(nc, [feed], core_ids=[0]).results[0]["out_x"]
```
